# Optimizing a Trainium2 kernel written in Bass

```python
import numpy as np
import jax
import jax.numpy as jnp

def _softmax(x, axis=-1):
    return jax.nn.softmax(x, axis=axis)

def _gelu(x):
    return jax.nn.gelu(x, approximate=True)

def _silu(x):
    return jax.nn.silu(x)

def _sigmoid(x):
    return jax.nn.sigmoid(x)

def _layernorm(x, axis=-1, eps=1e-05):
    m = jnp.mean(x, axis=axis, keepdims=True)
    v = jnp.var(x, axis=axis, keepdims=True)
    return (x - m) / jnp.sqrt(v + eps)

def _scatter_add(tgt, idx, src, axis=0):
    return tgt.at[idx].add(src)

def _segment_sum(src, seg, n):
    return jax.ops.segment_sum(src, seg, n)
kernel_name = 'mk_gnn_preln_d2_gnn_r32_9cba7a'

def setup_inputs(seed: int=0):
    np.random.seed(seed)
    _w = jnp.asarray

    def _rec_inputs():
        import jax
        import jax.numpy as jnp
        _gk = jax.random.key(seed)
        x = -0.000202 + 1 * jax.random.normal(jax.random.fold_in(_gk, 1), (3125, 128), jnp.float32)
        src = jax.random.randint(jax.random.fold_in(_gk, 2), (50000,), 0, 3125, jnp.int32)
        dst = jnp.minimum((3125 * jax.random.uniform(jax.random.fold_in(_gk, 3), (50000,)) ** 2.0).astype(jnp.int32), 99999)
        _o = jnp.argsort(dst, stable=True)
        src = src[_o]
        dst = dst[_o]
        edge_attr_16 = -0.00019784 + 0.999804 * jax.random.normal(jax.random.fold_in(_gk, 12), (50000, 16), jnp.float32)
        return (x, src, dst, edge_attr_16)
    x, src, dst, edge_attr_16 = _rec_inputs()

    def _L0_gnn_setup():
        import jax, jax.numpy as jnp
        import numpy as np
        N, E = (50000, 12500)
        D_NODE, D_EDGE = (128, 16)
        MSG_DIM, OUT_DIM = (128, 128)
        H_MSG, H_AGGR, H_UP = (256, 128, 256)

        def _dense(key, fin, fout):
            scale = jnp.sqrt(2.0 / (fin + fout)).astype(jnp.float32)
            w = jax.random.normal(key, (fin, fout), jnp.float32) * scale
            b = jnp.zeros((fout,), jnp.float32)
            return (w, b)
        key = jax.random.key(seed)
        ks = jax.random.split(key, 13)
        nodes = jax.random.normal(ks[0], (N, D_NODE), jnp.float32)
        edges = jax.random.normal(ks[1], (E, D_EDGE), jnp.float32)
        senders = jax.random.randint(ks[2], (E,), 0, N, jnp.int32)
        receivers = jax.random.randint(ks[3], (E,), 0, N, jnp.int32)
        msg_in = D_EDGE + 2 * D_NODE
        msg_w1, msg_b1 = _dense(ks[4], msg_in, H_MSG)
        msg_w2, msg_b2 = _dense(ks[5], H_MSG, H_MSG)
        msg_w3, msg_b3 = _dense(ks[6], H_MSG, MSG_DIM)
        ag_w1, ag_b1 = _dense(ks[7], MSG_DIM, H_AGGR)
        ag_w2, ag_b2 = _dense(ks[8], H_AGGR, H_AGGR)
        ag_w3, ag_b3 = _dense(ks[9], H_AGGR, 1)
        up_w1, up_b1 = _dense(ks[10], D_NODE + MSG_DIM, H_UP)
        up_w2, up_b2 = _dense(ks[11], H_UP, H_UP)
        up_w3, up_b3 = _dense(ks[12], H_UP, OUT_DIM)
        return dict(nodes=nodes, edges=edges, senders=senders, receivers=receivers, msg_w1=msg_w1, msg_b1=msg_b1, msg_w2=msg_w2, msg_b2=msg_b2, msg_w3=msg_w3, msg_b3=msg_b3, ag_w1=ag_w1, ag_b1=ag_b1, ag_w2=ag_w2, ag_b2=ag_b2, ag_w3=ag_w3, ag_b3=ag_b3, up_w1=up_w1, up_b1=up_b1, up_w2=up_w2, up_b2=up_b2, up_w3=up_w3, up_b3=up_b3)
    _L0_gnn_all = _L0_gnn_setup()
    _L0_gnn_in = {k: v for k, v in _L0_gnn_all.items() if k in ('msg_w1', 'msg_b1', 'msg_w2', 'msg_b2', 'msg_w3', 'msg_b3', 'ag_w1', 'ag_b1', 'ag_w2', 'ag_b2', 'ag_w3', 'ag_b3', 'up_w1', 'up_b1', 'up_w2', 'up_b2', 'up_w3', 'up_b3')}
    del _L0_gnn_all

    def _L1_gnn_setup():
        import jax, jax.numpy as jnp
        import numpy as np
        N = 50000
        E = 37500
        IN_DIM = 128
        HID = 16
        HEADS1 = 8
        OUT_DIM = 128
        EPS = 1e-16

        def _linear_params(key, fan_in, fan_out):
            kw, kb = jax.random.split(key)
            s = 1.0 / np.sqrt(fan_in)
            W = jax.random.uniform(kw, (fan_in, fan_out), minval=-s, maxval=s, dtype=jnp.float32)
            b = jax.random.uniform(kb, (fan_out,), minval=-s, maxval=s, dtype=jnp.float32)
            return (W, b)

        def _transformer_conv(x, src, dst, Wq, bq, Wk, bk, Wv, bv, Ws, bs, heads, ch):
            n = x.shape[0]
            q = (x @ Wq + bq).reshape(n, heads, ch)
            k = (x @ Wk + bk).reshape(n, heads, ch)
            v = (x @ Wv + bv).reshape(n, heads, ch)
            alpha = jnp.einsum('ehc,ehc->eh', q[dst], k[src]) / np.sqrt(ch)
            m = jax.ops.segment_max(alpha, dst, num_segments=n)
            m = jnp.where(jnp.isfinite(m), m, 0.0)
            ea = jnp.exp(alpha - jax.lax.stop_gradient(m)[dst])
            denom = jax.ops.segment_sum(ea, dst, num_segments=n)
            attn = ea / (denom[dst] + EPS)
            out = jax.ops.segment_sum(attn[:, :, None] * v[src], dst, num_segments=n)
            return out.reshape(n, heads * ch) + (x @ Ws + bs)
        key = jax.random.key(seed)
        ks = jax.random.split(key, 10)
        x = jax.random.normal(ks[0], (N, IN_DIM), dtype=jnp.float32)
        edge_index = jax.random.randint(ks[1], (2, E), 0, N, dtype=jnp.int64)
        Wq1, bq1 = _linear_params(ks[2], IN_DIM, HEADS1 * HID)
        Wk1, bk1 = _linear_params(ks[3], IN_DIM, HEADS1 * HID)
        Wv1, bv1 = _linear_params(ks[4], IN_DIM, HEADS1 * HID)
        Ws1, bs1 = _linear_params(ks[5], IN_DIM, HEADS1 * HID)
        Wq2, bq2 = _linear_params(ks[6], HEADS1 * HID, OUT_DIM)
        Wk2, bk2 = _linear_params(ks[7], HEADS1 * HID, OUT_DIM)
        Wv2, bv2 = _linear_params(ks[8], HEADS1 * HID, OUT_DIM)
        Ws2, bs2 = _linear_params(ks[9], HEADS1 * HID, OUT_DIM)
        return dict(x=x, edge_index=edge_index, Wq1=Wq1, bq1=bq1, Wk1=Wk1, bk1=bk1, Wv1=Wv1, bv1=bv1, Ws1=Ws1, bs1=bs1, Wq2=Wq2, bq2=bq2, Wk2=Wk2, bk2=bk2, Wv2=Wv2, bv2=bv2, Ws2=Ws2, bs2=bs2)
    _L1_gnn_all = _L1_gnn_setup()
    _L1_gnn_in = {k: v for k, v in _L1_gnn_all.items() if k in ('Wq1', 'bq1', 'Wk1', 'bk1', 'Wv1', 'bv1', 'Ws1', 'bs1', 'Wq2', 'bq2', 'Wk2', 'bk2', 'Wv2', 'bv2', 'Ws2', 'bs2')}
    del _L1_gnn_all
    return {'x': x, 'src': src, 'dst': dst, 'edge_attr_16': edge_attr_16, 'L0_gnn_msg_w1': _L0_gnn_in['msg_w1'], 'L0_gnn_msg_b1': _L0_gnn_in['msg_b1'], 'L0_gnn_msg_w2': _L0_gnn_in['msg_w2'], 'L0_gnn_msg_b2': _L0_gnn_in['msg_b2'], 'L0_gnn_msg_w3': _L0_gnn_in['msg_w3'], 'L0_gnn_msg_b3': _L0_gnn_in['msg_b3'], 'L0_gnn_ag_w1': _L0_gnn_in['ag_w1'], 'L0_gnn_ag_b1': _L0_gnn_in['ag_b1'], 'L0_gnn_ag_w2': _L0_gnn_in['ag_w2'], 'L0_gnn_ag_b2': _L0_gnn_in['ag_b2'], 'L0_gnn_ag_w3': _L0_gnn_in['ag_w3'], 'L0_gnn_ag_b3': _L0_gnn_in['ag_b3'], 'L0_gnn_up_w1': _L0_gnn_in['up_w1'], 'L0_gnn_up_b1': _L0_gnn_in['up_b1'], 'L0_gnn_up_w2': _L0_gnn_in['up_w2'], 'L0_gnn_up_b2': _L0_gnn_in['up_b2'], 'L0_gnn_up_w3': _L0_gnn_in['up_w3'], 'L0_gnn_up_b3': _L0_gnn_in['up_b3'], 'L1_gnn_Wq1': _L1_gnn_in['Wq1'], 'L1_gnn_bq1': _L1_gnn_in['bq1'], 'L1_gnn_Wk1': _L1_gnn_in['Wk1'], 'L1_gnn_bk1': _L1_gnn_in['bk1'], 'L1_gnn_Wv1': _L1_gnn_in['Wv1'], 'L1_gnn_bv1': _L1_gnn_in['bv1'], 'L1_gnn_Ws1': _L1_gnn_in['Ws1'], 'L1_gnn_bs1': _L1_gnn_in['bs1'], 'L1_gnn_Wq2': _L1_gnn_in['Wq2'], 'L1_gnn_bq2': _L1_gnn_in['bq2'], 'L1_gnn_Wk2': _L1_gnn_in['Wk2'], 'L1_gnn_bk2': _L1_gnn_in['bk2'], 'L1_gnn_Wv2': _L1_gnn_in['Wv2'], 'L1_gnn_bv2': _L1_gnn_in['bv2'], 'L1_gnn_Ws2': _L1_gnn_in['Ws2'], 'L1_gnn_bs2': _L1_gnn_in['bs2']}

def reference(x, src, dst, edge_attr_16, L0_gnn_msg_w1, L0_gnn_msg_b1, L0_gnn_msg_w2, L0_gnn_msg_b2, L0_gnn_msg_w3, L0_gnn_msg_b3, L0_gnn_ag_w1, L0_gnn_ag_b1, L0_gnn_ag_w2, L0_gnn_ag_b2, L0_gnn_ag_w3, L0_gnn_ag_b3, L0_gnn_up_w1, L0_gnn_up_b1, L0_gnn_up_w2, L0_gnn_up_b2, L0_gnn_up_w3, L0_gnn_up_b3, L1_gnn_Wq1, L1_gnn_bq1, L1_gnn_Wk1, L1_gnn_bk1, L1_gnn_Wv1, L1_gnn_bv1, L1_gnn_Ws1, L1_gnn_bs1, L1_gnn_Wq2, L1_gnn_bq2, L1_gnn_Wk2, L1_gnn_bk2, L1_gnn_Wv2, L1_gnn_bv2, L1_gnn_Ws2, L1_gnn_bs2):
    import jax
    import jax.numpy as jnp

    def _L0_gnn_ref(nodes, edges, senders, receivers, msg_w1, msg_b1, msg_w2, msg_b2, msg_w3, msg_b3, ag_w1, ag_b1, ag_w2, ag_b2, ag_w3, ag_b3, up_w1, up_b1, up_w2, up_b2, up_w3, up_b3):
        import jax, jax.numpy as jnp
        import numpy as np
        N, E = (50000, 12500)
        D_NODE, D_EDGE = (128, 16)
        MSG_DIM, OUT_DIM = (128, 128)
        H_MSG, H_AGGR, H_UP = (256, 128, 256)

        def _dense(key, fin, fout):
            scale = jnp.sqrt(2.0 / (fin + fout)).astype(jnp.float32)
            w = jax.random.normal(key, (fin, fout), jnp.float32) * scale
            b = jnp.zeros((fout,), jnp.float32)
            return (w, b)
        n = nodes.shape[0]
        feats = jnp.concatenate([edges, nodes[senders], nodes[receivers]], axis=-1)
        h = jax.nn.relu(feats @ msg_w1 + msg_b1)
        h = h @ msg_w2 + msg_b2
        msgs = h @ msg_w3 + msg_b3
        g = jax.nn.relu(msgs @ ag_w1 + ag_b1)
        g = g @ ag_w2 + ag_b2
        gate = (g @ ag_w3 + ag_b3)[:, 0]
        seg_max = jax.ops.segment_max(gate, receivers, num_segments=n)
        w = jnp.exp(gate - seg_max[receivers])
        denom = jax.ops.segment_sum(w, receivers, num_segments=n)
        attn = w / denom[receivers]
        aggr = jax.ops.segment_sum(attn[:, None] * msgs, receivers, num_segments=n)
        u = jnp.concatenate([nodes, aggr], axis=-1)
        h = jax.nn.relu(u @ up_w1 + up_b1)
        h = h @ up_w2 + up_b2
        out = h @ up_w3 + up_b3
        return out

    def _L1_gnn_ref(x, edge_index, Wq1, bq1, Wk1, bk1, Wv1, bv1, Ws1, bs1, Wq2, bq2, Wk2, bk2, Wv2, bv2, Ws2, bs2):
        import jax, jax.numpy as jnp
        import numpy as np
        N = 50000
        E = 37500
        IN_DIM = 128
        HID = 16
        HEADS1 = 8
        OUT_DIM = 128
        EPS = 1e-16

        def _linear_params(key, fan_in, fan_out):
            kw, kb = jax.random.split(key)
            s = 1.0 / np.sqrt(fan_in)
            W = jax.random.uniform(kw, (fan_in, fan_out), minval=-s, maxval=s, dtype=jnp.float32)
            b = jax.random.uniform(kb, (fan_out,), minval=-s, maxval=s, dtype=jnp.float32)
            return (W, b)

        def _transformer_conv(x, src, dst, Wq, bq, Wk, bk, Wv, bv, Ws, bs, heads, ch):
            n = x.shape[0]
            q = (x @ Wq + bq).reshape(n, heads, ch)
            k = (x @ Wk + bk).reshape(n, heads, ch)
            v = (x @ Wv + bv).reshape(n, heads, ch)
            alpha = jnp.einsum('ehc,ehc->eh', q[dst], k[src]) / np.sqrt(ch)
            m = jax.ops.segment_max(alpha, dst, num_segments=n)
            m = jnp.where(jnp.isfinite(m), m, 0.0)
            ea = jnp.exp(alpha - jax.lax.stop_gradient(m)[dst])
            denom = jax.ops.segment_sum(ea, dst, num_segments=n)
            attn = ea / (denom[dst] + EPS)
            out = jax.ops.segment_sum(attn[:, :, None] * v[src], dst, num_segments=n)
            return out.reshape(n, heads * ch) + (x @ Ws + bs)
        src, dst = (edge_index[0], edge_index[1])
        h = _transformer_conv(x, src, dst, Wq1, bq1, Wk1, bk1, Wv1, bv1, Ws1, bs1, HEADS1, HID)
        out = _transformer_conv(h, src, dst, Wq2, bq2, Wk2, bk2, Wv2, bv2, Ws2, bs2, 1, OUT_DIM)
        return out
    edge_index = jnp.stack([src, dst])
    h = jnp.maximum(_layernorm(x, axis=-1), 0.0)
    x = x + _L0_gnn_ref(h, edge_attr_16, src, dst, L0_gnn_msg_w1, L0_gnn_msg_b1, L0_gnn_msg_w2, L0_gnn_msg_b2, L0_gnn_msg_w3, L0_gnn_msg_b3, L0_gnn_ag_w1, L0_gnn_ag_b1, L0_gnn_ag_w2, L0_gnn_ag_b2, L0_gnn_ag_w3, L0_gnn_ag_b3, L0_gnn_up_w1, L0_gnn_up_b1, L0_gnn_up_w2, L0_gnn_up_b2, L0_gnn_up_w3, L0_gnn_up_b3)
    h = jnp.maximum(_layernorm(x, axis=-1), 0.0)
    x = x + _L1_gnn_ref(h, edge_index, L1_gnn_Wq1, L1_gnn_bq1, L1_gnn_Wk1, L1_gnn_bk1, L1_gnn_Wv1, L1_gnn_bv1, L1_gnn_Ws1, L1_gnn_bs1, L1_gnn_Wq2, L1_gnn_bq2, L1_gnn_Wk2, L1_gnn_bk2, L1_gnn_Wv2, L1_gnn_bv2, L1_gnn_Ws2, L1_gnn_bs2)
    return x

_drawn_inputs = setup_inputs


def setup_inputs(seed=0):
    import zlib

    import numpy as np

    out = dict(_drawn_inputs(seed))
    spreads = {'L0_gnn_msg_b1': (0.0, 0.1),
     'L0_gnn_msg_b2': (0.0, 0.1),
     'L0_gnn_msg_b3': (0.0, 0.1),
     'L0_gnn_ag_b1': (0.0, 0.8),
     'L0_gnn_ag_b2': (0.0, 0.8),
     'L0_gnn_up_b1': (0.0, 0.1),
     'L0_gnn_up_b2': (0.0, 0.1),
     'L0_gnn_up_b3': (0.0, 0.1)}
    factors = {'L0_gnn_ag_w1': 3.474,
     'L0_gnn_ag_w2': 3.407,
     'L0_gnn_ag_w3': 2.938,
     'L1_gnn_Wq1': 8.0,
     'L1_gnn_bq1': 8.0,
     'L1_gnn_Wk1': 8.0,
     'L1_gnn_bk1': 8.0,
     'L1_gnn_Wq2': 8.0,
     'L1_gnn_bq2': 8.0,
     'L1_gnn_Wk2': 8.0,
     'L1_gnn_bk2': 8.0}
    for name, (base, spread) in spreads.items():
        noise = np.random.default_rng([zlib.crc32(name.encode()), seed]).standard_normal(out[name].shape)
        drawn = base * np.exp(spread * noise) if base else spread * noise
        out[name] = jnp.asarray(drawn.astype(out[name].dtype))
    for name, factor in factors.items():
        out[name] = (out[name] * factor).astype(out[name].dtype)
    return out
```

```python
import concourse.bass as bass
from concourse import mybir
from contextlib import ExitStack

F32 = mybir.dt.float32
BF16 = mybir.dt.bfloat16
I32 = mybir.dt.int32
ALU = mybir.AluOpType
ACT = mybir.ActivationFunctionType
AX = mybir.AxisListType

P = 128
N, E, D, DE = 3125, 50000, 128, 16
TILES = -(-N // P)
CHUNKS = -(-E // P)
LAST_ROWS = N - (TILES - 1) * P
FULL_CHUNKS = E // P
TAIL = E - FULL_CHUNKS * P
UNROLL = 8
STEPS = -(-(CHUNKS + TILES - 1) // UNROLL) * UNROLL
ITERS = STEPS // UNROLL
PAIRS = UNROLL // 2
ROWS = STEPS // 4
KB = -(-CHUNKS // P)
NO_NODE = TILES * P + 800.0
NOT_HERE = 255.0
BIG = 1.0e30
NPAD = TILES * P
HEADS = 8
HM = 256
LN_EPS = 1e-5
ATTN_EPS = 1e-16


class Stage:

    def __init__(self, nc, name):
        self.nc, self.name, self.ctx, self.sems = nc, name, ExitStack(), []

    def __enter__(self):
        self.ctx.__enter__()
        return self

    def __exit__(self, *a):
        self.ctx.__exit__(*a)
        if self.sems:
            self.nc.clear_and_free_semaphores(self.sems)
            self.nc.all_engine_barrier()

    def sb(self, name, shape, dt=F32):
        return self.ctx.enter_context(self.nc.sbuf_tensor(f"{self.name}_{name}", shape, dt))

    def ps(self, name, shape, dt=F32):
        return self.ctx.enter_context(self.nc.psum_tensor(f"{self.name}_{name}", shape, dt))

    def sem(self, name):
        self.sems.append(self.nc.alloc_semaphore(f"{self.name}_{name}"))
        return self.sems[-1]

    def block(self):
        return self.ctx.enter_context(self.nc.Block())


def linker(eng, sem):
    done = [0]

    def link(ins):
        done[0] += 1
        ins.then_inc(sem, 1)
        eng.wait_ge(sem, done[0])
    return link


def make_constants(nc, c):
    with Stage(nc, "const") as st:
        s_pool, s_made, s_int = st.sem("pool_chain"), st.sem("made"), st.sem("ints")
        node_i = st.sb("node_i", [P, P], I32)
        step_i = st.sb("step_i", [P, STEPS], I32)
        part_i = st.sb("part_i", [P, KB], I32)
        block = st.block()

        @block.gpsimd
        def _(pool):
            link = linker(pool, s_pool)
            nc.gpsimd.memset(c.ones[:], 1.0)
            link(nc.gpsimd.memset(c.ident[:], 0.0))
            nc.gpsimd.affine_select(out=c.ident[:], in_=c.ident[:], compare_op=ALU.not_equal, fill=1.0,
                                    base=0, pattern=[[-1, P]], channel_multiplier=1)
            nc.gpsimd.iota(node_i[:], [[1, P]], base=0, channel_multiplier=0).then_inc(s_int, 1)
            nc.gpsimd.iota(step_i[:], [[1, STEPS]], base=0, channel_multiplier=0).then_inc(s_int, 1)
            nc.gpsimd.iota(part_i[:], [[P, KB]], base=0, channel_multiplier=1).then_inc(s_int, 1)

        @block.vector
        def _(dve):
            dve.wait_ge(s_int, 3)
            nc.vector.tensor_copy(c.node_row[:], node_i[:])
            nc.vector.tensor_copy(c.step_row[:], step_i[:])
            nc.vector.tensor_copy(c.part_col[:], part_i[:])


def plan_steps(nc, c, src, dst):
    with Stage(nc, "plan") as st:
        ends = st.sb("ends", [P, KB * P], I32)
        starts = st.sb("starts", [P, KB * P], I32)
        endf = st.sb("endf", [P, KB * P])
        startf = st.sb("startf", [P, KB * P])
        junk = st.sb("junk", [P, KB * P])
        count = st.sb("count", [P, TILES - 1])
        count_i = st.sb("count_i", [P, TILES - 1], I32)
        chunk_i = st.sb("chunk_i", [P, TILES - 1], I32)
        turn = st.sb("turn", [P, TILES - 1])
        tile = st.sb("tile", [P, STEPS])
        chunk = st.sb("chunk", [P, STEPS])
        pick = st.sb("pick", [P, KB, STEPS])
        dst_slot = st.sb("dst_slot", [P, STEPS])
        local = st.sb("local", [P, STEPS])
        valid = st.sb("valid", [P, STEPS])
        upper = st.sb("upper", [P, STEPS])
        key = st.sb("key", [P, STEPS])
        local_row = st.sb("local_row", [ROWS, 4 * P], BF16)
        key_row = st.sb("key_row", [ROWS, 4 * P])
        key_prev = st.sb("key_prev", [ROWS, 4 * P])
        key_next = st.sb("key_next", [ROWS, 4 * P])
        fence = st.sb("fence", [1, 2])
        flag = st.sb("flag", [ROWS, 4])
        flag8 = st.sb("flag8", [ROWS, 16])
        ps_count = st.ps("count_ps", [P, TILES - 1])
        ps_dst = st.ps("dst_ps", [P, STEPS])
        ps_src = st.ps("src_ps", [P, STEPS])
        ps_row = [st.ps(f"row_ps{i}", [ROWS, 4 * P]) for i in range(2)]
        ps_flag = st.ps("flag_ps", [8, 2 * P])
        s_padded, s_in, s_counted, s_total = (st.sem(n) for n in ("padded", "in", "counted", "total"))
        s_picked, s_slots, s_local, s_turned = (st.sem(n) for n in ("picked", "slots", "local", "turned"))
        s_rows, s_out, s_shift, s_dve = (st.sem(n) for n in ("rows", "out", "shift", "dve_chain"))
        s_flag, s_flagt = st.sem("flag"), st.sem("flagt")
        block = st.block()

        @block.sync
        def _(sp):
            sp.wait_ge(s_padded, 2)
            for to, of in ((ends, dst), (starts, src)):
                whole = (KB - 1) * P * P
                sp.dma_start(to[:, 0:(KB - 1) * P].rearrange("q (k p) -> q k p", p=P),
                             of[0:whole].rearrange("(k q p) -> q k p", q=P, p=P)).then_inc(s_in, 16)
                rows = FULL_CHUNKS - (KB - 1) * P
                sp.dma_start(to[0:rows, (KB - 1) * P:KB * P],
                             of[whole:FULL_CHUNKS * P].rearrange("(q p) -> q p", p=P)).then_inc(s_in, 16)
                sp.dma_start(to[rows:rows + 1, (KB - 1) * P:(KB - 1) * P + TAIL],
                             of[FULL_CHUNKS * P:E].rearrange("(q p) -> q p", q=1)).then_inc(s_in, 16)
            sp.wait_ge(s_rows, 2)
            sp.dma_start(c.local_dram.rearrange("(r s) -> r s", r=ROWS), local_row[:]).then_inc(s_out, 16)
            sp.dma_start(c.key_dram[1:1 + STEPS * P].rearrange("(r s) -> r s", r=ROWS), key_row[:]).then_inc(s_out, 16)
            sp.dma_start(c.key_dram[0:1].rearrange("(a b) -> a b", a=1), fence[0:1, 0:1]).then_inc(s_out, 16)
            sp.dma_start(c.key_dram[1 + STEPS * P:2 + STEPS * P].rearrange("(a b) -> a b", a=1),
                         fence[0:1, 1:2]).then_inc(s_out, 16)
            sp.wait_ge(s_out, 64)
            sp.dma_start(key_prev[:], c.key_dram[0:STEPS * P].rearrange("(r s) -> r s", r=ROWS)).then_inc(s_shift, 16)
            sp.dma_start(key_next[:], c.key_dram[2:2 + STEPS * P].rearrange("(r s) -> r s", r=ROWS)).then_inc(s_shift, 16)

        @block.vector
        def _(dve):
            link = linker(dve, s_dve)
            v = nc.vector
            v.memset(ends[:, (KB - 1) * P:KB * P], int(NO_NODE)).then_inc(s_padded, 1)
            v.memset(starts[:, (KB - 1) * P:KB * P], 0).then_inc(s_padded, 1)
            v.memset(fence[:], -5.0)
            dve.wait_ge(s_in, 96)
            v.tensor_copy(startf[:], starts[:])
            link(v.tensor_copy(endf[:], ends[:]))
            for t in range(TILES - 1):
                v.tensor_scalar(junk[:], endf[:], float(P * (t + 1)), 0.0, ALU.is_lt, ALU.add,
                                accum_out=count[:, t:t + 1]).then_inc(s_counted, 1)
                dve.wait_ge(s_counted, t + 1)
            dve.wait_ge(s_total, 1)
            link(v.tensor_copy(count_i[:], ps_count[:]))
            link(v.tensor_single_scalar(chunk_i[:], count_i[:], 7, ALU.arith_shift_right))
            link(v.tensor_copy(turn[:], chunk_i[:]))
            link(v.tensor_tensor(turn[:], turn[:], c.step_row[:, 0:TILES - 1], ALU.add))
            link(v.memset(tile[:], 0.0))
            for t in range(TILES - 1):
                link(v.scalar_tensor_tensor(tile[:], c.step_row[:], turn[:, t:t + 1], tile[:], ALU.is_gt, ALU.add))
            link(v.tensor_tensor(chunk[:], c.step_row[:], tile[:], ALU.subtract))
            for k in range(KB):
                ins = v.tensor_scalar(pick[:, k, :], chunk[:], c.part_col[:, k:k + 1], None, ALU.is_equal)
                ins.then_inc(s_picked, 1)
            v.tensor_copy(c.tile_at[:], tile[0:1, :])
            v.tensor_copy(c.chunk_at[:], chunk[0:1, :])
            dve.wait_ge(s_slots, 1)
            link(v.tensor_copy(dst_slot[:], ps_dst[:]))
            v.tensor_copy(c.src_slot[:, 0:STEPS], ps_src[:])
            v.memset(c.src_slot[:, STEPS:], 0)
            link(v.scalar_tensor_tensor(local[:], tile[:], -float(P), dst_slot[:], ALU.mult, ALU.add))
            v.tensor_scalar(upper[:], local[:], float(P), None, ALU.is_lt)
            link(v.tensor_scalar(valid[:], local[:], 0.0, None, ALU.is_ge))
            link(v.tensor_tensor(valid[:], valid[:], upper[:], ALU.mult))
            link(v.scalar_tensor_tensor(c.local[:], local[:], -NOT_HERE, valid[:], ALU.add, ALU.mult))
            link(v.tensor_scalar(c.local[:], c.local[:], NOT_HERE, None, ALU.add))
            link(v.scalar_tensor_tensor(key[:], dst_slot[:], 1.0, valid[:], ALU.add, ALU.mult))
            v.tensor_copy(fence[:], fence[:]).then_inc(s_local, 1)
            dve.wait_ge(s_turned, 2)
            v.tensor_copy(local_row[:], ps_row[0][:]).then_inc(s_rows, 1)
            v.tensor_copy(key_row[:], ps_row[1][:]).then_inc(s_rows, 1)
            dve.wait_ge(s_rows, 2)
            dve.wait_ge(s_shift, 32)
            link(v.tensor_tensor(c.start_big[:], key_row[:], key_prev[:], ALU.not_equal))
            link(v.tensor_tensor(c.last[:], key_row[:], key_next[:], ALU.not_equal))
            link(v.reduce_max(flag[:, 0:1], c.start_big[:], AX.X))
            link(v.tensor_scalar(c.start_big[:], c.start_big[:], -BIG, None, ALU.mult))
            link(v.tensor_scalar(c.not_last[:], c.last[:], -1.0, 1.0, ALU.mult, ALU.add))
            link(v.tensor_reduce(flag[:, 1:2], c.not_last[:], AX.X, ALU.min))
            link(v.tensor_scalar(flag[:, 0:1], flag[:, 0:1], -BIG, None, ALU.mult))
            link(v.tensor_copy(flag8[:, 0:8], flag[:, 0:1].to_broadcast([ROWS, 8])))
            v.tensor_copy(flag8[:, 8:16], flag[:, 1:2].to_broadcast([ROWS, 8])).then_inc(s_flag, 1)
            dve.wait_ge(s_flagt, 1)
            v.tensor_copy(c.row_start[:], ps_flag[:, 0:ROWS])
            v.tensor_copy(c.row_open[:], ps_flag[:, P:P + ROWS])

        @block.tensor
        def _(pe):
            pe.wait_ge(s_counted, TILES - 1)
            nc.tensor.matmul(ps_count[:], c.ones[:], count[:], start=True, stop=True).then_inc(s_total, 1)
            pe.wait_ge(s_picked, KB)
            for ps, rows in ((ps_dst, endf), (ps_src, startf)):
                for k in range(KB):
                    last = nc.tensor.matmul(ps[:], rows[:, k * P:(k + 1) * P], pick[:, k, :],
                                            start=(k == 0), stop=(k == KB - 1))
            last.then_inc(s_slots, 1)
            pe.wait_ge(s_local, 1)
            for ps, x in zip(ps_row, (c.local, key)):
                for a in range(4):
                    last = nc.tensor.transpose(ps[:, a * P:(a + 1) * P],
                                               x[:].rearrange("p (r a) -> p a r", a=4)[:, a, :], c.ident[:])
                last.then_inc(s_turned, 1)
            pe.wait_ge(s_flag, 1)
            nc.tensor.transpose(ps_flag[:, 0:ROWS], flag8[:, 0:8], c.ident[0:ROWS, 0:ROWS])
            nc.tensor.transpose(ps_flag[:, P:P + ROWS], flag8[:, 8:16],
                                c.ident[0:ROWS, 0:ROWS]).then_inc(s_flagt, 1)



def fold_weights(nc, c, a):
    with Stage(nc, "fold") as st:
        w2 = st.sb("w2", [P, 2, HM])
        w3 = st.sb("w3", [P, 2, D])
        u2 = st.sb("u2", [P, 2, HM])
        u3 = st.sb("u3", [P, 2, D])
        w2t = st.sb("w2t", [P, 2, HM])
        u2t = st.sb("u2t", [P, 2, HM])
        w23t = st.sb("w23t", [P, HM])
        ag1, ag2, ag2t = (st.sb(n, [P, D]) for n in ("ag1", "ag2", "ag2t"))
        ag3 = st.sb("ag3", [P, 1])
        cols = st.sb("cols", [P, 8])
        rows = st.sb("rows", [1, 2 * D + 2])
        agb2 = st.sb("agb2", [P, P])
        pt = [st.ps(f"turn{i}", [P, 4 * P]) for i in range(2)]
        pa = st.ps("pa", [P, 4 * P])
        pw, pg, pu, px = (st.ps(n, [P, 4 * P]) for n in ("pw", "pg", "pu", "px"))
        s_in, s_turn, s_flat, s_mm = (st.sem(n) for n in ("in", "turn", "flat", "mm"))
        s_mid, s_g, s_b23, s_bcol = (st.sem(n) for n in ("mid", "g", "b23", "bcol"))
        s_x, s_bg = st.sem("x"), st.sem("bg")
        LOADS = []

        def col(name, k):
            return a[name][k * P:(k + 1) * P].rearrange("(p o) -> p o", o=1)

        def row(name):
            return a[name].rearrange("(o n) -> o n", o=1)

        pre = "L0_gnn_"
        LOADS += [(w2[:], a[pre + "msg_w2"].rearrange("(k p) n -> p k n", p=P)),
                  (w3[:], a[pre + "msg_w3"].rearrange("(k p) n -> p k n", p=P)),
                  (u2[:], a[pre + "up_w2"].rearrange("(k p) n -> p k n", p=P)),
                  (u3[:], a[pre + "up_w3"].rearrange("(k p) n -> p k n", p=P)),
                  (c.up1[:], a[pre + "up_w1"].rearrange("(k p) n -> p k n", p=P)),
                  (c.w_edge[:], a[pre + "msg_w1"][0:DE, :]),
                  (c.w_node[0][:, HM:2 * HM], a[pre + "msg_w1"][DE:DE + D, :]),
                  (c.w_node[0][:, 0:HM], a[pre + "msg_w1"][DE + D:DE + 2 * D, :]),
                  (c.b_node[0][:, 0:HM], row(pre + "msg_b1")),
                  (ag1[:], a[pre + "ag_w1"]), (ag2[:], a[pre + "ag_w2"]), (ag3[:], a[pre + "ag_w3"]),
                  (cols[:, 0:1], col(pre + "msg_b2", 0)), (cols[:, 1:2], col(pre + "msg_b2", 1)),
                  (cols[:, 2:3], col(pre + "msg_b3", 0)), (cols[:, 3:4], col(pre + "ag_b1", 0)),
                  (cols[:, 4:5], col(pre + "ag_b2", 0)),
                  (cols[:, 5:6], col(pre + "up_b2", 0)), (cols[:, 6:7], col(pre + "up_b2", 1)),
                  (c.up_b1[:, 0:1], col(pre + "up_b1", 0)), (c.up_b1[:, 1:2], col(pre + "up_b1", 1)),
                  (rows[:, 0:D], row(pre + "msg_b3")), (rows[:, D:2 * D], row(pre + "up_b3")),
                  (rows[:, 2 * D:2 * D + 1], row(pre + "ag_b3"))]
        for layer in (1, 2):
            for n, x in enumerate("qkvs"):
                LOADS.append((c.w_node[layer][:, n * D:(n + 1) * D], a[f"L1_gnn_W{x}{layer}"]))
                LOADS.append((c.b_node[layer][:, n * D:(n + 1) * D], row(f"L1_gnn_b{x}{layer}")))
        block = st.block()

        @block.sync
        def _(sp):
            for to, of in LOADS:
                sp.dma_start(to, of).then_inc(s_in, 16)

        @block.tensor
        def _(pe):
            mm = nc.tensor.matmul
            pe.wait_ge(s_in, 16 * len(LOADS))
            for x, ps in ((w2, pt[0]), (u2, pt[1])):
                for k in range(2):
                    for i in range(2):
                        last = nc.tensor.transpose(ps[:, (k * 2 + i) * P:(k * 2 + i + 1) * P],
                                                   x[:, i, k * P:(k + 1) * P], c.ident[:])
            last = nc.tensor.transpose(pa[:, 0:P], ag2[:], c.ident[:])
            last.then_inc(s_turn, 1)
            pe.wait_ge(s_flat, 3)
            for k in range(2):
                mm(pw[:, 0:HM], w3[:, k, :], w2t[:, k, :], start=(k == 0), stop=(k == 1))
            for i in range(2):
                for k in range(2):
                    mm(pg[:, i * P:(i + 1) * P], w2t[:, k, i * P:(i + 1) * P], w3[:, k, :],
                       start=(k == 0), stop=(k == 1))
            for i in range(2):
                for k in range(2):
                    last = mm(pu[:, i * P:(i + 1) * P], u2t[:, k, i * P:(i + 1) * P], u3[:, k, :],
                              start=(k == 0), stop=(k == 1))
            for k in range(2):
                mm(px[:, 0:1], w3[:, k, :], cols[:, k:k + 1], start=(k == 0), stop=(k == 1))
            mm(px[:, 1:2], ag2t[:], ag3[:], start=True, stop=True)
            mm(px[:, 2:3], agb2[:], ag3[:], start=True, stop=False)
            mm(px[:, 2:3], c.ones[0:1, :], rows[0:1, 2 * D:2 * D + 1], start=False, stop=True)
            for to, b, w, r in ((px[0:1, P:2 * P], 0, w3, 0), (px[0:1, 2 * P:3 * P], 5, u3, D)):
                for k in range(2):
                    mm(to, cols[:, b + k:b + k + 1], w[:, k, :], start=(k == 0), stop=False)
                last = mm(to, c.ones[0:1, 0:1], rows[0:1, r:r + D], start=False, stop=True)
            last.then_inc(s_mm, 1)
            pe.wait_ge(s_mid, 2)
            for i in range(2):
                mm(pa[:, P + i * P:P + (i + 1) * P], w23t[:, i * P:(i + 1) * P], ag1[:], start=True, stop=True)
            mm(pa[:, 3 * P:3 * P + 1], ag1[:], cols[:, 7:8], start=True, stop=True).then_inc(s_g, 1)

        @block.vector
        def _(dve):
            v = nc.vector
            dve.wait_ge(s_in, 16 * len(LOADS))
            v.memset(c.b_node[0][:, HM:2 * HM], 0.0)
            v.tensor_copy(agb2[:], cols[:, 4:5].to_broadcast([P, P])).then_inc(s_flat, 1)
            dve.wait_ge(s_turn, 1)
            v.tensor_copy(w2t[:].rearrange("p k n -> p (k n)"), pt[0][:])
            v.tensor_copy(ag2t[:], pa[:, 0:P]).then_inc(s_flat, 1)
            v.tensor_copy(u2t[:].rearrange("p k n -> p (k n)"), pt[1][:]).then_inc(s_flat, 1)
            dve.wait_ge(s_mm, 1)
            v.tensor_copy(w23t[:], pw[:, 0:HM]).then_inc(s_mid, 1)
            v.tensor_tensor(cols[:, 7:8], px[:, 0:1], cols[:, 2:3], ALU.add).then_inc(s_mid, 1)
            v.tensor_copy(c.w23[:].rearrange("p k n -> p (k n)"), pg[:, 0:HM])
            v.tensor_copy(c.u23[:].rearrange("p k n -> p (k n)"), pu[:, 0:HM])
            v.tensor_copy(c.gate_w[:], px[:, 1:2])
            v.tensor_copy(c.gate_b[:], px[:, 2:3])
            v.tensor_copy(c.b23[:], px[0:1, P:2 * P])
            v.tensor_copy(c.ub23[:], px[0:1, 2 * P:3 * P])
            dve.wait_ge(s_g, 1)
            v.tensor_copy(c.wg[:].rearrange("p k n -> p (k n)"), pa[:, P:3 * P])
            v.tensor_tensor(c.bg[:], pa[:, 3 * P:3 * P + 1], cols[:, 3:4], ALU.add)


def load_nodes(nc, c, x):
    with Stage(nc, "load") as st:
        s_zero, s_in = st.sem("zero"), st.sem("in")
        block = st.block()

        @block.vector
        def _(dve):
            nc.vector.memset(c.x[:, TILES - 1, :], 0.0).then_inc(s_zero, 1)

        @block.sync
        def _(sp):
            sp.wait_ge(s_zero, 1)
            for t in range(TILES - 1):
                sp.dma_start(c.x[:, t, :], x[t * P:(t + 1) * P, :]).then_inc(s_in, 16)
            sp.dma_start(c.x[0:LAST_ROWS, TILES - 1, :], x[(TILES - 1) * P:N, :]).then_inc(s_in, 16)
            sp.wait_ge(s_in, 16 * TILES)


def layer_norm(nc, c, name):
    with Stage(nc, name) as st:
        sq = st.sb("sq", [P, TILES, D])
        mean, var, std, rstd = (st.sb(n, [P, TILES]) for n in ("mean", "var", "std", "rstd"))
        s_chain, s_cent, s_sq, s_var, s_std = (st.sem(n) for n in ("chain", "cent", "sq", "var", "std"))
        block = st.block()

        @block.vector
        def _(dve):
            v = nc.vector
            link = linker(dve, s_chain)
            link(v.tensor_reduce(mean[:], c.x[:], AX.X, ALU.add))
            link(v.tensor_scalar(mean[:], mean[:], 1.0 / D, None, ALU.mult))
            v.tensor_tensor(c.h[:], c.x[:], mean[:].unsqueeze(2).to_broadcast([P, TILES, D]),
                            ALU.subtract).then_inc(s_cent, 1)
            dve.wait_ge(s_sq, 1)
            link(v.tensor_reduce(var[:], sq[:], AX.X, ALU.add))
            v.tensor_scalar(var[:], var[:], 1.0 / D, LN_EPS, ALU.mult, ALU.add).then_inc(s_var, 1)
            dve.wait_ge(s_std, 1)
            link(v.reciprocal(rstd[:], std[:]))
            link(v.tensor_tensor(std[:], rstd[:], rstd[:], ALU.mult))
            link(v.tensor_tensor(std[:], std[:], var[:], ALU.mult))
            link(v.tensor_scalar(std[:], std[:], -0.5, 1.5, ALU.mult, ALU.add))
            link(v.tensor_tensor(rstd[:], rstd[:], std[:], ALU.mult))
            v.scalar_tensor_tensor(c.h[:], c.h[:], 0.0, rstd[:].unsqueeze(2).to_broadcast([P, TILES, D]),
                                   ALU.max, ALU.mult)

        @block.scalar
        def _(act):
            act.wait_ge(s_cent, 1)
            nc.scalar.activation(sq[:], c.h[:], ACT.Square).then_inc(s_sq, 1)
            act.wait_ge(s_var, 1)
            nc.scalar.activation(std[:], var[:], ACT.Sqrt).then_inc(s_std, 1)


GROUP = 5
GROUPS = TILES // GROUP


def project(nc, c, name, layer, table_width, scale, table, keep_ht):
    Q = table_width
    w, b = c.w_node[layer], c.b_node[layer]
    with Stage(nc, name) as st:
        hs = st.sb("hs", [P, GROUP, D])
        ht = st.sb("ht", [P, GROUP, P])
        kv = st.sb("kv", [P, GROUP, HM])
        rest = st.sb("rest", [P, GROUP, Q])
        rest2 = st.sb("rest2", [P, GROUP, Q])
        p_t = [st.ps(f"t{i}", [P, 4 * P]) for i in range(2)]
        p_o = [st.ps(f"o{i}", [P, 4 * P]) for i in range(GROUP)]
        s_t, s_ht, s_o = (st.sem(n) for n in ("t", "ht", "o"))
        s_kv, s_rest, s_mid = (st.sem(n) for n in ("kv", "rest", "mid"))
        s_out, s_hs, s_kept = st.sem("out"), st.sem("hs"), st.sem("kept")
        block = st.block()

        banks = ((0, 4), (4, GROUP))

        @block.gpsimd
        def _(pool):
            def body(g):
                if not isinstance(g, int):
                    pool.wait_ge(s_t, 2 * g)
                nc.gpsimd.tensor_copy(hs[:], c.h[:, bass.ds(g * GROUP, GROUP), :]).then_inc(s_hs, 1)

            body(0)
            with pool.Fori(1, GROUPS) as g:
                body(g)

        @block.tensor
        def _(pe):
            def body(g):
                pe.wait_ge(s_hs, g + 1)
                for n, (first, end) in enumerate(banks):
                    if not isinstance(g, int):
                        pe.wait_ge(s_ht, 2 * g + n - 1)
                    for j in range(first, end):
                        last = nc.tensor.transpose(p_t[n][:, (j - first) * P:(j - first + 1) * P], hs[:, j, :],
                                                   c.ident[:])
                    last.then_inc(s_t, 1)
                for j in range(GROUP):
                    pe.wait_ge(s_ht, 2 * g + 1 + j // 4)
                    if not isinstance(g, int):
                        pe.wait_ge(s_rest, g * GROUP + j - GROUP + 1)
                    nc.tensor.matmul(p_o[j][:], ht[:, j, :], w[:], start=True, stop=False)
                    nc.tensor.matmul(p_o[j][:], c.ones[0:1, :], b[:], start=False, stop=True).then_inc(s_o, 1)

            body(0)
            with pe.Fori(1, GROUPS) as g:
                body(g)

        @block.scalar
        def _(act):
            def body(g):
                for n, (first, end) in enumerate(banks):
                    act.wait_ge(s_t, 2 * g + n + 1)
                    if not isinstance(g, int):
                        act.wait_ge(s_o, g * GROUP + end - GROUP)
                        if keep_ht:
                            act.wait_ge(s_kept, 1 + 2 * g + n - 2)
                    nc.scalar.copy(ht[:, first:end, :].rearrange("p j n -> p (j n)"),
                                   p_t[n][:, 0:(end - first) * P]).then_inc(s_ht, 1)
                for j in range(GROUP):
                    act.wait_ge(s_o, g * GROUP + j + 1)
                    nc.scalar.activation(table[:, bass.ds(g * GROUP + j, 1), 0, :].rearrange("p o d -> p (o d)"),
                                         p_o[j][:, 0:Q], ACT.Copy, scale=scale)
                    if not isinstance(g, int):
                        act.wait_ge(s_out, 16 * g)
                    ins = nc.scalar.copy(kv[:, j, :], p_o[j][:, Q:Q + HM])
                    if 4 * P > Q + HM:
                        nc.scalar.copy(c.skip[:, bass.ds(g * GROUP + j, 1), :].rearrange("p o d -> p (o d)"),
                                       p_o[j][:, Q + HM:4 * P]).then_inc(s_kv, 1)
                    else:
                        ins.then_inc(s_kv, 1)

            body(0)
            with act.Fori(1, GROUPS) as g:
                body(g)

        @block.vector
        def _(dve):
            v = nc.vector

            def body(g):
                def part(j, s):
                    return table[:, bass.ds(g * GROUP + j, 1), s, :].rearrange("p o d -> p (o d)")
                for n, (first, end) in enumerate(banks):
                    if keep_ht:
                        dve.wait_ge(s_ht, 2 * g + n + 1)
                        v.tensor_copy(c.ht[:, bass.ds(g * GROUP + first, end - first), :],
                                      ht[:, first:end, :]).then_inc(s_kept, 1)
                for j in range(GROUP):
                    dve.wait_ge(s_kv, g * GROUP + j + 1)
                    v.scalar_tensor_tensor(rest[:, j, :], p_o[j][:, 0:Q], scale, part(j, 0),
                                           ALU.mult, ALU.subtract).then_inc(s_rest, 1)
                    dve.wait_ge(s_rest, g * GROUP + j + 1)
                    v.tensor_copy(part(j, 1), rest[:, j, :]).then_inc(s_mid, 1)
                    dve.wait_ge(s_mid, g * GROUP + j + 1)
                    v.tensor_tensor(part(j, 2), rest[:, j, :], part(j, 1), ALU.subtract)

            body(0)
            with dve.Fori(1, GROUPS) as g:
                body(g)

        @block.sync
        def _(sp):
            rows = c.gather_dram.rearrange("(g j p) d -> g p j d", p=P, j=GROUP)

            def body(g):
                sp.wait_ge(s_kv, GROUP * g + GROUP)
                sp.dma_start(rows[bass.ds(g, 1)].rearrange("o p j d -> (o p) j d"), kv[:]).then_inc(s_out, 16)

            body(0)
            with sp.Fori(1, GROUPS) as g:
                body(g)
            sp.wait_ge(s_out, 16 * GROUPS)


def need(eng, sem, value):
    if not isinstance(value, int) or value > 0:
        eng.wait_ge(sem, value)


def skewed(eng, stages, depth):
    def run(it, k):
        for lag, stage in stages:
            if isinstance(it, int) and it == 0 and k < lag:
                continue
            if isinstance(it, int) and it == ITERS and k >= lag:
                continue
            if k >= lag:
                stage(it, k - lag)
            else:
                stage(it - 1, k - lag + PAIRS)

    for k in range(PAIRS):
        run(0, k)
    with eng.Fori(1, ITERS) as it:
        for k in range(PAIRS):
            run(it, k)
    for k in range(depth):
        run(ITERS, k)


def edge_scores(nc, c, name, heads, messages, table):
    Q = HM if messages else D
    with Stage(nc, name) as st:
        got = st.sb("got", [P, PAIRS, 2, HM])
        local = st.sb("local", [P, PAIRS, 2 * P], BF16)
        hot = st.sb("hot", [P, 2, 2 * P], BF16)
        index = st.sb("index", [P, 2, 4], I32)
        prod = st.sb("prod", [P, 2, 2, D])
        attr = st.sb("attr", [P, PAIRS, 2, DE])
        attr_t = st.sb("attr_t", [DE, 2, 2 * P])
        hid_t = st.sb("hid_t", [P, 2, 2, 2 * P])
        gate = st.sb("gate", [P, 2, 2 * P])
        p_dst = [st.ps(f"dst{i}", [P, 2 * HM]) for i in range(2)]
        p_hid = [st.ps(f"hid{i}", [P, 4 * P]) for i in range(2)]
        p_gate = [st.ps(f"gate{i}", [P, 4 * P]) for i in range(2)]
        p_attr = st.ps("attr_ps", [DE, 4 * P])
        s_got = [st.sem(f"got{k}") for k in range(PAIRS)]
        s_local = [st.sem(f"local{k}") for k in range(PAIRS)]
        s_attr = [st.sem(f"attr{k}") for k in range(PAIRS)]
        s_stored = [st.sem(f"stored{k}") for k in range(PAIRS)]
        s_index, s_hot, s_dst, s_sum, s_clear = (st.sem(n) for n in ("index", "hot", "dst", "sum", "clear"))
        s_aturn, s_attr_t, s_hturn, s_hid_t = (st.sem(n) for n in ("aturn", "attr_t", "hturn", "hid_t"))
        s_gmm, s_gate, s_dot, s_score = (st.sem(n) for n in ("gmm", "gate_s", "dot", "score"))
        block = st.block()
        payload = c.payload_dram[0:STEPS * P * Q].rearrange("(q p f) -> q p f", p=P, f=2 * Q)
        local_rows = c.local_dram.rearrange("(q s) -> q s", s=2 * P)

        @block.sync
        def _(sp):
            def load(it, k):
                q = it * PAIRS + k
                need(sp, s_hot, q - PAIRS + 1)
                sp.dma_start(local[:, k, :], local_rows[bass.ds(q, 1), :].to_broadcast([P, 2 * P])).then_inc(s_local[k], 16)
                if messages:
                    need(sp, s_aturn, q - PAIRS + 1)
                    for j in range(2):
                        chunk = sp.value_load(c.chunk_at[0:1, bass.ds(2 * q + j, 1)], min_val=0, max_val=CHUNKS)
                        sp.dma_start(attr[:, k, j, :], c.attr_dram[bass.ds(chunk * P, P), :]).then_inc(s_attr[k], 16)

            def store(it, k):
                q = it * PAIRS + k
                if messages:
                    sp.wait_ge(s_sum, q + 1)
                    of = got[:, k, :, :].rearrange("p j f -> p (j f)")
                    sp.dma_start(payload[bass.ds(q, 1), :, :].rearrange("o p f -> (o p) f"), of).then_inc(s_stored[k], 16)
                else:
                    sp.wait_ge(s_got[k], 32 * it + 32)
                    sp.dma_start(payload[bass.ds(q, 1), :, :].rearrange("o p (j f) -> (o p) j f", j=2),
                                 got[:, k, :, D:2 * D]).then_inc(s_stored[k], 16)

            skewed(sp, [(0, load), (2, store)], 2)
            for k in range(PAIRS):
                sp.wait_ge(s_stored[k], 16 * ITERS)

        @block.gpsimd
        def _(pool):
            def gather(it, k):
                q = it * PAIRS + k
                if k % 2 == 0:
                    pool.wait_ge(s_index, 2 * it + k // 2 + 1)
                need(pool, s_stored[k], 16 * it)
                need(pool, s_hturn if messages else s_sum, q - PAIRS + 1)
                pool.sem_inc(s_clear, 1)
                for j in range(2):
                    nc.gpsimd.indirect_dma_start(
                        got[:, k, j, :], None, c.gather_dram[:, :],
                        bass.IndirectOffsetOnAxis(ap=index[:, k // 2, k % 2 * 2 + j:k % 2 * 2 + j + 1], axis=0),
                    ).then_inc(s_got[k], 16)

            skewed(pool, [(0, gather)], 0)

        @block.tensor
        def _(pe):
            def turn_attr(it, k):
                q = it * PAIRS + k
                pe.wait_ge(s_attr[k], 32 * it + 32)
                need(pe, s_attr_t, q)
                for j in range(2):
                    last = nc.tensor.transpose(p_attr[:, j * P:(j + 1) * P], attr[:, k, j, :], c.ident[:])
                last.then_inc(s_aturn, 1)

            def pick(it, k):
                q, s = it * PAIRS + k, k % 2
                pe.wait_ge(s_hot, q + 1)
                need(pe, s_sum, q - 1)
                if messages:
                    pe.wait_ge(s_attr_t, q + 1)
                for j in range(2):
                    tile = pe.value_load(c.tile_at[0:1, bass.ds(2 * q + j, 1)], min_val=0, max_val=TILES - 1)
                    to = p_dst[s][:, j * Q:(j + 1) * Q]
                    for part in range(3):
                        last = nc.tensor.matmul(to, hot[:, s, j * P:(j + 1) * P],
                                                table[:, bass.ds(tile, 1), part, :].rearrange("p o d -> p (o d)"),
                                                start=(part == 0), stop=(part == 2 and not messages))
                    if messages:
                        last = nc.tensor.matmul(to, attr_t[:, s, j * P:(j + 1) * P], c.w_edge[:],
                                                start=False, stop=True)
                last.then_inc(s_dst, 1)

            def turn_hidden(it, k):
                q, s = it * PAIRS + k, k % 2
                pe.wait_ge(s_sum, q + 1)
                need(pe, s_hid_t, q - 1)
                for f in range(2):
                    for j in range(2):
                        last = nc.tensor.transpose(p_hid[s][:, (f * 2 + j) * P:(f * 2 + j + 1) * P],
                                                   got[:, k, j, f * P:(f + 1) * P], c.ident[:])
                last.then_inc(s_hturn, 1)

            def gate_hidden(it, k):
                q, s = it * PAIRS + k, k % 2
                pe.wait_ge(s_hid_t, q + 1)
                need(pe, s_score, q - 1)
                for f in range(2):
                    last = nc.tensor.matmul(p_gate[s][:, 0:2 * P], c.wg[:, f, :], hid_t[:, s, f, :],
                                            start=(f == 0), stop=(f == 1))
                last.then_inc(s_gmm, 1)

            def gate_score(it, k):
                q, s = it * PAIRS + k, k % 2
                pe.wait_ge(s_gate, q + 1)
                for j in range(2):
                    last = nc.tensor.matmul(p_gate[s][:, j:j + 1], gate[:, s, j * P:(j + 1) * P], c.gate_w[:],
                                            start=True, stop=True)
                last.then_inc(s_dot, 1)

            if messages:
                skewed(pe, [(4, gate_score), (3, gate_hidden), (2, turn_hidden), (1, pick), (0, turn_attr)], 4)
            else:
                skewed(pe, [(0, pick)], 0)

        if messages:
            @block.scalar
            def _(act):
                def keep_attr(it, k):
                    q, s = it * PAIRS + k, k % 2
                    act.wait_ge(s_aturn, q + 1)
                    need(act, s_dst, q - 1)
                    nc.scalar.copy(attr_t[:, s, :], p_attr[:, 0:2 * P]).then_inc(s_attr_t, 1)

                def relu_hidden(it, k):
                    q, s = it * PAIRS + k, k % 2
                    act.wait_ge(s_hturn, q + 1)
                    need(act, s_gmm, q - 1)
                    nc.scalar.activation(hid_t[:, s, :, :].rearrange("p f e -> p (f e)"), p_hid[s][:],
                                         ACT.Relu).then_inc(s_hid_t, 1)

                def relu_gate(it, k):
                    q, s = it * PAIRS + k, k % 2
                    act.wait_ge(s_gmm, q + 1)
                    need(act, s_dot, q - 1)
                    nc.scalar.activation(gate[:, s, :], p_gate[s][:, 0:2 * P], ACT.Relu,
                                         bias=c.bg[:]).then_inc(s_gate, 1)

                skewed(act, [(3, relu_gate), (2, relu_hidden), (0, keep_attr)], 3)

        @block.vector
        def _(dve):
            v = nc.vector

            def indices(half, step):
                v.tensor_copy(index[:, half, :], c.src_slot[:, bass.ds(step, 4)]).then_inc(s_index, 1)

            def one_hot(it, k):
                q, s = it * PAIRS + k, k % 2
                dve.wait_ge(s_local[k], 16 * it + 16)
                need(dve, s_dst, q - 1)
                v.tensor_scalar(hot[:, s, :], local[:, k, :], c.part_col[:, 0:1], None,
                                ALU.is_equal).then_inc(s_hot, 1)

            def combine(it, k):
                q, s = it * PAIRS + k, k % 2
                dve.wait_ge(s_dst, q + 1)
                dve.wait_ge(s_got[k], 32 * it + 32)
                ps = p_dst[s][:, 0:2 * Q].rearrange("p (j f) -> p j f", j=2)
                if messages:
                    v.tensor_tensor(got[:, k, :, :], ps, got[:, k, :, :], ALU.add).then_inc(s_sum, 1)
                else:
                    need(dve, s_score, q - 1)
                    v.tensor_tensor(prod[:, s, :, :], ps, got[:, k, :, 0:D], ALU.mult).then_inc(s_sum, 1)
                if k % 2 == 1:
                    indices(k // 2, it * UNROLL + UNROLL + k // 2 * 4)

            def score(it, k):
                q, s = it * PAIRS + k, k % 2
                to = c.score[:, bass.ds(q * 2 * heads, 2 * heads)]
                if messages:
                    dve.wait_ge(s_dot, q + 1)
                    v.tensor_scalar(to, p_gate[s][:, 0:2], c.gate_b[:], None, ALU.add).then_inc(s_score, 1)
                else:
                    dve.wait_ge(s_sum, q + 1)
                    v.tensor_reduce(to, prod[:, s, :, :].rearrange("p j (h f) -> p (j h) f", h=heads),
                                    AX.X, ALU.add).then_inc(s_score, 1)

            indices(0, 0)
            indices(1, 4)
            if messages:
                skewed(dve, [(0, one_hot), (1, combine), (4, score)], 4)
            else:
                skewed(dve, [(0, one_hot), (1, combine), (2, score)], 2)


def softmax_weights(nc, c, name, heads):
    H, L = heads, 4 * P
    with Stage(nc, name) as st:
        score = st.sb("score", [ROWS, H, L])
        run = st.sb("run", [ROWS, H, L])
        top = st.sb("top", [ROWS, H, L])
        edge = st.sb("edge", [ROWS, H])
        edge_t = st.sb("edge_t", [H, ROWS])
        carry = st.sb("carry", [H, ROWS + 1])
        carry_t = st.sb("carry_t", [ROWS, H])
        back = st.sb("back", [H, ROWS + 1])
        back_t = st.sb("back_t", [ROWS, H])
        p_in = [st.ps(f"in{i}", [P, L]) for i in range(2)]
        p_out = [st.ps(f"out{i}", [P, L]) for i in range(2)]
        p_e = st.ps("e", [P, 4 * P])
        s_in, s_row, s_dve, s_edge, s_edge_t = (st.sem(n) for n in ("in", "row", "dve_chain", "edge_s", "edge_ts"))
        s_carry, s_carry_t, s_shift, s_exp, s_turn, s_back = (
            st.sem(n) for n in ("carry_s", "carry_ts", "shift", "exp", "turn", "back_s"))
        block = st.block()
        by_row = c.score[:, 0:STEPS * H].rearrange("p (r a h) -> p a h r", a=4, h=H)

        @block.tensor
        def _(pe):
            for h in range(H):
                need(pe, s_row, h - 1)
                for a in range(4):
                    last = nc.tensor.transpose(p_in[h % 2][0:ROWS, a * P:(a + 1) * P], by_row[:, a, h, :], c.ident[:])
                last.then_inc(s_in, 1)
            for n in range(2):
                pe.wait_ge(s_edge, n + 1)
                nc.tensor.transpose(p_e[0:H, 0:ROWS], edge[:], c.ident[0:ROWS, 0:ROWS]).then_inc(s_edge_t, 1)
                pe.wait_ge(s_carry, n + 1)
                carried = carry[:, 0:ROWS] if n == 0 else back[:, 1:ROWS + 1]
                nc.tensor.transpose(p_e[0:ROWS, 0:H], carried, c.ident[0:H, 0:H]).then_inc(s_carry_t, 1)
            for h in range(H):
                pe.wait_ge(s_exp, h + 1)
                need(pe, s_back, h - 1)
                for a in range(4):
                    last = nc.tensor.transpose(p_out[h % 2][:, a * ROWS:(a + 1) * ROWS], score[:, h, a * P:(a + 1) * P],
                                               c.ident[0:ROWS, 0:ROWS])
                last.then_inc(s_turn, 1)

        @block.scalar
        def _(act):
            for h in range(H):
                act.wait_ge(s_in, h + 1)
                nc.scalar.copy(score[:, h, :], p_in[h % 2][0:ROWS, :]).then_inc(s_row, 1)
            for h in range(H):
                act.wait_ge(s_shift, h + 1)
                nc.scalar.activation(score[:, h, :], score[:, h, :], ACT.Exp).then_inc(s_exp, 1)

        @block.vector
        def _(dve):
            v = nc.vector
            link = linker(dve, s_dve)
            scan = v.tensor_tensor_scan
            rev = slice(None, None, -1)
            for n in range(2):
                for h in range(H):
                    if n == 0:
                        dve.wait_ge(s_row, h + 1)
                    ins = scan(run[:, h, :], c.start_big[:], score[:, h, :],
                               -BIG if n == 0 else carry_t[:, h:h + 1], ALU.add, ALU.max)
                link(ins)
                if n == 0:
                    v.memset(carry[:, 0:1], -BIG)
                    v.tensor_copy(edge[:], run[:, :, L - 1]).then_inc(s_edge, 1)
                    dve.wait_ge(s_edge_t, 1)
                    link(v.tensor_copy(edge_t[:], p_e[0:H, 0:ROWS]))
                    scan(carry[:, 1:ROWS + 1], c.row_start[0:H, :], edge_t[:], -BIG, ALU.add,
                         ALU.max).then_inc(s_carry, 1)
                    dve.wait_ge(s_carry_t, 1)
                    link(v.tensor_copy(carry_t[:], p_e[0:ROWS, 0:H]))
            link(v.tensor_tensor(run[:], run[:], c.last[:].unsqueeze(1).to_broadcast([ROWS, H, L]), ALU.mult))
            for n in range(2):
                for h in range(H):
                    ins = scan(top[:, h, rev], c.not_last[:, rev], run[:, h, rev],
                               0.0 if n == 0 else back_t[:, h:h + 1], ALU.mult, ALU.add)
                link(ins)
                if n == 0:
                    v.memset(back[:, ROWS:ROWS + 1], 0.0)
                    v.tensor_copy(edge[:], top[:, :, 0]).then_inc(s_edge, 1)
                    dve.wait_ge(s_edge_t, 2)
                    link(v.tensor_copy(edge_t[:], p_e[0:H, 0:ROWS]))
                    scan(back[:, slice(ROWS - 1, None, -1)], c.row_open[0:H, rev], edge_t[:, rev], 0.0, ALU.mult,
                         ALU.add).then_inc(s_carry, 1)
                    dve.wait_ge(s_carry_t, 2)
                    link(v.tensor_copy(back_t[:], p_e[0:ROWS, 0:H]))
            for h in range(H):
                v.tensor_tensor(score[:, h, :], score[:, h, :], top[:, h, :], ALU.subtract).then_inc(s_shift, 1)
            for h in range(H):
                dve.wait_ge(s_turn, h + 1)
                v.tensor_copy(by_row[:, :, h, :], p_out[h % 2][:, 0:4 * ROWS].rearrange("p (a r) -> p a r", a=4)
                              ).then_inc(s_back, 1)


def aggregate(nc, c, name, heads, messages):
    F = HM if messages else D
    H = heads
    with Stage(nc, name) as st:
        pay = st.sb("pay", [P, PAIRS, 2, F])
        hot = st.sb("hot", [P, 2, 2, P])
        p_sum = [st.ps(f"sum{i}", [P, 4 * P]) for i in range(UNROLL)]
        s_pay = [st.sem(f"pay{k}") for k in range(PAIRS)]
        s_hot, s_weighted, s_mm, s_sum, s_zero = (st.sem(n) for n in ("hot", "weighted", "mm", "sum", "zero"))
        block = st.block()
        payload = c.payload_dram[0:STEPS * P * F].rearrange("(q p f) -> q p f", p=P, f=2 * F)

        @block.sync
        def _(sp):
            def load(it, k):
                q = it * PAIRS + k
                need(sp, s_mm, q - PAIRS + 1)
                sp.dma_start(pay[:, k, :, :].rearrange("p j f -> p (j f)"),
                             payload[bass.ds(q, 1), :, :].rearrange("o p f -> (o p) f")).then_inc(s_pay[k], 16)
            skewed(sp, [(0, load)], 0)

        def weigh(eng, it, k):
            q = it * PAIRS + k
            eng.wait_ge(s_pay[k], 16 * it + 16)
            if messages:
                for j in range(2):
                    ins = nc.scalar.activation(pay[:, k, j, :], pay[:, k, j, :], ACT.Relu,
                                               scale=c.score[:, bass.ds(2 * q + j, 1)])
            else:
                of = pay[:, k, :, :].rearrange("p j (h f) -> p (j h) f", h=H)
                ins = nc.gpsimd.tensor_tensor(of, of, c.score[:, bass.ds(2 * q * H, 2 * H)].unsqueeze(2)
                                              .to_broadcast([P, 2 * H, D // H]), ALU.mult)
            ins.then_inc(s_weighted, 1)

        if messages:
            @block.scalar
            def _(act):
                skewed(act, [(0, lambda it, k: weigh(act, it, k))], 0)
        else:
            @block.gpsimd
            def _(pool):
                skewed(pool, [(0, lambda it, k: weigh(pool, it, k))], 0)

        @block.tensor
        def _(pe):
            def matmul(it, k):
                q, s = it * PAIRS + k, k % 2
                pe.wait_ge(s_hot, q + 1)
                pe.wait_ge(s_weighted, q + 1)
                need(pe, s_sum, 2 * q - UNROLL + 2)
                for j in range(2):
                    ps = p_sum[2 * k + j]
                    nc.tensor.matmul(ps[:, 0:F], hot[:, s, j, :], pay[:, k, j, :], start=True, stop=True)
                    last = nc.tensor.matmul(ps[:, F:F + H], hot[:, s, j, :], c.score[:, bass.ds((2 * q + j) * H, H)],
                                            start=True, stop=True)
                last.then_inc(s_mm, 1)
            skewed(pe, [(0, matmul)], 0)

        @block.vector
        def _(dve):
            nc.vector.memset(c.sum[:, :, 0:F + H], 0.0).then_inc(s_zero, 1)
            dve.wait_ge(s_zero, 1)

            def one_hot(it, k):
                q, s = it * PAIRS + k, k % 2
                need(dve, s_mm, q - 1)
                nc.vector.tensor_tensor(hot[:, s, :, :], c.node_row[:].unsqueeze(1).to_broadcast([P, 2, P]),
                                        c.local[:, bass.ds(2 * q, 2)].unsqueeze(2).to_broadcast([P, 2, P]),
                                        ALU.is_equal).then_inc(s_hot, 1)

            def accumulate(it, k):
                q = it * PAIRS + k
                dve.wait_ge(s_mm, q + 1)
                for j in range(2):
                    tile = dve.value_load(c.tile_at[0:1, bass.ds(2 * q + j, 1)], min_val=0, max_val=TILES - 1)
                    need(dve, s_sum, 2 * q + j)
                    to = c.sum[:, bass.ds(tile, 1), 0:F + H].rearrange("p o f -> p (o f)")
                    nc.vector.tensor_tensor(to, to, p_sum[2 * k + j][:, 0:F + H], ALU.add).then_inc(s_sum, 1)

            skewed(dve, [(0, one_hot), (1, accumulate)], 1)


def update_nodes(nc, c):
    with Stage(nc, "update") as st:
        inv = st.sb("inv", [P, TILES])
        mean = st.sb("mean", [P, GROUP, HM + 1])
        mean_t = st.sb("mean_t", [P, GROUP, 3 * P])
        agg_t = st.sb("agg_t", [P, GROUP, P])
        hid_t = st.sb("hid_t", [P, GROUP, 2 * P])
        bank = [st.ps(f"bank{j}", [P, 4 * P]) for j in range(GROUP)]
        s_inv, s_mean, s_turn, s_mean_t, s_agg = (st.sem(n) for n in ("inv_s", "mean_s", "turn", "mean_ts", "agg"))
        s_agg_t, s_hid, s_hid_t, s_out, s_done = (st.sem(n) for n in ("agg_ts", "hid", "hid_ts", "out", "done"))
        block = st.block()

        @block.tensor
        def _(pe):
            mm = nc.tensor.matmul

            def body(g):
                n = g * GROUP
                pe.wait_ge(s_mean, g + 1)
                for j in range(GROUP):
                    need(pe, s_done, n + j - GROUP + 1)
                    for f in range(2):
                        nc.tensor.transpose(bank[j][:, f * P:(f + 1) * P], mean[:, j, f * P:(f + 1) * P], c.ident[:])
                    nc.tensor.transpose(bank[j][0:1, 2 * P:3 * P], mean[:, j, HM:HM + 1], c.ident[:]).then_inc(s_turn, 1)
                for j in range(GROUP):
                    pe.wait_ge(s_mean_t, n + j + 1)
                    to = bank[j][:, 0:P]
                    for f in range(2):
                        mm(to, c.w23[:, f, :], mean_t[:, j, f * P:(f + 1) * P], start=(f == 0), stop=False)
                    mm(to, c.b23[:], mean_t[0:1, j, 2 * P:3 * P], start=False, stop=True).then_inc(s_agg, 1)
                for j in range(GROUP):
                    pe.wait_ge(s_agg_t, n + j + 1)
                    for f in range(2):
                        to = bank[j][:, f * P:(f + 1) * P]
                        mm(to, c.up1[:, 0, f * P:(f + 1) * P],
                           c.ht[:, bass.ds(n + j, 1), :].rearrange("p o n -> p (o n)"), start=True, stop=False)
                        last = mm(to, c.up1[:, 1, f * P:(f + 1) * P], agg_t[:, j, :], start=False, stop=True)
                    last.then_inc(s_hid, 1)
                for j in range(GROUP):
                    pe.wait_ge(s_hid_t, n + j + 1)
                    to = bank[j][:, 0:P]
                    for f in range(2):
                        mm(to, hid_t[:, j, f * P:(f + 1) * P], c.u23[:, f, :], start=(f == 0), stop=False)
                    mm(to, c.ones[0:1, :], c.ub23[:], start=False, stop=True).then_inc(s_out, 1)

            body(0)
            with pe.Fori(1, GROUPS) as g:
                body(g)

        @block.scalar
        def _(act):
            def body(g):
                n = g * GROUP
                for j in range(GROUP):
                    act.wait_ge(s_turn, n + j + 1)
                    need(act, s_agg, n + j - GROUP + 1)
                    nc.scalar.copy(mean_t[:, j, 0:2 * P], bank[j][:, 0:2 * P])
                    nc.scalar.copy(mean_t[0:1, j, 2 * P:3 * P], bank[j][0:1, 2 * P:3 * P]).then_inc(s_mean_t, 1)
                for j in range(GROUP):
                    act.wait_ge(s_hid, n + j + 1)
                    need(act, s_out, n + j - GROUP + 1)
                    for f in range(2):
                        ins = nc.scalar.activation(hid_t[:, j, f * P:(f + 1) * P], bank[j][:, f * P:(f + 1) * P],
                                                   ACT.Relu, bias=c.up_b1[:, f:f + 1])
                    ins.then_inc(s_hid_t, 1)

            body(0)
            with act.Fori(1, GROUPS) as g:
                body(g)

        @block.vector
        def _(dve):
            v = nc.vector
            v.tensor_scalar(inv[:], c.sum[:, :, HM], ATTN_EPS, None, ALU.add).then_inc(s_inv, 1)
            dve.wait_ge(s_inv, 1)
            v.reciprocal(inv[:], inv[:]).then_inc(s_inv, 1)
            dve.wait_ge(s_inv, 2)

            def body(g):
                n = g * GROUP
                need(dve, s_turn, n)
                v.tensor_tensor(mean[:], c.sum[:, bass.ds(n, GROUP), 0:HM + 1],
                                inv[:, bass.ds(n, GROUP)].unsqueeze(2).to_broadcast([P, GROUP, HM + 1]),
                                ALU.mult).then_inc(s_mean, 1)
                for j in range(GROUP):
                    dve.wait_ge(s_agg, n + j + 1)
                    need(dve, s_hid, n + j - GROUP + 1)
                    v.tensor_copy(agg_t[:, j, :], bank[j][:, 0:P]).then_inc(s_agg_t, 1)
                for j in range(GROUP):
                    dve.wait_ge(s_out, n + j + 1)
                    to = c.x[:, bass.ds(n + j, 1), :].rearrange("p o d -> p (o d)")
                    v.tensor_tensor(to, to, bank[j][:, 0:P], ALU.add).then_inc(s_done, 1)

            body(0)
            with dve.Fori(1, GROUPS) as g:
                body(g)


def combine_heads(nc, c, name, heads, out):
    H = heads
    with Stage(nc, name) as st:
        inv = st.sb("inv", [P, TILES, H])
        s_chain, s_done, s_out = st.sem("chain"), st.sem("done"), st.sem("out")
        block = st.block()

        @block.vector
        def _(dve):
            v = nc.vector
            link = linker(dve, s_chain)
            link(v.tensor_scalar(inv[:], c.sum[:, :, D:D + H], ATTN_EPS, None, ALU.add))
            link(v.reciprocal(inv[:], inv[:]))
            if H > 1:
                link(v.tensor_tensor(c.h[:].rearrange("p t (h f) -> p t h f", h=H),
                                     c.sum[:, :, 0:D].rearrange("p t (h f) -> p t h f", h=H),
                                     inv[:].unsqueeze(3).to_broadcast([P, TILES, H, D // H]), ALU.mult))
            else:
                link(v.tensor_tensor(c.h[:], c.sum[:, :, 0:D], inv[:].to_broadcast([P, TILES, D]), ALU.mult))
            link(v.tensor_tensor(c.h[:], c.h[:], c.skip[:], ALU.add))
            if out is not None:
                v.tensor_tensor(c.h[:], c.h[:], c.x[:], ALU.add).then_inc(s_done, 1)

        if out is not None:
            @block.sync
            def _(sp):
                sp.wait_ge(s_done, 1)
                sp.dma_start(out[0:(TILES - 1) * P, :].rearrange("(t p) d -> p t d", p=P),
                             c.h[:, 0:TILES - 1, :]).then_inc(s_out, 16)
                sp.dma_start(out[(TILES - 1) * P:N, :], c.h[0:LAST_ROWS, TILES - 1, :]).then_inc(s_out, 16)
                sp.wait_ge(s_out, 32)


def pad_attributes(nc, c, attr):
    with Stage(nc, "pad") as st:
        rows = (CHUNKS + 1) * P - E
        zeros = st.sb("zeros", [P, rows * DE // P])
        s_zero, s_in = st.sem("zero"), st.sem("in")
        block = st.block()

        @block.vector
        def _(dve):
            nc.vector.memset(zeros[:], 0.0).then_inc(s_zero, 1)

        @block.sync
        def _(sp):
            sp.dma_start(c.attr_dram[0:E, :].rearrange("(a b) d -> a (b d)", a=80),
                         attr.rearrange("(a b) d -> a (b d)", a=80)).then_inc(s_in, 16)
            sp.wait_ge(s_zero, 1)
            sp.dma_start(c.attr_dram[E:E + rows, :].rearrange("r d -> (r d)").rearrange("(p f) -> p f", p=P),
                         zeros[:]).then_inc(s_in, 16)
            sp.wait_ge(s_in, 32)


class Shared:
    pass


def build(nc, a, out):
    c = Shared()
    with Stage(nc, "keep") as st:
        c.ones = st.sb("ones", [P, P])
        c.ident = st.sb("ident", [P, P])
        c.node_row = st.sb("node_row", [P, P])
        c.step_row = st.sb("step_row", [P, STEPS])
        c.part_col = st.sb("part_col", [P, KB])
        c.src_slot = st.sb("src_slot", [P, STEPS + UNROLL], I32)
        c.local = st.sb("local", [P, STEPS])
        c.start_big = st.sb("start_big", [ROWS, 4 * P])
        c.last = st.sb("last", [ROWS, 4 * P])
        c.not_last = st.sb("not_last", [ROWS, 4 * P])
        c.row_start = st.sb("row_start", [8, ROWS])
        c.row_open = st.sb("row_open", [8, ROWS])
        c.tile_at = st.sb("tile_at", [1, STEPS], I32)
        c.chunk_at = st.sb("chunk_at", [1, STEPS], I32)
        c.x = st.sb("x", [P, TILES, D])
        c.h = st.sb("h", [P, TILES, D])
        c.ht = st.sb("ht", [P, TILES, P])
        c.skip = c.ht
        c.w_edge = st.sb("w_edge", [DE, HM])
        c.w_node = [st.sb(f"w_node{i}", [P, 4 * D]) for i in range(3)]
        c.b_node = [st.sb(f"b_node{i}", [1, 4 * D]) for i in range(3)]
        c.up1 = st.sb("up1", [P, 2, HM])
        c.up_b1 = st.sb("up_b1", [P, 2])
        c.w23 = st.sb("w23", [P, 2, D])
        c.u23 = st.sb("u23", [P, 2, D])
        c.wg = st.sb("wg", [P, 2, D])
        c.bg, c.gate_w, c.gate_b = (st.sb(n, [P, 1]) for n in ("bg", "gate_w", "gate_b"))
        c.b23, c.ub23 = (st.sb(n, [1, D]) for n in ("b23", "ub23"))
        c.score = st.sb("score", [P, (STEPS + UNROLL) * HEADS])
        c.payload_dram = nc.dram_tensor("payload_dram", [STEPS * P * HM], F32, kind="Internal").ap()
        c.attr_dram = nc.dram_tensor("attr_dram", [(CHUNKS + 1) * P, DE], F32, kind="Internal").ap()
        c.gather_dram = nc.dram_tensor("gather_dram", [NPAD, HM], F32, kind="Internal").ap()
        c.local_dram = nc.dram_tensor("local_dram", [STEPS * P], BF16, kind="Internal").ap()
        c.key_dram = nc.dram_tensor("key_dram", [STEPS * P + 2], F32, kind="Internal").ap()
        make_constants(nc, c)
        pad_attributes(nc, c, a["edge_attr_16"])
        plan_steps(nc, c, a["src"], a["dst"])
        fold_weights(nc, c, a)
        load_nodes(nc, c, a["x"])
        layer_norm(nc, c, "ln0")
        with Stage(nc, "layer0") as s0:
            table = s0.sb("table", [P, TILES, 3, HM], BF16)
            project(nc, c, "proj0", 0, HM, 1.0, table, True)
            edge_scores(nc, c, "score0", 1, True, table)
        softmax_weights(nc, c, "soft0", 1)
        with Stage(nc, "sums0") as s1:
            c.sum = s1.sb("sum", [P, TILES, HM + 1])
            aggregate(nc, c, "agg0", 1, True)
            update_nodes(nc, c)
        layer_norm(nc, c, "ln1")
        for layer, heads in ((1, HEADS), (2, 1)):
            with Stage(nc, f"layer{layer}") as s2:
                table = s2.sb("table", [P, TILES, 3, D], BF16)
                project(nc, c, f"proj{layer}", layer, D, float(heads / D) ** 0.5, table, False)
                edge_scores(nc, c, f"score{layer}", heads, False, table)
            softmax_weights(nc, c, f"soft{layer}", heads)
            with Stage(nc, f"sums{layer}") as s3:
                c.sum = s3.sb("sum", [P, TILES, D + heads])
                aggregate(nc, c, f"agg{layer}", heads, False)
                combine_heads(nc, c, f"heads{layer}", heads, out if layer == 2 else None)


_OUTS = [((N, D), "float32")]


def kernel(**inputs):
    import numpy as _np
    import concourse.bacc as _bacc
    from concourse import mybir as _mybir
    from concourse.bass_utils import run_bass_kernel_spmd as _run

    nc = _bacc.Bacc("TRN2", target_bir_lowering=False, num_devices=1)
    arrays, args = {}, {}
    for name, value in inputs.items():
        a = _np.ascontiguousarray(value)
        arrays[f"in_{name}_dram"] = a
        args[name] = nc.dram_tensor(f"in_{name}_dram", a.shape, _mybir.dt.from_np(a.dtype), kind="ExternalInput").ap()
    shape, dtype = _OUTS[0]
    out = nc.dram_tensor("out_0_dram", shape, _mybir.dt.from_np(_np.dtype(dtype)), kind="ExternalOutput").ap()
    build(nc, args, out)
    r = _run(nc, [arrays], core_ids=[0])
    return r.results[0]["out_0_dram"]
```

```python
import concourse.bass as bass
from concourse import mybir
from contextlib import ExitStack

F32 = mybir.dt.float32
BF16 = mybir.dt.bfloat16
I32 = mybir.dt.int32
ALU = mybir.AluOpType
ACT = mybir.ActivationFunctionType
AX = mybir.AxisListType
SP, PE, DVE = mybir.EngineType.SP, mybir.EngineType.PE, mybir.EngineType.DVE

P = 128
N, E, D, DE = 3125, 50000, 128, 16
TILES = -(-N // P)
CHUNKS = -(-E // P)
LAST_ROWS = N - (TILES - 1) * P
FULL_CHUNKS = E // P
TAIL = E - FULL_CHUNKS * P
UNROLL = 16
STEPS = -(-(CHUNKS + TILES - 1) // UNROLL) * UNROLL
ITERS = STEPS // UNROLL
PAIRS = UNROLL // 2
ROWS = STEPS // 4
KB = -(-CHUNKS // P)
NO_NODE = TILES * P + 800.0
NOT_HERE = 255.0
BIG = 1.0e30
NPAD = TILES * P
HEADS = 8
PARTS = 6
STACK = PARTS * DE
STACK_BLOCKS = 8


def value_width(heads, width):
    return width + heads
HM = 256
LN_EPS = 1e-5
ATTN_EPS = 1e-16


class Stage:

    def __init__(self, nc, name):
        self.nc, self.name, self.ctx, self.sems = nc, name, ExitStack(), []

    def __enter__(self):
        self.ctx.__enter__()
        return self

    def __exit__(self, *a):
        self.ctx.__exit__(*a)
        if self.sems:
            self.nc.clear_and_free_semaphores(self.sems)
            self.nc.all_engine_barrier()

    def sb(self, name, shape, dt=F32):
        return self.ctx.enter_context(self.nc.sbuf_tensor(f"{self.name}_{name}", shape, dt))

    def ps(self, name, shape, dt=F32):
        return self.ctx.enter_context(self.nc.psum_tensor(f"{self.name}_{name}", shape, dt))

    def sem(self, name):
        self.sems.append(self.nc.alloc_semaphore(f"{self.name}_{name}"))
        return self.sems[-1]

    def block(self):
        return self.ctx.enter_context(self.nc.Block())


def linker(eng, sem):
    done = [0]

    def link(ins):
        done[0] += 1
        ins.then_inc(sem, 1)
        eng.wait_ge(sem, done[0])
    return link


def make_constants(nc, c):
    with Stage(nc, "const") as st:
        s_pool, s_made, s_int = st.sem("pool_chain"), st.sem("made"), st.sem("ints")
        node_i = st.sb("node_i", [P, P], I32)
        step_i = st.sb("step_i", [P, STEPS], I32)
        part_i = st.sb("part_i", [P, KB], I32)
        block = st.block()

        @block.gpsimd
        def _(pool):
            link = linker(pool, s_pool)
            nc.gpsimd.memset(c.ones[:], 1.0)
            link(nc.gpsimd.memset(c.ident[:], 0.0))
            nc.gpsimd.affine_select(out=c.ident[:], in_=c.ident[:], compare_op=ALU.not_equal, fill=1.0,
                                    base=0, pattern=[[-1, P]], channel_multiplier=1).then_inc(s_made, 1)
            nc.gpsimd.iota(node_i[:], [[1, P]], base=0, channel_multiplier=0).then_inc(s_int, 1)
            nc.gpsimd.iota(step_i[:], [[1, STEPS]], base=0, channel_multiplier=0).then_inc(s_int, 1)
            nc.gpsimd.iota(part_i[:], [[P, KB]], base=0, channel_multiplier=1).then_inc(s_int, 1)

        @block.vector
        def _(dve):
            dve.wait_ge(s_int, 3)
            nc.vector.tensor_copy(c.node_row[:], node_i[:])
            nc.vector.tensor_copy(c.step_row[:], step_i[:])
            nc.vector.tensor_copy(c.part_col[:], part_i[:])
            dve.wait_ge(s_made, 1)
            nc.vector.tensor_copy(c.ident_bf[:], c.ident[:])


def check_order(nc, c, dst):
    rows = P - 3
    cols = E // rows
    with Stage(nc, "order") as st:
        this = st.sb("this", [rows, cols], I32)
        following = st.sb("following", [rows, cols], I32)
        descends = st.sb("descends", [rows, cols])
        found = st.sb("found", [rows, 1])
        p_found = st.ps("found_ps", [1, 4])
        s_last, s_in, s_chain, s_sum = (st.sem(n) for n in ("last", "in", "chain", "sum"))
        block = st.block()

        @block.sync
        def _(sp):
            sp.dma_start(this[:], dst.rearrange("(r s) -> r s", r=rows)).then_inc(s_in, 16)
            sp.wait_ge(s_last, 1)
            sp.dma_start(following[0:rows - 1, :], dst[1:1 + (rows - 1) * cols]
                         .rearrange("(r s) -> r s", s=cols)).then_inc(s_in, 16)
            sp.dma_start(following[rows - 1:rows, 0:cols - 1], dst[1 + (rows - 1) * cols:E]
                         .rearrange("(r s) -> r s", r=1)).then_inc(s_in, 16)

        @block.gpsimd
        def _(pool):
            nc.gpsimd.memset(following[:, cols - 1:cols], int(NO_NODE)).then_inc(s_last, 1)

        @block.vector
        def _(dve):
            v = nc.vector
            link = linker(dve, s_chain)
            dve.wait_ge(s_in, 48)
            link(v.tensor_tensor(descends[:], this[:], following[:], ALU.is_gt))
            link(v.reduce_max(found[:], descends[:], AX.X))
            dve.wait_ge(s_sum, 1)
            v.tensor_copy(c.unsorted[:], p_found[:])

        @block.tensor
        def _(pe):
            pe.wait_ge(s_chain, 2)
            for n in range(4):
                last = nc.tensor.matmul(p_found[:, n:n + 1], c.ones[0:rows, 0:1], found[:], start=True, stop=True)
            last.then_inc(s_sum, 1)


def load_unsorted(nc, c, engine):
    _, values = nc.values_load_multi_w_load_instructions(
        c.unsorted[0:1, 0:4], engines=[engine], min_val=0, max_val=P,
        skip_runtime_bounds_check_because="check_order counts at most 128 rows")
    return values[0]


PIECES = 8
PIECE_CHUNKS = -(-CHUNKS // PIECES)


def sort_edges(nc, c, src, dst, attr):
    COLS, L = PIECES * PIECE_CHUNKS, PIECE_CHUNKS * P
    with Stage(nc, "sort") as st:
        raw = st.sb("raw", [P, L], I32)
        others = st.sb("others", [P, L])
        less = st.sb("less", [P, L], BF16)
        same = st.sb("same", [P, P])
        earlier = st.sb("earlier", [P, P])
        dst_col = st.sb("dst_col", [P, COLS], I32)
        src_col = st.sb("src_col", [P, COLS], I32)
        own = st.sb("own", [P, COLS])
        below = st.sb("below", [P, PIECES + 1, COLS])
        rank = st.sb("rank", [P, COLS])
        place = st.sb("place", [P, COLS], I32)
        edge_attr = st.sb("edge_attr", [P, CHUNKS, DE])
        slot_place, slot_src, slot_dst = (st.sb(n, [P, 1], I32) for n in ("slot_place", "slot_src", "slot_dst"))
        slot_attr = st.sb("slot_attr", [P, DE])
        s_padded, s_cols, s_piece, s_used = (st.sem(n) for n in ("padded", "cols", "piece", "used"))
        s_chain, s_placed, s_slot, s_clear, s_moved = (
            st.sem(n) for n in ("chain", "placed", "slot", "clear", "moved"))
        block = st.block()

        @block.sync
        def _(sp):
            with sp.If(load_unsorted(nc, c, SP) > 0):
                sp.wait_ge(s_padded, 2)
                full = FULL_CHUNKS * P
                for to, of in ((dst_col, dst), (src_col, src)):
                    sp.dma_start(to[:, 0:FULL_CHUNKS], of[0:full].rearrange("(c p) -> p c", p=P),
                                 allow_slow_non_contiguous=True).then_inc(s_cols, 16)
                    sp.dma_start(to[0:TAIL, FULL_CHUNKS:CHUNKS],
                                 of[full:E].rearrange("(c p) -> p c", c=1)).then_inc(s_cols, 16)
                for n in range(PIECES):
                    lo, hi = n * PIECE_CHUNKS, min((n + 1) * PIECE_CHUNKS, FULL_CHUNKS)
                    sp.dma_start(edge_attr[:, lo:hi, :],
                                 attr[lo * P:hi * P, :].rearrange("(c p) d -> p c d", p=P)).then_inc(s_cols, 16)
                sp.dma_start(edge_attr[0:TAIL, FULL_CHUNKS, :], attr[full:E, :]).then_inc(s_cols, 16)
                for n in range(PIECES):
                    need(sp, s_used, n)
                    size = min(L, E - n * L)
                    sp.dma_start(raw[:, 0:size], dst[n * L:n * L + size].rearrange("(o s) -> o s", o=1)
                                 .to_broadcast([P, size])).then_inc(s_piece, 16)

        @block.vector
        def _(dve):
            v = nc.vector
            with dve.If(load_unsorted(nc, c, DVE) > 0):
                v.memset(dst_col[:, FULL_CHUNKS:COLS], int(NO_NODE)).then_inc(s_padded, 1)
                v.memset(src_col[:, FULL_CHUNKS:COLS], 0).then_inc(s_padded, 1)
                v.memset(below[:], 0.0)
                v.tensor_scalar(earlier[:], c.node_row[:], c.part_col[:, 0:1], None, ALU.is_lt)
                dve.wait_ge(s_cols, 16 * (5 + PIECES))
                v.tensor_scalar(own[:], dst_col[:], 2.0, None, ALU.mult).then_inc(s_chain, 1)
                done = 1
                for n in range(PIECES):
                    dve.wait_ge(s_piece, 16 * n + 16)
                    if n == PIECES - 1:
                        v.memset(raw[:, E - n * L:L], int(NO_NODE)).then_inc(s_chain, 1)
                        done += 1
                    dve.wait_ge(s_chain, done)
                    v.tensor_scalar(others[:], raw[:], 2.0, None, ALU.mult).then_inc(s_used, 1)
                    dve.wait_ge(s_used, n + 1)
                    first, end = n * PIECE_CHUNKS, (n + 1) * PIECE_CHUNKS
                    for lo, hi, each in ((0, first, 1), (first, end, 3), (end, COLS, 1)):
                        if lo == hi:
                            continue
                        with dve.Fori(lo, hi) as j:
                            chained = (j - lo) * each + done
                            mine = own[:, bass.ds(j, 1)]
                            v.tensor_scalar(less[:], others[:], mine, 0.0, ALU.is_lt, ALU.add,
                                            accum_out=below[:, n, bass.ds(j, 1)]).then_inc(s_chain, 1)
                            dve.wait_ge(s_chain, chained + 1)
                            if each == 3:
                                chunk = others[:, bass.ds((j - lo) * P, P)]
                                v.scalar_tensor_tensor(same[:], chunk, mine, earlier[:], ALU.is_equal, ALU.mult,
                                                       accum_out=below[:, PIECES, bass.ds(j, 1)]).then_inc(s_chain, 1)
                                dve.wait_ge(s_chain, chained + 2)
                                v.tensor_scalar(chunk, chunk, -1.0, None, ALU.add).then_inc(s_chain, 1)
                                dve.wait_ge(s_chain, chained + 3)
                        done += (hi - lo) * each
                v.tensor_reduce(rank[:], below[:].rearrange("p n c -> p c n"), AX.X, ALU.add).then_inc(s_chain, 1)
                dve.wait_ge(s_chain, done + 1)
                v.tensor_copy(place[:], rank[:]).then_inc(s_placed, 1)

        @block.gpsimd
        def _(pool):
            def move(j, rows):
                for to, of in ((slot_place[0:rows, :], place[0:rows, bass.ds(j, 1)]),
                               (slot_src[0:rows, :], src_col[0:rows, bass.ds(j, 1)]),
                               (slot_dst[0:rows, :], dst_col[0:rows, bass.ds(j, 1)]),
                               (slot_attr[0:rows, :],
                                edge_attr[0:rows, bass.ds(j, 1), :].rearrange("p o d -> p (o d)"))):
                    nc.gpsimd.tensor_copy(to, of).then_inc(s_slot, 1)
                pool.wait_ge(s_slot, j * 4 + 4)
                pool.sem_inc(s_clear, 1)
                for rows_in, to in zip((slot_src, slot_dst, slot_attr), c.edges):
                    nc.gpsimd.indirect_dma_start(to, bass.IndirectOffsetOnAxis(ap=slot_place[0:rows, 0:1], axis=0),
                                                 rows_in[0:rows, :], None).then_inc(s_moved, 16)
                pool.wait_ge(s_moved, j * 48 + 48)
                pool.sem_inc(s_clear, 1)

            with pool.If(load_unsorted(nc, c, mybir.EngineType.Pool) > 0):
                pool.wait_ge(s_placed, 1)
                pool.wait_ge(s_cols, 16 * (5 + PIECES))
                with pool.Fori(0, FULL_CHUNKS) as j:
                    move(j, P)
                move(FULL_CHUNKS, TAIL)


def edge_sources(nc, c, sp, load, given):
    unsorted = load_unsorted(nc, c, SP)
    with sp.If(unsorted < 1):
        load(*given)
    with sp.If(unsorted > 0):
        load(c.edges[0].rearrange("e o -> (e o)"), c.edges[1].rearrange("e o -> (e o)"), c.edges[2])


def plan_steps(nc, c, src, dst):
    with Stage(nc, "plan") as st:
        ends = st.sb("ends", [P, KB * P], I32)
        starts = st.sb("starts", [P, KB * P], I32)
        endf = st.sb("endf", [P, KB * P])
        startf = st.sb("startf", [P, KB * P])
        junk = st.sb("junk", [P, KB * P])
        count = st.sb("count", [P, TILES - 1])
        count_i = st.sb("count_i", [P, TILES - 1], I32)
        chunk_i = st.sb("chunk_i", [P, TILES - 1], I32)
        turn = st.sb("turn", [P, TILES - 1])
        tile = st.sb("tile", [P, STEPS])
        chunk = st.sb("chunk", [P, STEPS])
        pick = st.sb("pick", [P, KB, STEPS])
        dst_slot = st.sb("dst_slot", [P, STEPS])
        local = st.sb("local", [P, STEPS])
        valid = st.sb("valid", [P, STEPS])
        upper = st.sb("upper", [P, STEPS])
        key = st.sb("key", [P, STEPS])
        local_row = st.sb("local_row", [ROWS, 4 * P], BF16)
        key_row = st.sb("key_row", [ROWS, 4 * P])
        key_prev = st.sb("key_prev", [ROWS, 4 * P])
        key_next = st.sb("key_next", [ROWS, 4 * P])
        fence = st.sb("fence", [1, 2])
        flag = st.sb("flag", [ROWS, 4])
        flag8 = st.sb("flag8", [ROWS, 16])
        ps_count = st.ps("count_ps", [P, TILES - 1])
        ps_dst = st.ps("dst_ps", [P, STEPS])
        ps_src = st.ps("src_ps", [P, STEPS])
        ps_row = [st.ps(f"row_ps{i}", [ROWS, 4 * P]) for i in range(2)]
        ps_flag = st.ps("flag_ps", [8, 2 * P])
        s_padded, s_in, s_counted, s_total = (st.sem(n) for n in ("padded", "in", "counted", "total"))
        s_picked, s_slots, s_local, s_turned = (st.sem(n) for n in ("picked", "slots", "local", "turned"))
        s_rows, s_out, s_shift, s_dve = (st.sem(n) for n in ("rows", "out", "shift", "dve_chain"))
        s_flag, s_flagt = st.sem("flag"), st.sem("flagt")
        block = st.block()

        @block.sync
        def _(sp):
            sp.wait_ge(s_padded, 2)

            def load(src, dst, _):
                for to, of in ((ends, dst), (starts, src)):
                    whole = (KB - 1) * P * P
                    sp.dma_start(to[:, 0:(KB - 1) * P].rearrange("q (k p) -> q k p", p=P),
                                 of[0:whole].rearrange("(k q p) -> q k p", q=P, p=P)).then_inc(s_in, 16)
                    rows = FULL_CHUNKS - (KB - 1) * P
                    sp.dma_start(to[0:rows, (KB - 1) * P:KB * P],
                                 of[whole:FULL_CHUNKS * P].rearrange("(q p) -> q p", p=P)).then_inc(s_in, 16)
                    sp.dma_start(to[rows:rows + 1, (KB - 1) * P:(KB - 1) * P + TAIL],
                                 of[FULL_CHUNKS * P:E].rearrange("(q p) -> q p", q=1)).then_inc(s_in, 16)

            edge_sources(nc, c, sp, load, (src, dst, None))
            sp.wait_ge(s_rows, 2)
            sp.dma_start(c.local_dram.rearrange("(r s) -> r s", r=ROWS), local_row[:]).then_inc(s_out, 16)
            sp.dma_start(c.key_dram[1:1 + STEPS * P].rearrange("(r s) -> r s", r=ROWS), key_row[:]).then_inc(s_out, 16)
            sp.dma_start(c.key_dram[0:1].rearrange("(a b) -> a b", a=1), fence[0:1, 0:1]).then_inc(s_out, 16)
            sp.dma_start(c.key_dram[1 + STEPS * P:2 + STEPS * P].rearrange("(a b) -> a b", a=1),
                         fence[0:1, 1:2]).then_inc(s_out, 16)
            sp.wait_ge(s_out, 64)
            sp.dma_start(key_prev[:], c.key_dram[0:STEPS * P].rearrange("(r s) -> r s", r=ROWS)).then_inc(s_shift, 16)
            sp.dma_start(key_next[:], c.key_dram[2:2 + STEPS * P].rearrange("(r s) -> r s", r=ROWS)).then_inc(s_shift, 16)

        @block.vector
        def _(dve):
            link = linker(dve, s_dve)
            v = nc.vector
            v.memset(ends[:, (KB - 1) * P:KB * P], int(NO_NODE)).then_inc(s_padded, 1)
            v.memset(starts[:, (KB - 1) * P:KB * P], 0).then_inc(s_padded, 1)
            v.memset(fence[:], -5.0)
            dve.wait_ge(s_in, 96)
            v.tensor_copy(startf[:], starts[:])
            link(v.tensor_copy(endf[:], ends[:]))
            for t in range(TILES - 1):
                v.tensor_scalar(junk[:], endf[:], float(P * (t + 1)), 0.0, ALU.is_lt, ALU.add,
                                accum_out=count[:, t:t + 1]).then_inc(s_counted, 1)
                dve.wait_ge(s_counted, t + 1)
            dve.wait_ge(s_total, 1)
            link(v.tensor_copy(count_i[:], ps_count[:]))
            link(v.tensor_single_scalar(chunk_i[:], count_i[:], 7, ALU.arith_shift_right))
            link(v.tensor_copy(turn[:], chunk_i[:]))
            link(v.tensor_tensor(turn[:], turn[:], c.step_row[:, 0:TILES - 1], ALU.add))
            link(v.memset(tile[:], 0.0))
            for t in range(TILES - 1):
                link(v.scalar_tensor_tensor(tile[:], c.step_row[:], turn[:, t:t + 1], tile[:], ALU.is_gt, ALU.add))
            link(v.tensor_tensor(chunk[:], c.step_row[:], tile[:], ALU.subtract))
            for k in range(KB):
                ins = v.tensor_scalar(pick[:, k, :], chunk[:], c.part_col[:, k:k + 1], None, ALU.is_equal)
                ins.then_inc(s_picked, 1)
            for width, at in c.tile_at.items():
                v.tensor_scalar(at[:], tile[0:1, :], float(width), None, ALU.mult)
            v.tensor_scalar(c.chunk_at[:], chunk[0:1, :], float(P * STACK), None, ALU.mult)
            dve.wait_ge(s_slots, 1)
            link(v.tensor_copy(dst_slot[:], ps_dst[:]))
            v.tensor_copy(c.src_slot[:, 0:STEPS], ps_src[:])
            v.memset(c.src_slot[:, STEPS:], 0)
            link(v.scalar_tensor_tensor(local[:], tile[:], -float(P), dst_slot[:], ALU.mult, ALU.add))
            v.tensor_scalar(upper[:], local[:], float(P), None, ALU.is_lt)
            link(v.tensor_scalar(valid[:], local[:], 0.0, None, ALU.is_ge))
            link(v.tensor_tensor(valid[:], valid[:], upper[:], ALU.mult))
            link(v.scalar_tensor_tensor(c.local[:], local[:], -NOT_HERE, valid[:], ALU.add, ALU.mult))
            link(v.tensor_scalar(c.local[:], c.local[:], NOT_HERE, None, ALU.add))
            link(v.scalar_tensor_tensor(key[:], dst_slot[:], 1.0, valid[:], ALU.add, ALU.mult))
            v.tensor_copy(fence[:], fence[:]).then_inc(s_local, 1)
            dve.wait_ge(s_turned, 2)
            v.tensor_copy(local_row[:], ps_row[0][:]).then_inc(s_rows, 1)
            v.tensor_copy(key_row[:], ps_row[1][:]).then_inc(s_rows, 1)
            dve.wait_ge(s_rows, 2)
            dve.wait_ge(s_shift, 32)
            link(v.tensor_tensor(c.start_big[:], key_row[:], key_prev[:], ALU.not_equal))
            link(v.tensor_tensor(c.last[:], key_row[:], key_next[:], ALU.not_equal))
            link(v.reduce_max(flag[:, 0:1], c.start_big[:], AX.X))
            link(v.tensor_scalar(c.start_big[:], c.start_big[:], -BIG, None, ALU.mult))
            link(v.tensor_scalar(c.not_last[:], c.last[:], -1.0, 1.0, ALU.mult, ALU.add))
            link(v.tensor_reduce(flag[:, 1:2], c.not_last[:], AX.X, ALU.min))
            link(v.tensor_scalar(flag[:, 0:1], flag[:, 0:1], -BIG, None, ALU.mult))
            link(v.tensor_copy(flag8[:, 0:8], flag[:, 0:1].to_broadcast([ROWS, 8])))
            v.tensor_copy(flag8[:, 8:16], flag[:, 1:2].to_broadcast([ROWS, 8])).then_inc(s_flag, 1)
            dve.wait_ge(s_flagt, 1)
            v.tensor_copy(c.row_start[:], ps_flag[:, 0:ROWS])
            v.tensor_copy(c.row_open[:], ps_flag[:, P:P + ROWS])

        @block.tensor
        def _(pe):
            pe.wait_ge(s_counted, TILES - 1)
            nc.tensor.matmul(ps_count[:], c.ones[:], count[:], start=True, stop=True).then_inc(s_total, 1)
            pe.wait_ge(s_picked, KB)
            for ps, rows in ((ps_dst, endf), (ps_src, startf)):
                for k in range(KB):
                    last = nc.tensor.matmul(ps[:], rows[:, k * P:(k + 1) * P], pick[:, k, :],
                                            start=(k == 0), stop=(k == KB - 1))
            last.then_inc(s_slots, 1)
            pe.wait_ge(s_local, 1)
            for ps, x in zip(ps_row, (c.local, key)):
                for a in range(4):
                    last = nc.tensor.transpose(ps[:, a * P:(a + 1) * P],
                                               x[:].rearrange("p (r a) -> p a r", a=4)[:, a, :], c.ident[:])
                last.then_inc(s_turned, 1)
            pe.wait_ge(s_flag, 1)
            nc.tensor.transpose(ps_flag[:, 0:ROWS], flag8[:, 0:8], c.ident[0:ROWS, 0:ROWS])
            nc.tensor.transpose(ps_flag[:, P:P + ROWS], flag8[:, 8:16],
                                c.ident[0:ROWS, 0:ROWS]).then_inc(s_flagt, 1)



def fold_weights(nc, c, a):
    with Stage(nc, "fold") as st:
        w2 = st.sb("w2", [P, 2, HM])
        w3 = st.sb("w3", [P, 2, D])
        u2 = st.sb("u2", [P, 2, HM])
        u3 = st.sb("u3", [P, 2, D])
        w2t = st.sb("w2t", [P, 2, HM])
        u2t = st.sb("u2t", [P, 2, HM])
        w23t = st.sb("w23t", [P, HM])
        ag1, ag2, ag2t = (st.sb(n, [P, D]) for n in ("ag1", "ag2", "ag2t"))
        ag3 = st.sb("ag3", [P, 1])
        cols = st.sb("cols", [P, 8])
        rows = st.sb("rows", [1, 2 * D + 2])
        agb2 = st.sb("agb2", [P, P])
        pt = [st.ps(f"turn{i}", [P, 4 * P]) for i in range(2)]
        pa = st.ps("pa", [P, 4 * P])
        pw, pg, pu, px = (st.ps(n, [P, 4 * P]) for n in ("pw", "pg", "pu", "px"))
        s_in, s_turn, s_flat, s_mm = (st.sem(n) for n in ("in", "turn", "flat", "mm"))
        s_mid, s_g, s_b23, s_bcol = (st.sem(n) for n in ("mid", "g", "b23", "bcol"))
        s_x, s_bg = st.sem("x"), st.sem("bg")
        LOADS = []

        def col(name, k):
            return a[name][k * P:(k + 1) * P].rearrange("(p o) -> p o", o=1)

        def row(name):
            return a[name].rearrange("(o n) -> o n", o=1)

        pre = "L0_gnn_"
        LOADS += [(w2[:], a[pre + "msg_w2"].rearrange("(k p) n -> p k n", p=P)),
                  (w3[:], a[pre + "msg_w3"].rearrange("(k p) n -> p k n", p=P)),
                  (u2[:], a[pre + "up_w2"].rearrange("(k p) n -> p k n", p=P)),
                  (u3[:], a[pre + "up_w3"].rearrange("(k p) n -> p k n", p=P)),
                  (c.up1[:], a[pre + "up_w1"].rearrange("(k p) n -> p k n", p=P)),
                  (c.w_edge[:], a[pre + "msg_w1"][0:DE, :]),
                  (c.w_node[0][:, HM:2 * HM], a[pre + "msg_w1"][DE:DE + D, :]),
                  (c.w_node[0][:, 0:HM], a[pre + "msg_w1"][DE + D:DE + 2 * D, :]),
                  (c.b_node[0][:, 0:HM], row(pre + "msg_b1")),
                  (ag1[:], a[pre + "ag_w1"]), (ag2[:], a[pre + "ag_w2"]), (ag3[:], a[pre + "ag_w3"]),
                  (cols[:, 0:1], col(pre + "msg_b2", 0)), (cols[:, 1:2], col(pre + "msg_b2", 1)),
                  (cols[:, 2:3], col(pre + "msg_b3", 0)), (cols[:, 3:4], col(pre + "ag_b1", 0)),
                  (cols[:, 4:5], col(pre + "ag_b2", 0)),
                  (cols[:, 5:6], col(pre + "up_b2", 0)), (cols[:, 6:7], col(pre + "up_b2", 1)),
                  (c.up_b1[:, 0:1], col(pre + "up_b1", 0)), (c.up_b1[:, 1:2], col(pre + "up_b1", 1)),
                  (rows[:, 0:D], row(pre + "msg_b3")), (rows[:, D:2 * D], row(pre + "up_b3")),
                  (rows[:, 2 * D:2 * D + 1], row(pre + "ag_b3"))]
        for layer in (1, 2):
            for n, x in enumerate("qkvs"):
                LOADS.append((c.w_node[layer][:, n * D:(n + 1) * D], a[f"L1_gnn_W{x}{layer}"]))
                LOADS.append((c.b_node[layer][:, n * D:(n + 1) * D], row(f"L1_gnn_b{x}{layer}")))
        block = st.block()

        @block.sync
        def _(sp):
            for to, of in LOADS:
                sp.dma_start(to, of).then_inc(s_in, 16)

        @block.tensor
        def _(pe):
            mm = nc.tensor.matmul
            pe.wait_ge(s_in, 16 * len(LOADS))
            for x, ps in ((w2, pt[0]), (u2, pt[1])):
                for k in range(2):
                    for i in range(2):
                        last = nc.tensor.transpose(ps[:, (k * 2 + i) * P:(k * 2 + i + 1) * P],
                                                   x[:, i, k * P:(k + 1) * P], c.ident[:])
            last = nc.tensor.transpose(pa[:, 0:P], ag2[:], c.ident[:])
            last.then_inc(s_turn, 1)
            pe.wait_ge(s_flat, 3)
            for k in range(2):
                mm(pw[:, 0:HM], w3[:, k, :], w2t[:, k, :], start=(k == 0), stop=(k == 1))
            for i in range(2):
                for k in range(2):
                    mm(pg[:, i * P:(i + 1) * P], w2t[:, k, i * P:(i + 1) * P], w3[:, k, :],
                       start=(k == 0), stop=(k == 1))
            for i in range(2):
                for k in range(2):
                    last = mm(pu[:, i * P:(i + 1) * P], u2t[:, k, i * P:(i + 1) * P], u3[:, k, :],
                              start=(k == 0), stop=(k == 1))
            for k in range(2):
                mm(px[:, 0:1], w3[:, k, :], cols[:, k:k + 1], start=(k == 0), stop=(k == 1))
            mm(px[:, 1:2], ag2t[:], ag3[:], start=True, stop=True)
            mm(px[:, 2:3], agb2[:], ag3[:], start=True, stop=False)
            mm(px[:, 2:3], c.ones[0:1, :], rows[0:1, 2 * D:2 * D + 1], start=False, stop=True)
            for to, b, w, r in ((px[0:1, P:2 * P], 0, w3, 0), (px[0:1, 2 * P:3 * P], 5, u3, D)):
                for k in range(2):
                    mm(to, cols[:, b + k:b + k + 1], w[:, k, :], start=(k == 0), stop=False)
                last = mm(to, c.ones[0:1, 0:1], rows[0:1, r:r + D], start=False, stop=True)
            last.then_inc(s_mm, 1)
            pe.wait_ge(s_mid, 2)
            for i in range(2):
                mm(pa[:, P + i * P:P + (i + 1) * P], w23t[:, i * P:(i + 1) * P], ag1[:], start=True, stop=True)
            mm(pa[:, 3 * P:3 * P + 1], ag1[:], cols[:, 7:8], start=True, stop=True).then_inc(s_g, 1)

        @block.vector
        def _(dve):
            v = nc.vector
            dve.wait_ge(s_in, 16 * len(LOADS))
            v.memset(c.b_node[0][:, HM:2 * HM], 0.0)
            v.tensor_copy(agb2[:], cols[:, 4:5].to_broadcast([P, P])).then_inc(s_flat, 1)
            dve.wait_ge(s_turn, 1)
            v.tensor_copy(w2t[:].rearrange("p k n -> p (k n)"), pt[0][:])
            v.tensor_copy(ag2t[:], pa[:, 0:P]).then_inc(s_flat, 1)
            v.tensor_copy(u2t[:].rearrange("p k n -> p (k n)"), pt[1][:]).then_inc(s_flat, 1)
            dve.wait_ge(s_mm, 1)
            v.tensor_copy(w23t[:], pw[:, 0:HM]).then_inc(s_mid, 1)
            v.tensor_tensor(cols[:, 7:8], px[:, 0:1], cols[:, 2:3], ALU.add).then_inc(s_mid, 1)
            v.tensor_copy(c.w23[:].rearrange("p k n -> p (k n)"), pg[:, 0:HM])
            v.tensor_copy(c.u23[:].rearrange("p k n -> p (k n)"), pu[:, 0:HM])
            v.tensor_copy(c.gate_w[:], px[:, 1:2])
            v.tensor_copy(c.gate_b[:], px[:, 2:3])
            v.tensor_copy(c.b23[:], px[0:1, P:2 * P])
            v.tensor_copy(c.ub23[:], px[0:1, 2 * P:3 * P])
            dve.wait_ge(s_g, 1)
            v.tensor_copy(c.wg[:].rearrange("p k n -> p (k n)"), pa[:, P:3 * P])
            v.tensor_tensor(c.bg[:], pa[:, 3 * P:3 * P + 1], cols[:, 3:4], ALU.add)


def load_nodes(nc, c, x):
    with Stage(nc, "load") as st:
        s_zero, s_in = st.sem("zero"), st.sem("in")
        block = st.block()

        @block.vector
        def _(dve):
            nc.vector.memset(c.x[:, TILES - 1, :], 0.0).then_inc(s_zero, 1)

        @block.sync
        def _(sp):
            sp.wait_ge(s_zero, 1)
            for t in range(TILES - 1):
                sp.dma_start(c.x[:, t, :], x[t * P:(t + 1) * P, :]).then_inc(s_in, 16)
            sp.dma_start(c.x[0:LAST_ROWS, TILES - 1, :], x[(TILES - 1) * P:N, :]).then_inc(s_in, 16)
            sp.wait_ge(s_in, 16 * TILES)


def layer_norm(nc, c, name):
    with Stage(nc, name) as st:
        sq = st.sb("sq", [P, TILES, D])
        mean, var, std, rstd = (st.sb(n, [P, TILES]) for n in ("mean", "var", "std", "rstd"))
        s_chain, s_cent, s_sq, s_var, s_std = (st.sem(n) for n in ("chain", "cent", "sq", "var", "std"))
        block = st.block()

        @block.vector
        def _(dve):
            v = nc.vector
            link = linker(dve, s_chain)
            link(v.tensor_reduce(mean[:], c.x[:], AX.X, ALU.add))
            link(v.tensor_scalar(mean[:], mean[:], 1.0 / D, None, ALU.mult))
            v.tensor_tensor(c.h[:], c.x[:], mean[:].unsqueeze(2).to_broadcast([P, TILES, D]),
                            ALU.subtract).then_inc(s_cent, 1)
            dve.wait_ge(s_sq, 1)
            link(v.tensor_reduce(var[:], sq[:], AX.X, ALU.add))
            v.tensor_scalar(var[:], var[:], 1.0 / D, LN_EPS, ALU.mult, ALU.add).then_inc(s_var, 1)
            dve.wait_ge(s_std, 1)
            link(v.reciprocal(rstd[:], std[:]))
            link(v.tensor_tensor(std[:], rstd[:], rstd[:], ALU.mult))
            link(v.tensor_tensor(std[:], std[:], var[:], ALU.mult))
            link(v.tensor_scalar(std[:], std[:], -0.5, 1.5, ALU.mult, ALU.add))
            link(v.tensor_tensor(rstd[:], rstd[:], std[:], ALU.mult))
            v.scalar_tensor_tensor(c.h[:], c.h[:], 0.0, rstd[:].unsqueeze(2).to_broadcast([P, TILES, D]),
                                   ALU.max, ALU.mult)

        @block.scalar
        def _(act):
            act.wait_ge(s_cent, 1)
            nc.scalar.activation(sq[:], c.h[:], ACT.Square).then_inc(s_sq, 1)
            act.wait_ge(s_var, 1)
            nc.scalar.activation(std[:], var[:], ACT.Sqrt).then_inc(s_std, 1)


GROUP = 5
GROUPS = TILES // GROUP


def project(nc, c, name, layer, heads, table_width, scale, table, keep_ht):
    W = c.gather_dram[layer].shape[1]
    keys = 0 if keep_ht else D
    per_head = (HM - keys) // heads
    Q = table_width
    w, b = c.w_node[layer], c.b_node[layer]
    with Stage(nc, name) as st:
        hs = st.sb("hs", [P, GROUP, D])
        ht = st.sb("ht", [P, GROUP, P])
        kv = st.sb("kv", [P, GROUP, W])
        rest = st.sb("rest", [P, GROUP, Q])
        rest2 = st.sb("rest2", [P, GROUP, Q])
        p_t = [st.ps(f"t{i}", [P, 4 * P]) for i in range(2)]
        p_o = [st.ps(f"o{i}", [P, 4 * P]) for i in range(GROUP)]
        s_t, s_ht, s_o = (st.sem(n) for n in ("t", "ht", "o"))
        s_kv, s_rest, s_mid = (st.sem(n) for n in ("kv", "rest", "mid"))
        s_out, s_hs, s_kept, s_ones = st.sem("out"), st.sem("hs"), st.sem("kept"), st.sem("ones")
        block = st.block()

        banks = ((0, 4), (4, GROUP))

        @block.gpsimd
        def _(pool):
            def body(g):
                if not isinstance(g, int):
                    pool.wait_ge(s_t, 2 * g)
                nc.gpsimd.tensor_copy(hs[:], c.h[:, bass.ds(g * GROUP, GROUP), :]).then_inc(s_hs, 1)

            body(0)
            with pool.Fori(1, GROUPS) as g:
                body(g)

        @block.tensor
        def _(pe):
            def body(g):
                pe.wait_ge(s_hs, g + 1)
                for n, (first, end) in enumerate(banks):
                    if not isinstance(g, int):
                        pe.wait_ge(s_ht, 2 * g + n - 1)
                    for j in range(first, end):
                        last = nc.tensor.transpose(p_t[n][:, (j - first) * P:(j - first + 1) * P], hs[:, j, :],
                                                   c.ident[:])
                    last.then_inc(s_t, 1)
                for j in range(GROUP):
                    pe.wait_ge(s_ht, 2 * g + 1 + j // 4)
                    if not isinstance(g, int):
                        pe.wait_ge(s_rest, g * GROUP + j - GROUP + 1)
                    nc.tensor.matmul(p_o[j][:], ht[:, j, :], w[:], start=True, stop=False)
                    nc.tensor.matmul(p_o[j][:], c.ones[0:1, :], b[:], start=False, stop=True).then_inc(s_o, 1)

            body(0)
            with pe.Fori(1, GROUPS) as g:
                body(g)

        @block.scalar
        def _(act):
            def body(g):
                for n, (first, end) in enumerate(banks):
                    act.wait_ge(s_t, 2 * g + n + 1)
                    if not isinstance(g, int):
                        act.wait_ge(s_o, g * GROUP + end - GROUP)
                        if keep_ht:
                            act.wait_ge(s_kept, 1 + 2 * g + n - 2)
                    nc.scalar.copy(ht[:, first:end, :].rearrange("p j n -> p (j n)"),
                                   p_t[n][:, 0:(end - first) * P]).then_inc(s_ht, 1)
                for j in range(GROUP):
                    act.wait_ge(s_o, g * GROUP + j + 1)
                    nc.scalar.activation(table[:, bass.ds(g * GROUP + j, 1), 0, :].rearrange("p o d -> p (o d)"),
                                         p_o[j][:, 0:Q], ACT.Copy, scale=scale)
                    if not isinstance(g, int):
                        act.wait_ge(s_out, 16 * g)
                    if keys:
                        nc.scalar.copy(kv[:, j, 0:keys], p_o[j][:, Q:Q + keys])
                    ins = nc.scalar.copy(kv[:, j, keys:W].rearrange("p (h f) -> p h f", h=heads)[:, :, 0:per_head],
                                         p_o[j][:, Q + keys:Q + HM].rearrange("p (h f) -> p h f", h=heads))
                    if 4 * P > Q + HM:
                        nc.scalar.copy(c.skip[:, bass.ds(g * GROUP + j, 1), :].rearrange("p o d -> p (o d)"),
                                       p_o[j][:, Q + HM:4 * P]).then_inc(s_kv, 1)
                    else:
                        ins.then_inc(s_kv, 1)

            act.wait_ge(s_ones, 1)
            body(0)
            with act.Fori(1, GROUPS) as g:
                body(g)

        @block.vector
        def _(dve):
            v = nc.vector
            v.memset(kv[:], 1.0).then_inc(s_ones, 1)

            def body(g):
                def part(j, s):
                    return table[:, bass.ds(g * GROUP + j, 1), s, :].rearrange("p o d -> p (o d)")
                for n, (first, end) in enumerate(banks):
                    if keep_ht:
                        dve.wait_ge(s_ht, 2 * g + n + 1)
                        v.tensor_copy(c.ht[:, bass.ds(g * GROUP + first, end - first), :],
                                      ht[:, first:end, :]).then_inc(s_kept, 1)
                for j in range(GROUP):
                    dve.wait_ge(s_kv, g * GROUP + j + 1)
                    v.scalar_tensor_tensor(rest[:, j, :], p_o[j][:, 0:Q], scale, part(j, 0),
                                           ALU.mult, ALU.subtract).then_inc(s_rest, 1)
                    dve.wait_ge(s_rest, g * GROUP + j + 1)
                    v.tensor_copy(part(j, 1), rest[:, j, :]).then_inc(s_mid, 1)
                    dve.wait_ge(s_mid, g * GROUP + j + 1)
                    v.tensor_tensor(part(j, 2), rest[:, j, :], part(j, 1), ALU.subtract)

            body(0)
            with dve.Fori(1, GROUPS) as g:
                body(g)

        @block.sync
        def _(sp):
            rows = c.gather_dram[layer].rearrange("(g j p) d -> g p j d", p=P, j=GROUP)

            def body(g):
                sp.wait_ge(s_kv, GROUP * g + GROUP)
                sp.dma_start(rows[bass.ds(g, 1)].rearrange("o p j d -> (o p) j d"), kv[:]).then_inc(s_out, 16)

            body(0)
            with sp.Fori(1, GROUPS) as g:
                body(g)
            sp.wait_ge(s_out, 16 * GROUPS)


def need(eng, sem, value):
    if not isinstance(value, int) or value > 0:
        eng.wait_ge(sem, value)


def skewed(eng, stages, depth):
    peeled = 1 + -(-depth // PAIRS)
    def run(it, k):
        for lag, stage in stages:
            if isinstance(it, int) and not 0 <= it * PAIRS + k - lag < ITERS * PAIRS:
                continue
            back, pair = divmod(k - lag, PAIRS)
            stage(it + back, pair)

    for it in range(peeled):
        for k in range(PAIRS):
            run(it, k)
    with eng.Fori(peeled, ITERS) as it:
        for k in range(PAIRS):
            run(it, k)
    for n in range(depth):
        run(ITERS + n // PAIRS, n % PAIRS)


def load_four(nc, engine, table, step, top):
    _, values = nc.values_load_multi_w_load_instructions(
        table[0:1, bass.ds(step, 4)], engines=[engine], min_val=0, max_val=top,
        skip_runtime_bounds_check_because="plan_steps computes tiles and chunks inside their ranges for any edges")
    return values


def edge_scores(nc, c, name, layer, heads, messages, table):
    Q = HM if messages else D
    W = c.gather_dram[layer].shape[1]
    keys = 0 if messages else D
    F = W - keys
    with Stage(nc, name) as st:
        got = st.sb("got", [P, PAIRS, 2, W])
        local = st.sb("local", [P, PAIRS // 2, 4 * P], BF16)
        hot = st.sb("hot", [P, PAIRS, 2 * P], BF16)
        index = st.sb("index", [P, PAIRS // 2, 4], I32)
        prod = st.sb("prod", [P, 2, 2, D])
        attr = st.sb("attr", [P, PAIRS, 2, STACK], BF16)
        attr_t = st.sb("attr_t", [STACK, PAIRS, 2 * P], BF16)
        hid_t = st.sb("hid_t", [P, 2, 2, 2 * P])
        gate = st.sb("gate", [P, 2, 2 * P])
        p_dst = [st.ps(f"dst{i}", [P, 2 * HM]) for i in range(2)]
        p_hid = [st.ps(f"hid{i}", [P, 4 * P]) for i in range(2)]
        p_gate = [st.ps(f"gate{i}", [P, 4 * P]) for i in range(2)]
        p_attr = st.ps("attr_ps", [STACK, 4 * P], BF16)
        s_got = [st.sem(f"got{k}") for k in range(PAIRS)]
        s_local = [st.sem(f"local{k}") for k in range(PAIRS // 2)]
        s_attr = [st.sem(f"attr{k}") for k in range(PAIRS)]
        s_stored = [st.sem(f"stored{k}") for k in range(PAIRS)]
        s_index, s_hot, s_dst, s_sum, s_clear = (st.sem(n) for n in ("index", "hot", "dst", "sum", "clear"))
        s_aturn, s_attr_t, s_hturn, s_hid_t = (st.sem(n) for n in ("aturn", "attr_t", "hturn", "hid_t"))
        s_gmm, s_gate, s_dot, s_score = (st.sem(n) for n in ("gmm", "gate_s", "dot", "score"))
        block = st.block()
        payload = c.payload_dram[0:STEPS * P * F].rearrange("(q p f) -> q p f", p=P, f=2 * F)
        table_flat = table[:].rearrange("p t s q -> p (t s q)")
        local_rows = c.local_dram.rearrange("(q s) -> q s", s=4 * P)

        def store(eng, it, k):
            q = it * PAIRS + k
            if messages:
                eng.wait_ge(s_sum, q + 1)
                of = got[:, k, :, :].rearrange("p j f -> p (j f)")
                eng.dma_start(payload[bass.ds(q, 1), :, :].rearrange("o p f -> (o p) f"), of).then_inc(s_stored[k], 16)
            else:
                eng.wait_ge(s_got[k], 32 * it + 32)
                eng.dma_start(payload[bass.ds(q, 1), :, :].rearrange("o p (j f) -> (o p) j f", j=2),
                              got[:, k, :, keys:W]).then_inc(s_stored[k], 16)

        @block.sync
        def _(sp):
            sp_chunk = []

            def load(it, k):
                q = it * PAIRS + k
                if messages and k % 2 == 0:
                    sp_chunk[:] = load_four(nc, SP, c.chunk_at, 2 * q, CHUNKS * P * STACK)
                if k % 2 == 0:
                    need(sp, s_hot, q - PAIRS + 2)
                    if messages:
                        need(sp, s_aturn, q - PAIRS + 2)
                    half = it * (PAIRS // 2) + k // 2
                    sp.dma_start(local[:, k // 2, :], local_rows[bass.ds(half, 1), :].to_broadcast([P, 4 * P])
                                 ).then_inc(s_local[k // 2], 16)
                if messages:
                    for j in range(2):
                        of = c.attr_dram[bass.ds(sp_chunk[k % 2 * 2 + j], P * STACK)]
                        sp.dma_start(attr[:, k, j, :], of.rearrange("(p d) -> p d", p=P)).then_inc(s_attr[k], 16)

            if messages:
                skewed(sp, [(0, load)], 0)
            else:
                skewed(sp, [(0, load), (3, lambda it, k: store(sp, it, k))], 3)
            for k in range(PAIRS):
                sp.wait_ge(s_stored[k], 16 * ITERS)

        @block.gpsimd
        def _(pool):
            def gather(it, k):
                q = it * PAIRS + k
                if k % 2 == 0:
                    pool.wait_ge(s_index, PAIRS // 2 * it + k // 2 + 1)
                need(pool, s_stored[k], 16 * it)
                need(pool, s_hturn if messages else s_sum, q - PAIRS + 1)
                pool.sem_inc(s_clear, 1)
                for j in range(2):
                    nc.gpsimd.indirect_dma_start(
                        got[:, k, j, :], None, c.gather_dram[layer][:, :],
                        bass.IndirectOffsetOnAxis(ap=index[:, k // 2, k % 2 * 2 + j:k % 2 * 2 + j + 1], axis=0),
                    ).then_inc(s_got[k], 16)

            skewed(pool, [(0, gather)], 0)

        @block.tensor
        def _(pe):
            pe_tile = []

            def turn_attr(it, k):
                q = it * PAIRS + k
                pe.wait_ge(s_attr[k], 32 * it + 32)
                need(pe, s_attr_t, q)
                for j in range(2):
                    last = nc.tensor.transpose(p_attr[:, j * P:(j + 1) * P], attr[:, k, j, :], c.ident_bf[:])
                last.then_inc(s_aturn, 1)

            def pick(it, k):
                q, s = it * PAIRS + k, k % 2
                if k % 2 == 0:
                    pe_tile[:] = load_four(nc, PE, c.tile_at[3 * Q], 2 * q, (TILES - 1) * 3 * Q)
                pe.wait_ge(s_hot, q + 1)
                need(pe, s_sum, q - 1)
                if messages:
                    pe.wait_ge(s_attr_t, q + 1)
                for j in range(2):
                    to = p_dst[s][:, j * Q:(j + 1) * Q]
                    parts = table_flat[:, bass.ds(pe_tile[k % 2 * 2 + j], 3 * Q)]
                    if messages:
                        nc.tensor.matmul(to, attr_t[:, k, j * P:(j + 1) * P], c.w_stack[:], start=True, stop=False)
                    for part in range(3):
                        last = nc.tensor.matmul(to, hot[:, k, j * P:(j + 1) * P],
                                                parts[:, part * Q:(part + 1) * Q],
                                                start=(part == 0 and not messages), stop=(part == 2))
                last.then_inc(s_dst, 1)

            def turn_hidden(it, k):
                q, s = it * PAIRS + k, k % 2
                pe.wait_ge(s_sum, q + 1)
                need(pe, s_hid_t, q - 1)
                for f in range(2):
                    for j in range(2):
                        last = nc.tensor.transpose(p_hid[s][:, (f * 2 + j) * P:(f * 2 + j + 1) * P],
                                                   got[:, k, j, f * P:(f + 1) * P], c.ident[:])
                last.then_inc(s_hturn, 1)

            def gate_hidden(it, k):
                q, s = it * PAIRS + k, k % 2
                pe.wait_ge(s_hid_t, q + 1)
                need(pe, s_score, q - 1)
                for f in range(2):
                    last = nc.tensor.matmul(p_gate[s][:, 0:2 * P], c.wg[:, f, :], hid_t[:, s, f, :],
                                            start=(f == 0), stop=(f == 1))
                last.then_inc(s_gmm, 1)

            def gate_score(it, k):
                q, s = it * PAIRS + k, k % 2
                pe.wait_ge(s_gate, q + 1)
                for j in range(2):
                    last = nc.tensor.matmul(p_gate[s][:, j:j + 1], gate[:, s, j * P:(j + 1) * P], c.gate_w[:],
                                            start=True, stop=True)
                last.then_inc(s_dot, 1)

            if messages:
                skewed(pe, [(5, gate_score), (4, gate_hidden), (3, turn_hidden), (2, pick), (0, turn_attr)], 5)
            else:
                skewed(pe, [(0, pick)], 0)

        if messages:
            @block.scalar
            def _(act):
                def keep_attr(it, k):
                    q = it * PAIRS + k
                    act.wait_ge(s_aturn, q + 1)
                    need(act, s_dst, q - PAIRS + 1)
                    nc.scalar.copy(attr_t[:, k, :], p_attr[:, 0:2 * P]).then_inc(s_attr_t, 1)

                def relu_hidden(it, k):
                    q, s = it * PAIRS + k, k % 2
                    act.wait_ge(s_hturn, q + 1)
                    need(act, s_gmm, q - 1)
                    nc.scalar.activation(hid_t[:, s, :, :].rearrange("p f e -> p (f e)"), p_hid[s][:],
                                         ACT.Relu).then_inc(s_hid_t, 1)

                def relu_gate(it, k):
                    q, s = it * PAIRS + k, k % 2
                    act.wait_ge(s_gmm, q + 1)
                    need(act, s_dot, q - 1)
                    nc.scalar.activation(gate[:, s, :], p_gate[s][:, 0:2 * P], ACT.Relu,
                                         bias=c.bg[:]).then_inc(s_gate, 1)

                skewed(act, [(4, relu_gate), (3, relu_hidden), (3, lambda it, k: store(act, it, k)), (0, keep_attr)], 4)

        @block.vector
        def _(dve):
            v = nc.vector

            def indices(half, step):
                v.tensor_copy(index[:, half, :], c.src_slot[:, bass.ds(step, 4)]).then_inc(s_index, 1)

            def one_hot(it, k):
                q = it * PAIRS + k
                dve.wait_ge(s_local[k // 2], 16 * it + 16)
                need(dve, s_dst, q - PAIRS + 1)
                v.tensor_scalar(hot[:, k, :], local[:, k // 2, k % 2 * 2 * P:(k % 2 + 1) * 2 * P], c.part_col[:, 0:1], None,
                                ALU.is_equal).then_inc(s_hot, 1)

            def combine(it, k):
                q, s = it * PAIRS + k, k % 2
                dve.wait_ge(s_dst, q + 1)
                dve.wait_ge(s_got[k], 32 * it + 32)
                ps = p_dst[s][:, 0:2 * Q].rearrange("p (j f) -> p j f", j=2)
                if messages:
                    v.tensor_tensor(got[:, k, :, 0:Q], ps, got[:, k, :, 0:Q], ALU.add).then_inc(s_sum, 1)
                else:
                    need(dve, s_score, q - 1)
                    v.tensor_tensor(prod[:, s, :, :], ps, got[:, k, :, 0:D], ALU.mult).then_inc(s_sum, 1)
                if k % 2 == 1:
                    indices(k // 2, it * UNROLL + UNROLL + k // 2 * 4)

            def score(it, k):
                q, s = it * PAIRS + k, k % 2
                to = c.score[:, bass.ds(q * 2 * heads, 2 * heads)]
                if messages:
                    dve.wait_ge(s_dot, q + 1)
                    v.tensor_scalar(to, p_gate[s][:, 0:2], c.gate_b[:], None, ALU.add).then_inc(s_score, 1)
                else:
                    dve.wait_ge(s_sum, q + 1)
                    v.tensor_reduce(to, prod[:, s, :, :].rearrange("p j (h f) -> p (j h) f", h=heads),
                                    AX.X, ALU.add).then_inc(s_score, 1)

            for half in range(PAIRS // 2):
                indices(half, half * 4)
            if messages:
                skewed(dve, [(5, score), (0, one_hot), (2, combine)], 5)
            else:
                skewed(dve, [(0, one_hot), (1, combine), (2, score)], 2)


def softmax_weights(nc, c, name, heads):
    H, L = heads, 4 * P
    with Stage(nc, name) as st:
        score = st.sb("score", [ROWS, H, L])
        run = st.sb("run", [ROWS, H, L])
        top = st.sb("top", [ROWS, H, L])
        edge = st.sb("edge", [ROWS, H])
        edge_t = st.sb("edge_t", [H, ROWS])
        carry = st.sb("carry", [H, ROWS + 1])
        carry_t = st.sb("carry_t", [ROWS, H])
        back = st.sb("back", [H, ROWS + 1])
        back_t = st.sb("back_t", [ROWS, H])
        p_in = [st.ps(f"in{i}", [P, L]) for i in range(2)]
        p_out = [st.ps(f"out{i}", [P, L]) for i in range(2)]
        p_e = st.ps("e", [P, 4 * P])
        s_in, s_row, s_dve, s_edge, s_edge_t = (st.sem(n) for n in ("in", "row", "dve_chain", "edge_s", "edge_ts"))
        s_carry, s_carry_t, s_shift, s_exp, s_turn, s_back = (
            st.sem(n) for n in ("carry_s", "carry_ts", "shift", "exp", "turn", "back_s"))
        block = st.block()
        by_row = c.score[:, 0:STEPS * H].rearrange("p (r a h) -> p a h r", a=4, h=H)

        @block.tensor
        def _(pe):
            for h in range(H):
                need(pe, s_row, h - 1)
                for a in range(4):
                    last = nc.tensor.transpose(p_in[h % 2][0:ROWS, a * P:(a + 1) * P], by_row[:, a, h, :], c.ident[:])
                last.then_inc(s_in, 1)
            for n in range(2):
                pe.wait_ge(s_edge, n + 1)
                nc.tensor.transpose(p_e[0:H, 0:ROWS], edge[:], c.ident[0:ROWS, 0:ROWS]).then_inc(s_edge_t, 1)
                pe.wait_ge(s_carry, n + 1)
                carried = carry[:, 0:ROWS] if n == 0 else back[:, 1:ROWS + 1]
                nc.tensor.transpose(p_e[0:ROWS, 0:H], carried, c.ident[0:H, 0:H]).then_inc(s_carry_t, 1)
            for h in range(H):
                pe.wait_ge(s_exp, h + 1)
                need(pe, s_back, h - 1)
                for a in range(4):
                    last = nc.tensor.transpose(p_out[h % 2][:, a * ROWS:(a + 1) * ROWS], score[:, h, a * P:(a + 1) * P],
                                               c.ident[0:ROWS, 0:ROWS])
                last.then_inc(s_turn, 1)

        @block.scalar
        def _(act):
            for h in range(H):
                act.wait_ge(s_in, h + 1)
                nc.scalar.copy(score[:, h, :], p_in[h % 2][0:ROWS, :]).then_inc(s_row, 1)
            for h in range(H):
                act.wait_ge(s_shift, h + 1)
                nc.scalar.activation(score[:, h, :], score[:, h, :], ACT.Exp).then_inc(s_exp, 1)

        @block.vector
        def _(dve):
            v = nc.vector
            link = linker(dve, s_dve)
            scan = v.tensor_tensor_scan
            rev = slice(None, None, -1)
            for n in range(2):
                for h in range(H):
                    if n == 0:
                        dve.wait_ge(s_row, h + 1)
                    ins = scan(run[:, h, :], c.start_big[:], score[:, h, :],
                               -BIG if n == 0 else carry_t[:, h:h + 1], ALU.add, ALU.max)
                link(ins)
                if n == 0:
                    v.memset(carry[:, 0:1], -BIG)
                    v.tensor_copy(edge[:], run[:, :, L - 1]).then_inc(s_edge, 1)
                    dve.wait_ge(s_edge_t, 1)
                    link(v.tensor_copy(edge_t[:], p_e[0:H, 0:ROWS]))
                    scan(carry[:, 1:ROWS + 1], c.row_start[0:H, :], edge_t[:], -BIG, ALU.add,
                         ALU.max).then_inc(s_carry, 1)
                    dve.wait_ge(s_carry_t, 1)
                    link(v.tensor_copy(carry_t[:], p_e[0:ROWS, 0:H]))
            link(v.tensor_tensor(run[:], run[:], c.last[:].unsqueeze(1).to_broadcast([ROWS, H, L]), ALU.mult))
            for n in range(2):
                for h in range(H):
                    ins = scan(top[:, h, rev], c.not_last[:, rev], run[:, h, rev],
                               0.0 if n == 0 else back_t[:, h:h + 1], ALU.mult, ALU.add)
                link(ins)
                if n == 0:
                    v.memset(back[:, ROWS:ROWS + 1], 0.0)
                    v.tensor_copy(edge[:], top[:, :, 0]).then_inc(s_edge, 1)
                    dve.wait_ge(s_edge_t, 2)
                    link(v.tensor_copy(edge_t[:], p_e[0:H, 0:ROWS]))
                    scan(back[:, slice(ROWS - 1, None, -1)], c.row_open[0:H, rev], edge_t[:, rev], 0.0, ALU.mult,
                         ALU.add).then_inc(s_carry, 1)
                    dve.wait_ge(s_carry_t, 2)
                    link(v.tensor_copy(back_t[:], p_e[0:ROWS, 0:H]))
            for h in range(H):
                v.tensor_tensor(score[:, h, :], score[:, h, :], top[:, h, :], ALU.subtract).then_inc(s_shift, 1)
            for h in range(H):
                dve.wait_ge(s_turn, h + 1)
                v.tensor_copy(by_row[:, :, h, :], p_out[h % 2][:, 0:4 * ROWS].rearrange("p (a r) -> p a r", a=4)
                              ).then_inc(s_back, 1)


BANKS = 8


def aggregate(nc, c, name, heads, messages):
    H = heads
    F = value_width(H, HM if messages else D)
    with Stage(nc, name) as st:
        pay = st.sb("pay", [P, PAIRS, 2, F])
        hot = st.sb("hot", [P, PAIRS, 2, P])
        sum_odd = st.sb("sum_odd", [P, TILES * F])
        sums = (c.sum[:].rearrange("p t f -> p (t f)"), sum_odd[:])
        p_sum = [st.ps(f"sum{i}", [P, 4 * P]) for i in range(BANKS)]
        s_pay = [st.sem(f"pay{k}") for k in range(PAIRS)]
        s_hot, s_weighted, s_mm, s_zero = (st.sem(n) for n in ("hot", "weighted", "mm", "zero"))
        s_sum = (st.sem("sum_even"), st.sem("sum_odd"))
        block = st.block()
        payload = c.payload_dram[0:STEPS * P * F].rearrange("(q p f) -> q p f", p=P, f=2 * F)

        @block.sync
        def _(sp):
            def load(it, k):
                q = it * PAIRS + k
                need(sp, s_mm, q - PAIRS + 1)
                sp.dma_start(pay[:, k, :, :].rearrange("p j f -> p (j f)"),
                             payload[bass.ds(q, 1), :, :].rearrange("o p f -> (o p) f")).then_inc(s_pay[k], 16)
            skewed(sp, [(0, load)], 0)

        if H == 1:
            @block.scalar
            def _(act):
                def weigh(it, k):
                    q = it * PAIRS + k
                    act.wait_ge(s_pay[k], 16 * it + 16)
                    for j in range(2):
                        ins = nc.scalar.activation(pay[:, k, j, :], pay[:, k, j, :], ACT.Relu if messages else ACT.Copy,
                                                   scale=c.score[:, bass.ds(2 * q + j, 1)])
                    ins.then_inc(s_weighted, 1)
                skewed(act, [(0, weigh)], 0)
        else:
            @block.gpsimd
            def _(pool):
                def weigh(it, k):
                    q = it * PAIRS + k
                    pool.wait_ge(s_pay[k], 16 * it + 16)
                    of = pay[:, k, :, :].rearrange("p j (h f) -> p (j h) f", h=H)
                    nc.gpsimd.tensor_tensor(of, of, c.score[:, bass.ds(2 * q * H, 2 * H)].unsqueeze(2)
                                            .to_broadcast([P, 2 * H, F // H]), ALU.mult).then_inc(s_weighted, 1)
                skewed(pool, [(0, weigh)], 0)

        @block.tensor
        def _(pe):
            def matmul(it, k):
                q = it * PAIRS + k
                pe.wait_ge(s_hot, q + 1)
                pe.wait_ge(s_weighted, q + 1)
                for j in range(2):
                    need(pe, s_sum[j], q - BANKS // 2 + 1)
                for j in range(2):
                    last = nc.tensor.matmul(p_sum[(2 * k + j) % BANKS][:, 0:F], hot[:, k, j, :], pay[:, k, j, :],
                                            start=True, stop=True)
                last.then_inc(s_mm, 1)
            skewed(pe, [(0, matmul)], 0)

        @block.vector
        def _(dve):
            for x in (c.sum, sum_odd):
                nc.vector.memset(x[:], 0.0).then_inc(s_zero, 1)
            dve.wait_ge(s_zero, 2)
            tile = []

            def one_hot(it, k):
                q = it * PAIRS + k
                if k % 2 == 0:
                    need(dve, s_mm, q - PAIRS + 2)
                    nc.vector.tensor_tensor(hot[:, k:k + 2, :, :].rearrange("p k j n -> p (k j) n"),
                                            c.node_row[:].unsqueeze(1).to_broadcast([P, 4, P]),
                                            c.local[:, bass.ds(2 * q, 4)].unsqueeze(2).to_broadcast([P, 4, P]),
                                            ALU.is_equal).then_inc(s_hot, 2)

            def accumulate(it, k):
                q = it * PAIRS + k
                if k % 2 == 0:
                    tile[:] = load_four(nc, DVE, c.tile_at[F], 2 * q, (TILES - 1) * F)
                dve.wait_ge(s_mm, q + 1)
                for j in range(2):
                    need(dve, s_sum[j], q)
                    to = sums[j][:, bass.ds(tile[k % 2 * 2 + j], F)]
                    nc.vector.tensor_tensor(to, to, p_sum[(2 * k + j) % BANKS][:, 0:F], ALU.add).then_inc(s_sum[j], 1)

            skewed(dve, [(0, one_hot), (2, accumulate)], 2)
            for j in range(2):
                dve.wait_ge(s_sum[j], ITERS * PAIRS)
            nc.vector.tensor_tensor(sums[0], sums[0], sums[1], ALU.add)


def update_nodes(nc, c):
    with Stage(nc, "update") as st:
        inv = st.sb("inv", [P, TILES])
        mean = st.sb("mean", [P, GROUP, HM + 1])
        mean_t = st.sb("mean_t", [P, GROUP, 3 * P])
        agg_t = st.sb("agg_t", [P, GROUP, P])
        hid_t = st.sb("hid_t", [P, GROUP, 2 * P])
        bank = [st.ps(f"bank{j}", [P, 4 * P]) for j in range(GROUP)]
        s_inv, s_mean, s_turn, s_mean_t, s_agg = (st.sem(n) for n in ("inv_s", "mean_s", "turn", "mean_ts", "agg"))
        s_agg_t, s_hid, s_hid_t, s_out, s_done = (st.sem(n) for n in ("agg_ts", "hid", "hid_ts", "out", "done"))
        block = st.block()

        @block.tensor
        def _(pe):
            mm = nc.tensor.matmul

            def body(g):
                n = g * GROUP
                pe.wait_ge(s_mean, g + 1)
                for j in range(GROUP):
                    need(pe, s_done, n + j - GROUP + 1)
                    for f in range(2):
                        nc.tensor.transpose(bank[j][:, f * P:(f + 1) * P], mean[:, j, f * P:(f + 1) * P], c.ident[:])
                    nc.tensor.transpose(bank[j][0:1, 2 * P:3 * P], mean[:, j, HM:HM + 1], c.ident[:]).then_inc(s_turn, 1)
                for j in range(GROUP):
                    pe.wait_ge(s_mean_t, n + j + 1)
                    to = bank[j][:, 0:P]
                    for f in range(2):
                        mm(to, c.w23[:, f, :], mean_t[:, j, f * P:(f + 1) * P], start=(f == 0), stop=False)
                    mm(to, c.b23[:], mean_t[0:1, j, 2 * P:3 * P], start=False, stop=True).then_inc(s_agg, 1)
                for j in range(GROUP):
                    pe.wait_ge(s_agg_t, n + j + 1)
                    for f in range(2):
                        to = bank[j][:, f * P:(f + 1) * P]
                        mm(to, c.up1[:, 0, f * P:(f + 1) * P],
                           c.ht[:, bass.ds(n + j, 1), :].rearrange("p o n -> p (o n)"), start=True, stop=False)
                        last = mm(to, c.up1[:, 1, f * P:(f + 1) * P], agg_t[:, j, :], start=False, stop=True)
                    last.then_inc(s_hid, 1)
                for j in range(GROUP):
                    pe.wait_ge(s_hid_t, n + j + 1)
                    to = bank[j][:, 0:P]
                    for f in range(2):
                        mm(to, hid_t[:, j, f * P:(f + 1) * P], c.u23[:, f, :], start=(f == 0), stop=False)
                    mm(to, c.ones[0:1, :], c.ub23[:], start=False, stop=True).then_inc(s_out, 1)

            body(0)
            with pe.Fori(1, GROUPS) as g:
                body(g)

        @block.scalar
        def _(act):
            def body(g):
                n = g * GROUP
                for j in range(GROUP):
                    act.wait_ge(s_turn, n + j + 1)
                    need(act, s_agg, n + j - GROUP + 1)
                    nc.scalar.copy(mean_t[:, j, 0:2 * P], bank[j][:, 0:2 * P])
                    nc.scalar.copy(mean_t[0:1, j, 2 * P:3 * P], bank[j][0:1, 2 * P:3 * P]).then_inc(s_mean_t, 1)
                for j in range(GROUP):
                    act.wait_ge(s_hid, n + j + 1)
                    need(act, s_out, n + j - GROUP + 1)
                    for f in range(2):
                        ins = nc.scalar.activation(hid_t[:, j, f * P:(f + 1) * P], bank[j][:, f * P:(f + 1) * P],
                                                   ACT.Relu, bias=c.up_b1[:, f:f + 1])
                    ins.then_inc(s_hid_t, 1)

            body(0)
            with act.Fori(1, GROUPS) as g:
                body(g)

        @block.vector
        def _(dve):
            v = nc.vector
            v.tensor_scalar(inv[:], c.sum[:, :, HM], ATTN_EPS, None, ALU.add).then_inc(s_inv, 1)
            dve.wait_ge(s_inv, 1)
            v.reciprocal(inv[:], inv[:]).then_inc(s_inv, 1)
            dve.wait_ge(s_inv, 2)

            def body(g):
                n = g * GROUP
                need(dve, s_turn, n)
                v.tensor_tensor(mean[:], c.sum[:, bass.ds(n, GROUP), 0:HM + 1],
                                inv[:, bass.ds(n, GROUP)].unsqueeze(2).to_broadcast([P, GROUP, HM + 1]),
                                ALU.mult).then_inc(s_mean, 1)
                for j in range(GROUP):
                    dve.wait_ge(s_agg, n + j + 1)
                    need(dve, s_hid, n + j - GROUP + 1)
                    v.tensor_copy(agg_t[:, j, :], bank[j][:, 0:P]).then_inc(s_agg_t, 1)
                for j in range(GROUP):
                    dve.wait_ge(s_out, n + j + 1)
                    to = c.x[:, bass.ds(n + j, 1), :].rearrange("p o d -> p (o d)")
                    v.tensor_tensor(to, to, bank[j][:, 0:P], ALU.add).then_inc(s_done, 1)

            body(0)
            with dve.Fori(1, GROUPS) as g:
                body(g)


def combine_heads(nc, c, name, heads, out):
    H = heads
    with Stage(nc, name) as st:
        inv = st.sb("inv", [P, TILES, H])
        s_chain, s_done, s_out = st.sem("chain"), st.sem("done"), st.sem("out")
        block = st.block()

        @block.vector
        def _(dve):
            v = nc.vector
            link = linker(dve, s_chain)
            sums = c.sum[:].rearrange("p t (h f) -> p t h f", h=H)
            link(v.tensor_scalar(inv[:], sums[:, :, :, D // H], ATTN_EPS, None, ALU.add))
            link(v.reciprocal(inv[:], inv[:]))
            link(v.tensor_tensor(c.h[:].rearrange("p t (h f) -> p t h f", h=H), sums[:, :, :, 0:D // H],
                                 inv[:].unsqueeze(3).to_broadcast([P, TILES, H, D // H]), ALU.mult))
            link(v.tensor_tensor(c.h[:], c.h[:], c.skip[:], ALU.add))
            if out is not None:
                v.tensor_tensor(c.h[:], c.h[:], c.x[:], ALU.add).then_inc(s_done, 1)

        if out is not None:
            @block.sync
            def _(sp):
                sp.wait_ge(s_done, 1)
                sp.dma_start(out[0:(TILES - 1) * P, :].rearrange("(t p) d -> p t d", p=P),
                             c.h[:, 0:TILES - 1, :]).then_inc(s_out, 16)
                sp.dma_start(out[(TILES - 1) * P:N, :], c.h[0:LAST_ROWS, TILES - 1, :]).then_inc(s_out, 16)
                sp.wait_ge(s_out, 32)


def stack_attributes(nc, c, attr):
    C = (CHUNKS + 1) // STACK_BLOCKS
    tail = FULL_CHUNKS % C
    with Stage(nc, "stack") as st:
        x = st.sb("x", [P, 2, C, DE])
        rest = st.sb("rest", [P, 2, C, DE])
        parts = st.sb("parts", [P, 2, C, STACK], BF16)
        w_rest = st.sb("w_rest", [DE, HM])
        w_part = st.sb("w_part", [DE, 3, HM], BF16)
        s_in = [st.sem(f"in{i}") for i in range(2)]
        s_out = [st.sem(f"out{i}") for i in range(2)]
        s_zero, s_hi, s_rest, s_mid, s_lo, s_copy, s_w, s_wout = (
            st.sem(n) for n in ("zero", "hi", "rest_s", "mid", "lo", "copy", "w", "wout"))
        block = st.block()
        rows = c.attr_dram.rearrange("(b c p d) -> b p c d", b=STACK_BLOCKS, p=P, d=STACK)

        def part(i, n):
            return parts[:, i, :, n * DE:(n + 1) * DE]

        @block.sync
        def _(sp):
            def load(_, __, attr):
                for n in range(STACK_BLOCKS):
                    i = n % 2
                    need(sp, s_lo, n - 1)
                    if n < STACK_BLOCKS - 1:
                        sp.dma_start(x[:, i, :, :], attr[n * C * P:(n + 1) * C * P, :]
                                     .rearrange("(c p) d -> p c d", p=P)).then_inc(s_in[i], 16)
                    else:
                        sp.wait_ge(s_zero, 1)
                        sp.dma_start(x[:, i, 0:tail, :], attr[n * C * P:FULL_CHUNKS * P, :]
                                     .rearrange("(c p) d -> p c d", p=P)).then_inc(s_in[i], 16)
                        sp.dma_start(x[0:TAIL, i, tail, :], attr[FULL_CHUNKS * P:E, :]).then_inc(s_in[i], 16)

            edge_sources(nc, c, sp, load, (None, None, attr))
            sp.wait_ge(s_w, 4)
            for n, of in enumerate((0, 1, 2, 0, 1, 0)):
                sp.dma_start(c.w_stack[n * DE:(n + 1) * DE, :], w_part[:, of, :]).then_inc(s_wout, 16)
            sp.wait_ge(s_wout, 16 * PARTS)

        @block.gpsimd
        def _(pool):
            for n in range(STACK_BLOCKS):
                pool.wait_ge(s_copy, n + 1)
                pool.wait_ge(s_lo, n + 1)
                pool.dma_start(rows[n], parts[:, n % 2, :, :]).then_inc(s_out[n % 2], 16)
            for i in range(2):
                pool.wait_ge(s_out[i], 16 * (STACK_BLOCKS // 2))

        @block.vector
        def _(dve):
            v = nc.vector
            v.tensor_copy(w_part[:, 0, :], c.w_edge[:]).then_inc(s_w, 1)
            dve.wait_ge(s_w, 1)
            v.tensor_tensor(w_rest[:], c.w_edge[:], w_part[:, 0, :], ALU.subtract).then_inc(s_w, 1)
            dve.wait_ge(s_w, 2)
            v.tensor_copy(w_part[:, 1, :], w_rest[:]).then_inc(s_w, 1)
            dve.wait_ge(s_w, 3)
            v.tensor_tensor(w_part[:, 2, :], w_rest[:], w_part[:, 1, :], ALU.subtract).then_inc(s_w, 1)
            for n in range(STACK_BLOCKS):
                i = n % 2
                if n == STACK_BLOCKS - 1:
                    v.memset(x[:, i, tail:C, :], 0.0).then_inc(s_zero, 1)
                dve.wait_ge(s_hi, n + 1)
                v.tensor_tensor(rest[:, i], x[:, i], part(i, 0), ALU.subtract).then_inc(s_rest, 1)
                v.tensor_copy(part(i, 1), part(i, 0))
                v.tensor_copy(part(i, 2), part(i, 0))
                dve.wait_ge(s_mid, n + 1)
                v.tensor_tensor(part(i, 5), rest[:, i], part(i, 3), ALU.subtract).then_inc(s_lo, 1)

        @block.scalar
        def _(act):
            for n in range(STACK_BLOCKS):
                i = n % 2
                act.wait_ge(s_in[i], 16 * (n // 2 + 1) + 16 * (n == STACK_BLOCKS - 1))
                need(act, s_out[i], 16 * (n // 2))
                nc.scalar.copy(part(i, 0), x[:, i]).then_inc(s_hi, 1)
                act.wait_ge(s_rest, n + 1)
                nc.scalar.copy(part(i, 3), rest[:, i]).then_inc(s_mid, 1)
                nc.scalar.copy(part(i, 4), rest[:, i]).then_inc(s_copy, 1)


class Shared:
    pass


def build(nc, a, out):
    c = Shared()
    with Stage(nc, "keep") as st:
        c.ones = st.sb("ones", [P, P])
        c.ident = st.sb("ident", [P, P])
        c.ident_bf = st.sb("ident_bf", [P, P], BF16)
        c.node_row = st.sb("node_row", [P, P])
        c.step_row = st.sb("step_row", [P, STEPS])
        c.part_col = st.sb("part_col", [P, KB])
        c.src_slot = st.sb("src_slot", [P, STEPS + UNROLL], I32)
        c.local = st.sb("local", [P, STEPS])
        c.start_big = st.sb("start_big", [ROWS, 4 * P])
        c.last = st.sb("last", [ROWS, 4 * P])
        c.not_last = st.sb("not_last", [ROWS, 4 * P])
        c.row_start = st.sb("row_start", [8, ROWS])
        c.row_open = st.sb("row_open", [8, ROWS])
        c.tile_at = {w: st.sb(f"tile_at{w}", [1, STEPS], I32)
                     for w in (3 * HM, 3 * D, HM + 1, HEADS * (D // HEADS + 1), D + 1)}
        c.unsorted = st.sb("unsorted", [1, 4], I32)
        c.chunk_at = st.sb("chunk_at", [1, STEPS], I32)
        c.x = st.sb("x", [P, TILES, D])
        c.h = st.sb("h", [P, TILES, D])
        c.ht = st.sb("ht", [P, TILES, P])
        c.skip = c.ht
        c.w_edge = st.sb("w_edge", [DE, HM])
        c.w_stack = st.sb("w_stack", [STACK, HM], BF16)
        c.w_node = [st.sb(f"w_node{i}", [P, 4 * D]) for i in range(3)]
        c.b_node = [st.sb(f"b_node{i}", [1, 4 * D]) for i in range(3)]
        c.up1 = st.sb("up1", [P, 2, HM])
        c.up_b1 = st.sb("up_b1", [P, 2])
        c.w23 = st.sb("w23", [P, 2, D])
        c.u23 = st.sb("u23", [P, 2, D])
        c.wg = st.sb("wg", [P, 2, D])
        c.bg, c.gate_w, c.gate_b = (st.sb(n, [P, 1]) for n in ("bg", "gate_w", "gate_b"))
        c.b23, c.ub23 = (st.sb(n, [1, D]) for n in ("b23", "ub23"))
        c.score = st.sb("score", [P, (STEPS + UNROLL) * HEADS])
        c.payload_dram = nc.dram_tensor("payload_dram", [STEPS * P * (HM + 1)], F32, kind="Internal").ap()
        c.attr_dram = nc.dram_tensor("attr_dram", [(CHUNKS + 1) * P * STACK], BF16, kind="Internal").ap()
        c.gather_dram = [nc.dram_tensor(f"gather{n}_dram", [NPAD, value_width(h, HM)], F32, kind="Internal").ap()
                         for n, h in enumerate((1, HEADS, 1))]
        c.local_dram = nc.dram_tensor("local_dram", [STEPS * P], BF16, kind="Internal").ap()
        c.key_dram = nc.dram_tensor("key_dram", [STEPS * P + 2], F32, kind="Internal").ap()
        c.edges = (nc.dram_tensor("src_dram", [E, 1], I32, kind="Internal").ap(),
                   nc.dram_tensor("dst_dram", [E, 1], I32, kind="Internal").ap(),
                   nc.dram_tensor("edge_attr_dram", [E, DE], F32, kind="Internal").ap())
        make_constants(nc, c)
        check_order(nc, c, a["dst"])
        sort_edges(nc, c, a["src"], a["dst"], a["edge_attr_16"])
        plan_steps(nc, c, a["src"], a["dst"])
        fold_weights(nc, c, a)
        stack_attributes(nc, c, a["edge_attr_16"])
        load_nodes(nc, c, a["x"])
        layer_norm(nc, c, "ln0")
        with Stage(nc, "layer0") as s0:
            table = s0.sb("table", [P, TILES, 3, HM], BF16)
            project(nc, c, "proj0", 0, 1, HM, 1.0, table, True)
            edge_scores(nc, c, "score0", 0, 1, True, table)
        softmax_weights(nc, c, "soft0", 1)
        with Stage(nc, "sums0") as s1:
            c.sum = s1.sb("sum", [P, TILES, HM + 1])
            aggregate(nc, c, "agg0", 1, True)
            update_nodes(nc, c)
        layer_norm(nc, c, "ln1")
        for layer, heads in ((1, HEADS), (2, 1)):
            with Stage(nc, f"layer{layer}") as s2:
                table = s2.sb("table", [P, TILES, 3, D], BF16)
                project(nc, c, f"proj{layer}", layer, heads, D, float(heads / D) ** 0.5, table, False)
                edge_scores(nc, c, f"score{layer}", layer, heads, False, table)
            softmax_weights(nc, c, f"soft{layer}", heads)
            with Stage(nc, f"sums{layer}") as s3:
                c.sum = s3.sb("sum", [P, TILES, D + heads])
                aggregate(nc, c, f"agg{layer}", heads, False)
                combine_heads(nc, c, f"heads{layer}", heads, out if layer == 2 else None)


_OUTS = [((N, D), "float32")]


def kernel(**inputs):
    import numpy as _np
    import concourse.bacc as _bacc
    from concourse import mybir as _mybir
    from concourse.bass_utils import run_bass_kernel_spmd as _run

    nc = _bacc.Bacc("TRN2", target_bir_lowering=False, num_devices=1)
    arrays, args = {}, {}
    for name, value in inputs.items():
        a = _np.ascontiguousarray(value)
        arrays[f"in_{name}_dram"] = a
        args[name] = nc.dram_tensor(f"in_{name}_dram", a.shape, _mybir.dt.from_np(a.dtype), kind="ExternalInput").ap()
    shape, dtype = _OUTS[0]
    out = nc.dram_tensor("out_0_dram", shape, _mybir.dt.from_np(_np.dtype(dtype)), kind="ExternalOutput").ap()
    build(nc, args, out)
    r = _run(nc, [arrays], core_ids=[0])
    return r.results[0]["out_0_dram"]
```

```python
import concourse.bass as bass
from concourse import mybir
from contextlib import ExitStack

F32 = mybir.dt.float32
BF16 = mybir.dt.bfloat16
I32 = mybir.dt.int32
ALU = mybir.AluOpType
ACT = mybir.ActivationFunctionType
AX = mybir.AxisListType
SP, PE, DVE = mybir.EngineType.SP, mybir.EngineType.PE, mybir.EngineType.DVE

P = 128
N, E, D, DE = 3125, 50000, 128, 16
TILES = -(-N // P)
CHUNKS = -(-E // P)
LAST_ROWS = N - (TILES - 1) * P
FULL_CHUNKS = E // P
TAIL = E - FULL_CHUNKS * P
BANKS = 8
UNROLL = 16
STEPS = -(-(CHUNKS + TILES - 1) // UNROLL) * UNROLL
ITERS = STEPS // UNROLL
PAIRS = UNROLL // 2
ROWS = STEPS // 4
KB = -(-CHUNKS // P)
NO_NODE = TILES * P + 800.0
NOT_HERE = 255.0
BIG = 1.0e30
NPAD = TILES * P
HEADS = 8
PARTS = 6
STACK = PARTS * DE
STACK_BLOCKS = 8


def value_width(heads, width):
    return width + heads
HM = 256
LN_EPS = 1e-5
ATTN_EPS = 1e-16


class Stage:

    def __init__(self, nc, name):
        self.nc, self.name, self.ctx, self.sems = nc, name, ExitStack(), []

    def __enter__(self):
        self.ctx.__enter__()
        return self

    def __exit__(self, *a):
        self.ctx.__exit__(*a)
        if self.sems:
            self.nc.clear_and_free_semaphores(self.sems)
            self.nc.all_engine_barrier()

    def sb(self, name, shape, dt=F32):
        return self.ctx.enter_context(self.nc.sbuf_tensor(f"{self.name}_{name}", shape, dt))

    def ps(self, name, shape, dt=F32):
        return self.ctx.enter_context(self.nc.psum_tensor(f"{self.name}_{name}", shape, dt))

    def sem(self, name):
        self.sems.append(self.nc.alloc_semaphore(f"{self.name}_{name}"))
        return self.sems[-1]

    def block(self):
        return self.ctx.enter_context(self.nc.Block())


def linker(eng, sem):
    done = [0]

    def link(ins):
        done[0] += 1
        ins.then_inc(sem, 1)
        eng.wait_ge(sem, done[0])
    return link


def make_constants(nc, c):
    with Stage(nc, "const") as st:
        s_pool, s_made, s_int = st.sem("pool_chain"), st.sem("made"), st.sem("ints")
        node_i = st.sb("node_i", [P, P], I32)
        step_i = st.sb("step_i", [P, STEPS], I32)
        part_i = st.sb("part_i", [P, KB], I32)
        block = st.block()

        @block.gpsimd
        def _(pool):
            link = linker(pool, s_pool)
            nc.gpsimd.memset(c.ones[:], 1.0)
            link(nc.gpsimd.memset(c.ident[:], 0.0))
            nc.gpsimd.affine_select(out=c.ident[:], in_=c.ident[:], compare_op=ALU.not_equal, fill=1.0,
                                    base=0, pattern=[[-1, P]], channel_multiplier=1).then_inc(s_made, 1)
            nc.gpsimd.iota(node_i[:], [[1, P]], base=0, channel_multiplier=0).then_inc(s_int, 1)
            nc.gpsimd.iota(step_i[:], [[1, STEPS]], base=0, channel_multiplier=0).then_inc(s_int, 1)
            nc.gpsimd.iota(part_i[:], [[P, KB]], base=0, channel_multiplier=1).then_inc(s_int, 1)

        @block.vector
        def _(dve):
            dve.wait_ge(s_int, 3)
            nc.vector.tensor_copy(c.node_row[:], node_i[:])
            nc.vector.tensor_copy(c.step_row[:], step_i[:])
            nc.vector.tensor_copy(c.part_col[:], part_i[:])
            dve.wait_ge(s_made, 1)
            nc.vector.tensor_copy(c.ident_bf[:], c.ident[:])
            nc.vector.tensor_copy(c.ones_bf[:], c.ones[:])


def check_order(nc, c, dst):
    rows = P - 3
    cols = E // rows
    with Stage(nc, "order") as st:
        this = st.sb("this", [rows, cols], I32)
        following = st.sb("following", [rows, cols], I32)
        descends = st.sb("descends", [rows, cols])
        found = st.sb("found", [rows, 1])
        p_found = st.ps("found_ps", [1, 4])
        s_last, s_in, s_chain, s_sum = (st.sem(n) for n in ("last", "in", "chain", "sum"))
        block = st.block()

        @block.sync
        def _(sp):
            sp.dma_start(this[:], dst.rearrange("(r s) -> r s", r=rows)).then_inc(s_in, 16)
            sp.wait_ge(s_last, 1)
            sp.dma_start(following[0:rows - 1, :], dst[1:1 + (rows - 1) * cols]
                         .rearrange("(r s) -> r s", s=cols)).then_inc(s_in, 16)
            sp.dma_start(following[rows - 1:rows, 0:cols - 1], dst[1 + (rows - 1) * cols:E]
                         .rearrange("(r s) -> r s", r=1)).then_inc(s_in, 16)

        @block.gpsimd
        def _(pool):
            nc.gpsimd.memset(following[:, cols - 1:cols], int(NO_NODE)).then_inc(s_last, 1)

        @block.vector
        def _(dve):
            v = nc.vector
            link = linker(dve, s_chain)
            dve.wait_ge(s_in, 48)
            link(v.tensor_tensor(descends[:], this[:], following[:], ALU.is_gt))
            link(v.reduce_max(found[:], descends[:], AX.X))
            dve.wait_ge(s_sum, 1)
            v.tensor_copy(c.unsorted[:], p_found[:])

        @block.tensor
        def _(pe):
            pe.wait_ge(s_chain, 2)
            for n in range(4):
                last = nc.tensor.matmul(p_found[:, n:n + 1], c.ones[0:rows, 0:1], found[:], start=True, stop=True)
            last.then_inc(s_sum, 1)


def load_unsorted(nc, c, engine):
    values = nc.values_load_multi_w_load_instructions(
        c.unsorted[0:1, 0:4], engines=[engine], min_val=0, max_val=P,
        skip_runtime_bounds_check_because="check_order counts at most 128 rows")[1]
    return values[0]


PIECES = 8
PIECE_CHUNKS = -(-CHUNKS // PIECES)


def sort_edges(nc, c, src, dst, attr):
    COLS, L = PIECES * PIECE_CHUNKS, PIECE_CHUNKS * P
    with Stage(nc, "sort") as st:
        raw = st.sb("raw", [P, L], I32)
        others = st.sb("others", [P, L])
        less = st.sb("less", [P, L], BF16)
        same = st.sb("same", [P, P])
        earlier = st.sb("earlier", [P, P])
        dst_col = st.sb("dst_col", [P, COLS], I32)
        src_col = st.sb("src_col", [P, COLS], I32)
        own = st.sb("own", [P, COLS])
        below = st.sb("below", [P, PIECES + 1, COLS])
        rank = st.sb("rank", [P, COLS])
        place = st.sb("place", [P, COLS], I32)
        edge_attr = st.sb("edge_attr", [P, CHUNKS, DE])
        slot_place, slot_src, slot_dst = (st.sb(n, [P, 1], I32) for n in ("slot_place", "slot_src", "slot_dst"))
        slot_attr = st.sb("slot_attr", [P, DE])
        s_padded, s_cols, s_piece, s_used = (st.sem(n) for n in ("padded", "cols", "piece", "used"))
        s_chain, s_placed, s_slot, s_clear, s_moved = (
            st.sem(n) for n in ("chain", "placed", "slot", "clear", "moved"))
        block = st.block()

        @block.sync
        def _(sp):
            with sp.If(load_unsorted(nc, c, SP) > 0):
                sp.wait_ge(s_padded, 2)
                full = FULL_CHUNKS * P
                for to, of in ((dst_col, dst), (src_col, src)):
                    sp.dma_start(to[:, 0:FULL_CHUNKS], of[0:full].rearrange("(c p) -> p c", p=P),
                                 allow_slow_non_contiguous=True).then_inc(s_cols, 16)
                    sp.dma_start(to[0:TAIL, FULL_CHUNKS:CHUNKS],
                                 of[full:E].rearrange("(c p) -> p c", c=1)).then_inc(s_cols, 16)
                for n in range(PIECES):
                    lo, hi = n * PIECE_CHUNKS, min((n + 1) * PIECE_CHUNKS, FULL_CHUNKS)
                    sp.dma_start(edge_attr[:, lo:hi, :],
                                 attr[lo * P:hi * P, :].rearrange("(c p) d -> p c d", p=P)).then_inc(s_cols, 16)
                sp.dma_start(edge_attr[0:TAIL, FULL_CHUNKS, :], attr[full:E, :]).then_inc(s_cols, 16)
                for n in range(PIECES):
                    need(sp, s_used, n)
                    size = min(L, E - n * L)
                    sp.dma_start(raw[:, 0:size], dst[n * L:n * L + size].rearrange("(o s) -> o s", o=1)
                                 .to_broadcast([P, size])).then_inc(s_piece, 16)

        @block.vector
        def _(dve):
            v = nc.vector
            with dve.If(load_unsorted(nc, c, DVE) > 0):
                v.memset(dst_col[:, FULL_CHUNKS:COLS], int(NO_NODE)).then_inc(s_padded, 1)
                v.memset(src_col[:, FULL_CHUNKS:COLS], 0).then_inc(s_padded, 1)
                v.memset(below[:], 0.0)
                v.tensor_scalar(earlier[:], c.node_row[:], c.part_col[:, 0:1], None, ALU.is_lt)
                dve.wait_ge(s_cols, 16 * (5 + PIECES))
                v.tensor_scalar(own[:], dst_col[:], 2.0, None, ALU.mult).then_inc(s_chain, 1)
                done = 1
                for n in range(PIECES):
                    dve.wait_ge(s_piece, 16 * n + 16)
                    if n == PIECES - 1:
                        v.memset(raw[:, E - n * L:L], int(NO_NODE)).then_inc(s_chain, 1)
                        done += 1
                    dve.wait_ge(s_chain, done)
                    v.tensor_scalar(others[:], raw[:], 2.0, None, ALU.mult).then_inc(s_used, 1)
                    dve.wait_ge(s_used, n + 1)
                    first, end = n * PIECE_CHUNKS, (n + 1) * PIECE_CHUNKS
                    for lo, hi, each in ((0, first, 1), (first, end, 3), (end, COLS, 1)):
                        if lo == hi:
                            continue
                        with dve.Fori(lo, hi) as j:
                            chained = (j - lo) * each + done
                            mine = own[:, bass.ds(j, 1)]
                            v.tensor_scalar(less[:], others[:], mine, 0.0, ALU.is_lt, ALU.add,
                                            accum_out=below[:, n, bass.ds(j, 1)]).then_inc(s_chain, 1)
                            dve.wait_ge(s_chain, chained + 1)
                            if each == 3:
                                chunk = others[:, bass.ds((j - lo) * P, P)]
                                v.scalar_tensor_tensor(same[:], chunk, mine, earlier[:], ALU.is_equal, ALU.mult,
                                                       accum_out=below[:, PIECES, bass.ds(j, 1)]).then_inc(s_chain, 1)
                                dve.wait_ge(s_chain, chained + 2)
                                v.tensor_scalar(chunk, chunk, -1.0, None, ALU.add).then_inc(s_chain, 1)
                                dve.wait_ge(s_chain, chained + 3)
                        done += (hi - lo) * each
                v.tensor_reduce(rank[:], below[:].rearrange("p n c -> p c n"), AX.X, ALU.add).then_inc(s_chain, 1)
                dve.wait_ge(s_chain, done + 1)
                v.tensor_copy(place[:], rank[:]).then_inc(s_placed, 1)

        @block.gpsimd
        def _(pool):
            def move(j, rows):
                for to, of in ((slot_place[0:rows, :], place[0:rows, bass.ds(j, 1)]),
                               (slot_src[0:rows, :], src_col[0:rows, bass.ds(j, 1)]),
                               (slot_dst[0:rows, :], dst_col[0:rows, bass.ds(j, 1)]),
                               (slot_attr[0:rows, :],
                                edge_attr[0:rows, bass.ds(j, 1), :].rearrange("p o d -> p (o d)"))):
                    nc.gpsimd.tensor_copy(to, of).then_inc(s_slot, 1)
                pool.wait_ge(s_slot, j * 4 + 4)
                pool.sem_inc(s_clear, 1)
                for rows_in, to in zip((slot_src, slot_dst, slot_attr), c.edges):
                    nc.gpsimd.indirect_dma_start(to, bass.IndirectOffsetOnAxis(ap=slot_place[0:rows, 0:1], axis=0),
                                                 rows_in[0:rows, :], None).then_inc(s_moved, 16)
                pool.wait_ge(s_moved, j * 48 + 48)
                pool.sem_inc(s_clear, 1)

            with pool.If(load_unsorted(nc, c, mybir.EngineType.Pool) > 0):
                pool.wait_ge(s_placed, 1)
                pool.wait_ge(s_cols, 16 * (5 + PIECES))
                with pool.Fori(0, FULL_CHUNKS) as j:
                    move(j, P)
                move(FULL_CHUNKS, TAIL)


def edge_sources(nc, c, sp, load, given):
    unsorted = load_unsorted(nc, c, SP)
    with sp.If(unsorted < 1):
        load(*given)
    with sp.If(unsorted > 0):
        load(c.edges[0].rearrange("e o -> (e o)"), c.edges[1].rearrange("e o -> (e o)"), c.edges[2])


def plan_and_stack(nc, c, src, dst, attr):
    with Stage(nc, "stack") as st2, Stage(nc, "plan") as st:
        load_stack, stack_weights, stack_pool, stack_act = stack_attributes(nc, c, st2, attr)
        ends = st.sb("ends", [P, KB * P], I32)
        starts = st.sb("starts", [P, KB * P], I32)
        endf = st.sb("endf", [P, KB * P])
        startf = st.sb("startf", [P, KB * P])
        junk = st.sb("junk", [P, 2, KB * P])
        count = st.sb("count", [P, TILES - 1])
        count_i = st.sb("count_i", [P, TILES - 1], I32)
        chunk_i = st.sb("chunk_i", [P, TILES - 1], I32)
        turn = st.sb("turn", [P, TILES - 1])
        tile = st.sb("tile", [P, STEPS])
        tile_half = st.sb("tile_half", [P, 2, STEPS])
        chunk = st.sb("chunk", [P, STEPS])
        pick = st.sb("pick", [P, KB, STEPS])
        dst_slot = st.sb("dst_slot", [P, STEPS])
        local = st.sb("local", [P, STEPS])
        valid = st.sb("valid", [P, STEPS])
        upper = st.sb("upper", [P, STEPS])
        key = st.sb("key", [P, STEPS])
        local_row = st.sb("local_row", [ROWS, 4 * P], BF16)
        key_row = st.sb("key_row", [ROWS, 4 * P])
        key_prev = st.sb("key_prev", [ROWS, 4 * P])
        key_next = st.sb("key_next", [ROWS, 4 * P])
        fence = st.sb("fence", [1, 2])
        flag = st.sb("flag", [ROWS, 4])
        flag8 = st.sb("flag8", [ROWS, 16])
        ps_count = st.ps("count_ps", [P, TILES - 1])
        ps_dst = st.ps("dst_ps", [P, STEPS])
        ps_src = st.ps("src_ps", [P, STEPS])
        ps_row = [st.ps(f"row_ps{i}", [ROWS, 4 * P]) for i in range(2)]
        ps_flag = st.ps("flag_ps", [8, 2 * P])
        s_padded, s_in, s_counted, s_total = (st.sem(n) for n in ("padded", "in", "counted", "total"))
        s_picked, s_slots, s_local, s_turned = (st.sem(n) for n in ("picked", "slots", "local", "turned"))
        s_rows, s_out, s_shift, s_dve = (st.sem(n) for n in ("rows", "out", "shift", "dve_chain"))
        s_flag, s_flagt, s_bias, s_left = (st.sem(n) for n in ("flag", "flagt", "bias", "left"))
        block = st.block()

        @block.sync
        def _(sp):
            sp.wait_ge(s_padded, 2)

            def load(src, dst, attr):
                for to, of in ((ends, dst), (starts, src)):
                    whole = (KB - 1) * P * P
                    sp.dma_start(to[:, 0:(KB - 1) * P].rearrange("q (k p) -> q k p", p=P),
                                 of[0:whole].rearrange("(k q p) -> q k p", q=P, p=P)).then_inc(s_in, 16)
                    rows = FULL_CHUNKS - (KB - 1) * P
                    sp.dma_start(to[0:rows, (KB - 1) * P:KB * P],
                                 of[whole:FULL_CHUNKS * P].rearrange("(q p) -> q p", p=P)).then_inc(s_in, 16)
                    sp.dma_start(to[rows:rows + 1, (KB - 1) * P:(KB - 1) * P + TAIL],
                                 of[FULL_CHUNKS * P:E].rearrange("(q p) -> q p", q=1)).then_inc(s_in, 16)
                load_stack(sp, attr)

            edge_sources(nc, c, sp, load, (src, dst, attr))
            for n in range(3):
                sp.dma_start(c.bg_parts[n:n + 1, :], c.bg_part[:, n, :]).then_inc(s_bias, 16)
            sp.wait_ge(s_bias, 48)
            stack_weights(sp)
            sp.wait_ge(s_rows, 2)
            sp.dma_start(c.local_dram.rearrange("(r s) -> r s", r=ROWS), local_row[:]).then_inc(s_out, 16)
            sp.dma_start(c.key_dram[1:1 + STEPS * P].rearrange("(r s) -> r s", r=ROWS), key_row[:]).then_inc(s_out, 16)
            sp.dma_start(c.key_dram[0:1].rearrange("(a b) -> a b", a=1), fence[0:1, 0:1]).then_inc(s_out, 16)
            sp.dma_start(c.key_dram[1 + STEPS * P:2 + STEPS * P].rearrange("(a b) -> a b", a=1),
                         fence[0:1, 1:2]).then_inc(s_out, 16)
            sp.wait_ge(s_out, 64)
            sp.dma_start(key_prev[:], c.key_dram[0:STEPS * P].rearrange("(r s) -> r s", r=ROWS)).then_inc(s_shift, 16)
            sp.dma_start(key_next[:], c.key_dram[2:2 + STEPS * P].rearrange("(r s) -> r s", r=ROWS)
                         ).then_inc(s_shift, 16)

        @block.gpsimd
        def _(pool):
            stack_pool(pool)

        @block.scalar
        def _(act):
            stack_act(act)

        @block.vector
        def _(dve):
            link = linker(dve, s_dve)
            v = nc.vector
            v.memset(ends[:, (KB - 1) * P:KB * P], int(NO_NODE)).then_inc(s_padded, 1)
            v.memset(starts[:, (KB - 1) * P:KB * P], 0).then_inc(s_padded, 1)
            v.memset(fence[:], -5.0)
            dve.wait_ge(s_in, 96)
            v.tensor_copy(startf[:], starts[:])
            link(v.tensor_copy(endf[:], ends[:]))
            for t in range(TILES - 1):
                need(dve, s_counted, t - 1)
                v.tensor_scalar(junk[:, t % 2], endf[:], float(P * (t + 1)), 0.0, ALU.is_lt, ALU.add,
                                accum_out=count[:, t:t + 1]).then_inc(s_counted, 1)
            dve.wait_ge(s_total, 1)
            link(v.tensor_copy(count_i[:], ps_count[:]))
            link(v.tensor_single_scalar(chunk_i[:], count_i[:], 7, ALU.arith_shift_right))
            link(v.tensor_copy(turn[:], chunk_i[:]))
            link(v.tensor_tensor(turn[:], turn[:], c.step_row[:, 0:TILES - 1], ALU.add))
            link(v.memset(tile_half[:], 0.0))
            for t in range(TILES - 1):
                to = tile_half[:, t % 2]
                need(dve, s_left, t - 1)
                v.scalar_tensor_tensor(to, c.step_row[:], turn[:, t:t + 1], to, ALU.is_gt, ALU.add).then_inc(s_left, 1)
            dve.wait_ge(s_left, TILES - 1)
            link(v.tensor_tensor(tile[:], tile_half[:, 0], tile_half[:, 1], ALU.add))
            link(v.tensor_tensor(chunk[:], c.step_row[:], tile[:], ALU.subtract))
            for k in range(KB):
                ins = v.tensor_scalar(pick[:, k, :], chunk[:], c.part_col[:, k:k + 1], None, ALU.is_equal)
                ins.then_inc(s_picked, 1)
            for width, at in c.tile_at.items():
                v.tensor_scalar(at[:], tile[0:1, :], float(width), None, ALU.mult)
            v.tensor_scalar(c.chunk_at[:], chunk[0:1, :], float(P * STACK), None, ALU.mult)
            dve.wait_ge(s_slots, 1)
            link(v.tensor_copy(dst_slot[:], ps_dst[:]))
            v.tensor_copy(c.src_slot[:, 0:STEPS], ps_src[:])
            v.memset(c.src_slot[:, STEPS:], 0)
            link(v.scalar_tensor_tensor(local[:], tile[:], -float(P), dst_slot[:], ALU.mult, ALU.add))
            v.tensor_scalar(upper[:], local[:], float(P), None, ALU.is_lt)
            link(v.tensor_scalar(valid[:], local[:], 0.0, None, ALU.is_ge))
            link(v.tensor_tensor(valid[:], valid[:], upper[:], ALU.mult))
            link(v.scalar_tensor_tensor(c.local[:], local[:], -NOT_HERE, valid[:], ALU.add, ALU.mult))
            link(v.tensor_scalar(c.local[:], c.local[:], NOT_HERE, None, ALU.add))
            v.scalar_tensor_tensor(key[:], dst_slot[:], 1.0, valid[:], ALU.add, ALU.mult).then_inc(s_local, 1)
            dve.wait_ge(s_turned, 2)
            v.tensor_copy(local_row[:], ps_row[0][:]).then_inc(s_rows, 1)
            v.tensor_copy(key_row[:], ps_row[1][:]).then_inc(s_rows, 1)
            dve.wait_ge(s_rows, 2)
            dve.wait_ge(s_shift, 32)
            link(v.tensor_tensor(c.start_big[:], key_row[:], key_prev[:], ALU.not_equal))
            link(v.tensor_tensor(c.last[:], key_row[:], key_next[:], ALU.not_equal))
            link(v.reduce_max(flag[:, 0:1], c.start_big[:], AX.X))
            link(v.tensor_scalar(c.start_big[:], c.start_big[:], -BIG, None, ALU.mult))
            link(v.tensor_scalar(c.not_last[:], c.last[:], -1.0, 1.0, ALU.mult, ALU.add))
            link(v.tensor_reduce(flag[:, 1:2], c.not_last[:], AX.X, ALU.min))
            link(v.tensor_scalar(flag[:, 0:1], flag[:, 0:1], -BIG, None, ALU.mult))
            link(v.tensor_copy(flag8[:, 0:8], flag[:, 0:1].to_broadcast([ROWS, 8])))
            v.tensor_copy(flag8[:, 8:16], flag[:, 1:2].to_broadcast([ROWS, 8])).then_inc(s_flag, 1)
            dve.wait_ge(s_flagt, 1)
            v.tensor_copy(c.row_start[:], ps_flag[:, 0:ROWS])
            v.tensor_copy(c.row_open[:], ps_flag[:, P:P + ROWS])

        @block.tensor
        def _(pe):
            pe.wait_ge(s_counted, TILES - 1)
            nc.tensor.matmul(ps_count[:], c.ones[:], count[:], start=True, stop=True).then_inc(s_total, 1)
            pe.wait_ge(s_picked, KB)
            for ps, rows in ((ps_dst, endf), (ps_src, startf)):
                for k in range(KB):
                    last = nc.tensor.matmul(ps[:], rows[:, k * P:(k + 1) * P], pick[:, k, :],
                                            start=(k == 0), stop=(k == KB - 1))
            last.then_inc(s_slots, 1)
            pe.wait_ge(s_local, 1)
            for ps, x in zip(ps_row, (c.local, key)):
                for a in range(4):
                    last = nc.tensor.transpose(ps[:, a * P:(a + 1) * P],
                                               x[:].rearrange("p (r a) -> p a r", a=4)[:, a, :], c.ident[:])
                last.then_inc(s_turned, 1)
            pe.wait_ge(s_flag, 1)
            nc.tensor.transpose(ps_flag[:, 0:ROWS], flag8[:, 0:8], c.ident[0:ROWS, 0:ROWS])
            nc.tensor.transpose(ps_flag[:, P:P + ROWS], flag8[:, 8:16],
                                c.ident[0:ROWS, 0:ROWS]).then_inc(s_flagt, 1)



def norm_programs(nc, c, st):
    sq = st.sb("sq", [P, TILES, D])
    mean, var, std, rstd = (st.sb(n, [P, TILES]) for n in ("mean", "var", "std", "rstd"))
    s_chain, s_cent, s_sq, s_var, s_std = (st.sem(n) for n in ("chain", "cent", "sq_s", "var_s", "std_s"))

    def vector(dve):
        v = nc.vector
        link = linker(dve, s_chain)
        link(v.tensor_reduce(mean[:], c.x[:], AX.X, ALU.add))
        link(v.tensor_scalar(mean[:], mean[:], 1.0 / D, None, ALU.mult))
        v.tensor_tensor(c.h[:], c.x[:], mean[:].unsqueeze(2).to_broadcast([P, TILES, D]),
                        ALU.subtract).then_inc(s_cent, 1)
        dve.wait_ge(s_sq, 1)
        link(v.tensor_reduce(var[:], sq[:], AX.X, ALU.add))
        v.tensor_scalar(var[:], var[:], 1.0 / D, LN_EPS, ALU.mult, ALU.add).then_inc(s_var, 1)
        dve.wait_ge(s_std, 1)
        link(v.reciprocal(rstd[:], std[:]))
        link(v.tensor_tensor(std[:], rstd[:], rstd[:], ALU.mult))
        link(v.tensor_tensor(std[:], std[:], var[:], ALU.mult))
        link(v.tensor_scalar(std[:], std[:], -0.5, 1.5, ALU.mult, ALU.add))
        link(v.tensor_tensor(rstd[:], rstd[:], std[:], ALU.mult))
        v.scalar_tensor_tensor(c.h[:], c.h[:], 0.0, rstd[:].unsqueeze(2).to_broadcast([P, TILES, D]),
                               ALU.max, ALU.mult)

    def scalar(act):
        act.wait_ge(s_cent, 1)
        nc.scalar.activation(sq[:], c.h[:], ACT.Square).then_inc(s_sq, 1)
        act.wait_ge(s_var, 1)
        nc.scalar.activation(std[:], var[:], ACT.Sqrt).then_inc(s_std, 1)

    return vector, scalar


def layer_norm(nc, c, name):
    with Stage(nc, name) as st:
        vector, scalar = norm_programs(nc, c, st)
        block = st.block()

        @block.vector
        def _(dve):
            vector(dve)

        @block.scalar
        def _(act):
            scalar(act)


def fold_weights(nc, c, a):
    with Stage(nc, "fold") as st:
        w2 = st.sb("w2", [P, 2, HM])
        w3 = st.sb("w3", [P, 2, D])
        u2 = st.sb("u2", [P, 2, HM])
        u3 = st.sb("u3", [P, 2, D])
        w2t = st.sb("w2t", [P, 2, HM])
        u2t = st.sb("u2t", [P, 2, HM])
        w23t = st.sb("w23t", [P, HM])
        ag1, ag2, ag2t = (st.sb(n, [P, D]) for n in ("ag1", "ag2", "ag2t"))
        ag3 = st.sb("ag3", [P, 1])
        ag3_wide = st.sb("ag3_wide", [P, P])
        cols = st.sb("cols", [P, 7])
        rows = st.sb("rows", [1, 3 * D + 1])
        bg = st.sb("bg", [1, D])
        bg_rest = st.sb("bg_rest", [1, D])
        agb2 = st.sb("agb2", [P, P])
        pt = [st.ps(f"turn{i}", [P, 4 * P]) for i in range(2)]
        pa = st.ps("pa", [P, 4 * P])
        pw, pg, pu, px = (st.ps(n, [P, 4 * P]) for n in ("pw", "pg", "pu", "px"))
        s_in, s_turn, s_flat, s_mm = (st.sem(n) for n in ("in", "turn", "flat", "mm"))
        s_mid, s_g = st.sem("mid"), st.sem("g")
        s_split, s_parts, s_gate = (st.sem(n) for n in ("split", "parts", "gate_s"))
        b_node = st.sb("b_node", [1, 3, 4 * D])
        b_rest = st.sb("b_rest", [1, 3, 4 * D])
        b_part = st.sb("b_part", [1, 3, 3, 4 * D], BF16)
        s_zero, s_x = st.sem("zero"), st.sem("x")
        norm_vector, norm_scalar = norm_programs(nc, c, st)
        LOADS = []

        def col(name, k):
            return a[name][k * P:(k + 1) * P].rearrange("(p o) -> p o", o=1)

        def row(name):
            return a[name].rearrange("(o n) -> o n", o=1)

        pre = "L0_gnn_"
        LOADS += [(w2[:], a[pre + "msg_w2"].rearrange("(k p) n -> p k n", p=P)),
                  (w3[:], a[pre + "msg_w3"].rearrange("(k p) n -> p k n", p=P)),
                  (u2[:], a[pre + "up_w2"].rearrange("(k p) n -> p k n", p=P)),
                  (u3[:], a[pre + "up_w3"].rearrange("(k p) n -> p k n", p=P)),
                  (c.up1[:], a[pre + "up_w1"].rearrange("(k p) n -> p k n", p=P)),
                  (c.w_edge[:], a[pre + "msg_w1"][0:DE, :]),
                  (c.w_node[0][:, HM:2 * HM], a[pre + "msg_w1"][DE:DE + D, :]),
                  (c.w_node[0][:, 0:HM], a[pre + "msg_w1"][DE + D:DE + 2 * D, :]),
                  (b_node[:, 0, 0:HM], row(pre + "msg_b1")),
                  (ag1[:], a[pre + "ag_w1"]), (ag2[:], a[pre + "ag_w2"]), (ag3[:], a[pre + "ag_w3"]),
                  (cols[:, 0:1], col(pre + "msg_b2", 0)), (cols[:, 1:2], col(pre + "msg_b2", 1)),
                  (cols[:, 2:3], col(pre + "msg_b3", 0)), (cols[:, 3:4], col(pre + "ag_b2", 0)),
                  (cols[:, 4:5], col(pre + "up_b2", 0)), (cols[:, 5:6], col(pre + "up_b2", 1)),
                  (c.up_b1[:, 0:1], col(pre + "up_b1", 0)), (c.up_b1[:, 1:2], col(pre + "up_b1", 1)),
                  (rows[:, 0:D], row(pre + "msg_b3")), (rows[:, D:2 * D], row(pre + "up_b3")),
                  (rows[:, 2 * D:3 * D], row(pre + "ag_b1")), (rows[:, 3 * D:3 * D + 1], row(pre + "ag_b3"))]
        for layer in (1, 2):
            for n, x in enumerate("qkvs"):
                LOADS.append((c.w_node[layer][:, n * D:(n + 1) * D], a[f"L1_gnn_W{x}{layer}"]))
                LOADS.append((b_node[:, layer, n * D:(n + 1) * D], row(f"L1_gnn_b{x}{layer}")))
        block = st.block()

        @block.sync
        def _(sp):
            for to, of in LOADS:
                sp.dma_start(to, of).then_inc(s_in, 16)
            sp.wait_ge(s_split, 5)
            for n in range(3):
                sp.dma_start(c.b_parts[n:n + 1, :, :], b_part[:, n, :, :]).then_inc(s_parts, 16)
            sp.wait_ge(s_parts, 48)

        @block.gpsimd
        def _(pool):
            v = nc.gpsimd
            link = linker(pool, s_split)
            pool.wait_ge(s_in, 16 * len(LOADS))
            link(v.memset(b_node[:, 0, HM:2 * HM], 0.0))
            link(v.tensor_copy(b_part[:, 0], b_node[:]))
            link(v.tensor_tensor(b_rest[:], b_node[:], b_part[:, 0], ALU.subtract))
            link(v.tensor_copy(b_part[:, 1], b_rest[:]))
            link(v.tensor_tensor(b_part[:, 2], b_rest[:], b_part[:, 1], ALU.subtract))

        @block.scalar
        def _(act):
            whole = (TILES - 1) * P
            act.dma_start(c.x[:, 0:TILES - 1, :], a["x"][0:whole, :].rearrange("(t p) d -> p t d", p=P)).then_inc(s_x, 16)
            act.wait_ge(s_zero, 1)
            act.dma_start(c.x[0:LAST_ROWS, TILES - 1, :], a["x"][whole:N, :]).then_inc(s_x, 16)
            norm_scalar(act)

        @block.tensor
        def _(pe):
            mm = nc.tensor.matmul
            pe.wait_ge(s_in, 16 * len(LOADS))
            for x, ps in ((w2, pt[0]), (u2, pt[1])):
                for k in range(2):
                    for i in range(2):
                        last = nc.tensor.transpose(ps[:, (k * 2 + i) * P:(k * 2 + i + 1) * P],
                                                   x[:, i, k * P:(k + 1) * P], c.ident[:])
            last = nc.tensor.transpose(pa[:, 0:P], ag2[:], c.ident[:])
            last.then_inc(s_turn, 1)
            pe.wait_ge(s_flat, 3)
            for k in range(2):
                mm(pw[:, 0:HM], w3[:, k, :], w2t[:, k, :], start=(k == 0), stop=(k == 1))
            for i in range(2):
                for k in range(2):
                    mm(pg[:, i * P:(i + 1) * P], w2t[:, k, i * P:(i + 1) * P], w3[:, k, :],
                       start=(k == 0), stop=(k == 1))
            for i in range(2):
                for k in range(2):
                    last = mm(pu[:, i * P:(i + 1) * P], u2t[:, k, i * P:(i + 1) * P], u3[:, k, :],
                              start=(k == 0), stop=(k == 1))
            for k in range(2):
                mm(px[:, 0:1], w3[:, k, :], cols[:, k:k + 1], start=(k == 0), stop=(k == 1))
            mm(px[:, 3 * P:4 * P], ag3_wide[:], ag2t[:], start=True, stop=True)
            mm(px[:, 2:3], agb2[:], ag3[:], start=True, stop=False)
            mm(px[:, 2:3], c.ones[0:1, :], rows[0:1, 3 * D:3 * D + 1], start=False, stop=True)
            for to, b, w, r in ((px[0:1, P:2 * P], 0, w3, 0), (px[0:1, 2 * P:3 * P], 4, u3, D)):
                for k in range(2):
                    mm(to, cols[:, b + k:b + k + 1], w[:, k, :], start=(k == 0), stop=False)
                last = mm(to, c.ones[0:1, 0:1], rows[0:1, r:r + D], start=False, stop=True)
            last.then_inc(s_mm, 1)
            pe.wait_ge(s_mid, 2)
            for i in range(2):
                mm(pa[:, P + i * P:P + (i + 1) * P], w23t[:, i * P:(i + 1) * P], ag1[:], start=True, stop=True)
            mm(pa[0:1, 3 * P:4 * P], cols[:, 6:7], ag1[:], start=True, stop=False)
            mm(pa[0:1, 3 * P:4 * P], c.ones[0:1, 0:1], rows[0:1, 2 * D:3 * D], start=False, stop=True).then_inc(s_g, 1)

        @block.vector
        def _(dve):
            v = nc.vector
            v.memset(c.x[:, TILES - 1, :], 0.0).then_inc(s_zero, 1)
            dve.wait_ge(s_x, 32)
            norm_vector(dve)
            dve.wait_ge(s_in, 16 * len(LOADS))
            v.tensor_copy(ag3_wide[:], ag3[:].to_broadcast([P, P]))
            v.tensor_copy(agb2[:], cols[:, 3:4].to_broadcast([P, P])).then_inc(s_flat, 1)
            dve.wait_ge(s_turn, 1)
            v.tensor_copy(w2t[:].rearrange("p k n -> p (k n)"), pt[0][:])
            v.tensor_copy(ag2t[:], pa[:, 0:P]).then_inc(s_flat, 1)
            v.tensor_copy(u2t[:].rearrange("p k n -> p (k n)"), pt[1][:]).then_inc(s_flat, 1)
            dve.wait_ge(s_mm, 1)
            v.tensor_copy(w23t[:], pw[:, 0:HM]).then_inc(s_mid, 1)
            v.tensor_tensor(cols[:, 6:7], px[:, 0:1], cols[:, 2:3], ALU.add).then_inc(s_mid, 1)
            v.tensor_copy(c.w23[:].rearrange("p k n -> p (k n)"), pg[:, 0:HM])
            v.tensor_copy(c.u23[:].rearrange("p k n -> p (k n)"), pu[:, 0:HM])
            v.tensor_copy(c.gate_w[:], px[:, 3 * P:4 * P])
            v.tensor_copy(c.gate_b[:], px[:, 2:3])
            v.tensor_copy(c.b23[:], px[0:1, P:2 * P])
            v.tensor_copy(c.ub23[:], px[0:1, 2 * P:3 * P])
            dve.wait_ge(s_g, 1)
            v.tensor_copy(c.wg[:].rearrange("p k n -> p (k n)"), pa[:, P:3 * P])
            link = linker(dve, s_gate)
            link(v.tensor_copy(bg[:], pa[0:1, 3 * P:4 * P]))
            link(v.tensor_copy(c.bg_part[:, 0, :], bg[:]))
            link(v.tensor_tensor(bg_rest[:], bg[:], c.bg_part[:, 0, :], ALU.subtract))
            link(v.tensor_copy(c.bg_part[:, 1, :], bg_rest[:]))
            v.tensor_tensor(c.bg_part[:, 2, :], bg_rest[:], c.bg_part[:, 1, :], ALU.subtract)


GROUP = 5
GROUPS = TILES // GROUP
TURN_BANK = (0, 1, 2, 0, 1)
TURN_SINCE = (2, 2, GROUP, 3, 3)


def project(nc, c, name, layer, heads, table_width, scale, table, keep_ht):
    W = c.gather_dram[layer].shape[1]
    keys = 0 if keep_ht else D
    per_head = (HM - keys) // heads
    Q = table_width
    w = c.w_node[layer]
    with Stage(nc, name) as st:
        hs = st.sb("hs", [P, GROUP, D])
        ht = st.sb("ht", [P, GROUP, P])
        kv = st.sb("kv", [P, GROUP, W])
        rest = st.sb("rest", [P, GROUP, Q])
        p_t = [st.ps(f"t{i}", [P, 4 * P]) for i in range(3)]
        p_o = [st.ps(f"o{i}", [P, 4 * P]) for i in range(GROUP)]
        s_hs, s_t, s_ht, s_kept, s_o = (st.sem(n) for n in ("hs", "t", "ht", "kept", "o"))
        s_kv, s_rest, s_mid, s_ones = (st.sem(n) for n in ("kv", "rest", "mid", "ones"))
        s_out = [st.sem(f"out{j}") for j in range(GROUP)]
        block = st.block()

        def one(x, n):
            return x[:, bass.ds(n, 1), :].rearrange("p o d -> p (o d)")

        @block.gpsimd
        def _(pool):
            def body(g):
                for j in range(GROUP):
                    n = g * GROUP + j
                    need(pool, s_t, n - GROUP + 1)
                    nc.gpsimd.tensor_copy(hs[:, j, :], one(c.h, n)).then_inc(s_hs, 1)

            body(0)
            with pool.Fori(1, GROUPS) as g:
                body(g)

        @block.tensor
        def _(pe):
            def turn(g, j):
                n = g * GROUP + j
                pe.wait_ge(s_hs, n + 1)
                need(pe, s_ht, n - TURN_SINCE[j] + 1)
                nc.tensor.transpose(p_t[TURN_BANK[j]][:, 0:P], hs[:, j, :], c.ident[:]).then_inc(s_t, 1)

            def product(g, j):
                n = g * GROUP + j
                pe.wait_ge(s_ht, n + 1)
                need(pe, s_rest, n - GROUP + 1)
                nc.tensor.matmul(p_o[j][:], c.ones_bf[0:3, :], c.b_parts[:, layer, :], start=True, stop=False)
                nc.tensor.matmul(p_o[j][:], ht[:, j, :], w[:], start=False, stop=True).then_inc(s_o, 1)

            def body(g):
                for j in range(GROUP):
                    product(g, j)
                    turn(g + 1, j)

            for j in range(GROUP):
                turn(0, j)
            body(0)
            with pe.Fori(1, GROUPS - 1) as g:
                body(g)
            for j in range(GROUP):
                product(GROUPS - 1, j)

        @block.scalar
        def _(act):
            def keep(g, j):
                n = g * GROUP + j
                act.wait_ge(s_t, n + 1)
                need(act, s_o, n - GROUP + 1)
                if keep_ht:
                    need(act, s_kept, n - GROUP + 1)
                nc.scalar.copy(ht[:, j, :], p_t[TURN_BANK[j]][:, 0:P]).then_inc(s_ht, 1)

            def take(g, j):
                n = g * GROUP + j
                act.wait_ge(s_o, n + 1)
                nc.scalar.activation(table[:, bass.ds(n, 1), 0, :].rearrange("p o d -> p (o d)"),
                                     p_o[j][:, 0:Q], ACT.Copy, scale=scale)
                need(act, s_out[j], 16 * g)
                if keys:
                    nc.scalar.copy(kv[:, j, 0:keys], p_o[j][:, Q:Q + keys])
                nc.scalar.copy(kv[:, j, keys:W].rearrange("p (h f) -> p h f", h=heads)[:, :, 0:per_head],
                               p_o[j][:, Q + keys:Q + HM].rearrange("p (h f) -> p h f", h=heads)).then_inc(s_kv, 1)

            def body(g):
                for j in range(GROUP):
                    take(g, j)
                    keep(g + 1, j)

            act.wait_ge(s_ones, 1)
            for j in range(GROUP):
                keep(0, j)
            body(0)
            with act.Fori(1, GROUPS - 1) as g:
                body(g)
            for j in range(GROUP):
                take(GROUPS - 1, j)

        @block.vector
        def _(dve):
            v = nc.vector
            v.memset(kv[:], 1.0).then_inc(s_ones, 1)

            def body(g):
                for j in range(GROUP):
                    n = g * GROUP + j
                    parts = [table[:, bass.ds(n, 1), s, :].rearrange("p o d -> p (o d)") for s in range(3)]
                    if keep_ht:
                        dve.wait_ge(s_ht, n + 1)
                        v.tensor_copy(one(c.ht, n), ht[:, j, :]).then_inc(s_kept, 1)
                    dve.wait_ge(s_kv, n + 1)
                    if 4 * P > Q + HM:
                        v.tensor_copy(one(c.skip, n), p_o[j][:, Q + HM:4 * P])
                    v.scalar_tensor_tensor(rest[:, j, :], p_o[j][:, 0:Q], scale, parts[0],
                                           ALU.mult, ALU.subtract).then_inc(s_rest, 1)
                    dve.wait_ge(s_rest, n + 1)
                    v.tensor_copy(parts[1], rest[:, j, :]).then_inc(s_mid, 1)
                    dve.wait_ge(s_mid, n + 1)
                    v.tensor_tensor(parts[2], rest[:, j, :], parts[1], ALU.subtract)

            body(0)
            with dve.Fori(1, GROUPS) as g:
                body(g)

        @block.sync
        def _(sp):
            rows = c.gather_dram[layer].rearrange("(n p) d -> n p d", p=P)

            def body(g):
                for j in range(GROUP):
                    n = g * GROUP + j
                    sp.wait_ge(s_kv, n + 1)
                    sp.dma_start(rows[bass.ds(n, 1)].rearrange("o p d -> (o p) d"), kv[:, j, :]).then_inc(s_out[j], 16)

            body(0)
            with sp.Fori(1, GROUPS) as g:
                body(g)
            for j in range(GROUP):
                sp.wait_ge(s_out[j], 16 * GROUPS)


def need(eng, sem, value):
    if not isinstance(value, int) or value > 0:
        eng.wait_ge(sem, value)


def skewed(eng, stages, depth):
    peeled = 1 + -(-depth // PAIRS)
    def run(it, k):
        for lag, stage in stages:
            if isinstance(it, int) and not 0 <= it * PAIRS + k - lag < ITERS * PAIRS:
                continue
            back, pair = divmod(k - lag, PAIRS)
            stage(it + back, pair)

    for it in range(peeled):
        for k in range(PAIRS):
            run(it, k)
    with eng.Fori(peeled, ITERS) as it:
        for k in range(PAIRS):
            run(it, k)
    for n in range(depth):
        run(ITERS + n // PAIRS, n % PAIRS)


def load_four(nc, engine, table, step, top):
    values = nc.values_load_multi_w_load_instructions(
        table[0:1, bass.ds(step, 4)], engines=[engine], min_val=0, max_val=top,
        skip_runtime_bounds_check_because="plan_and_stack computes tiles and chunks inside their ranges for any edges")[1]
    return values


def edge_scores(nc, c, name, layer, heads, messages, table):
    Q = HM if messages else D
    W = c.gather_dram[layer].shape[1]
    keys = 0 if messages else D
    F = W - keys
    with Stage(nc, name) as st:
        got = st.sb("got", [P, PAIRS, 2, W])
        local = st.sb("local", [P, PAIRS // 2, 4 * P], BF16)
        hot = st.sb("hot", [P, PAIRS, 2 * P], BF16)
        index = st.sb("index", [P, PAIRS // 2, 4], I32)
        prod = st.sb("prod", [P, 2, 2, D])
        attr = st.sb("attr", [P, PAIRS, 2, STACK], BF16)
        attr_t = st.sb("attr_t", [STACK, PAIRS, 2 * P], BF16)
        hid_t = st.sb("hid_t", [P, 2, 2, 2 * P])
        gated = st.sb("gated", [P, 2, 2, D])
        p_dst = [st.ps(f"dst{i}", [P, 2 * HM]) for i in range(2)]
        p_hid = [st.ps(f"hid{i}", [P, 4 * P]) for i in range(2)]
        p_gate = [st.ps(f"gate{i}", [P, 4 * P]) for i in range(2)]
        p_attr = st.ps("attr_ps", [STACK, 4 * P], BF16)
        s_got = [st.sem(f"got{k}") for k in range(PAIRS)]
        s_local = [st.sem(f"local{k}") for k in range(PAIRS // 2)]
        s_attr = [st.sem(f"attr{k}") for k in range(PAIRS)]
        s_stored = [st.sem(f"stored{k}") for k in range(PAIRS)]
        s_index, s_hot, s_dst, s_sum, s_clear = (st.sem(n) for n in ("index", "hot", "dst", "sum", "clear"))
        s_aturn, s_attr_t, s_hturn, s_hid_t = (st.sem(n) for n in ("aturn", "attr_t", "hturn", "hid_t"))
        s_gmm, s_score = st.sem("gmm"), st.sem("score")
        block = st.block()
        payload = c.payload_dram[0:STEPS * P * F].rearrange("(q p f) -> q p f", p=P, f=2 * F)
        table_flat = table[:].rearrange("p t s q -> p (t s q)")
        local_rows = c.local_dram.rearrange("(q s) -> q s", s=4 * P)

        def store(eng, it, k):
            q = it * PAIRS + k
            if messages:
                eng.wait_ge(s_sum, q + 1)
                of = got[:, k, :, :].rearrange("p j f -> p (j f)")
                eng.dma_start(payload[bass.ds(q, 1), :, :].rearrange("o p f -> (o p) f"), of).then_inc(s_stored[k], 16)
            else:
                eng.wait_ge(s_got[k], 32 * it + 32)
                eng.dma_start(payload[bass.ds(q, 1), :, :].rearrange("o p (j f) -> (o p) j f", j=2),
                              got[:, k, :, keys:W]).then_inc(s_stored[k], 16)

        @block.sync
        def _(sp):
            sp_chunk = []

            def load(it, k):
                q = it * PAIRS + k
                if messages and k % 2 == 0:
                    sp_chunk[:] = load_four(nc, SP, c.chunk_at, 2 * q, CHUNKS * P * STACK)
                if k % 2 == 0:
                    need(sp, s_hot, q - PAIRS + 2)
                    if messages:
                        need(sp, s_aturn, q - PAIRS + 2)
                    half = it * (PAIRS // 2) + k // 2
                    sp.dma_start(local[:, k // 2, :], local_rows[bass.ds(half, 1), :].to_broadcast([P, 4 * P])
                                 ).then_inc(s_local[k // 2], 16)
                if messages:
                    for j in range(2):
                        of = c.attr_dram[bass.ds(sp_chunk[k % 2 * 2 + j], P * STACK)]
                        sp.dma_start(attr[:, k, j, :], of.rearrange("(p d) -> p d", p=P)).then_inc(s_attr[k], 16)

            if messages:
                skewed(sp, [(0, load)], 0)
            else:
                skewed(sp, [(0, load), (3, lambda it, k: store(sp, it, k))], 3)
            for k in range(PAIRS):
                sp.wait_ge(s_stored[k], 16 * ITERS)

        @block.gpsimd
        def _(pool):
            def gather(it, k):
                q = it * PAIRS + k
                if k % 2 == 0:
                    pool.wait_ge(s_index, PAIRS // 2 * it + k // 2 + 1)
                need(pool, s_stored[k], 16 * it)
                need(pool, s_hturn if messages else s_sum, q - PAIRS + 1)
                pool.sem_inc(s_clear, 1)
                for j in range(2):
                    nc.gpsimd.indirect_dma_start(
                        got[:, k, j, :], None, c.gather_dram[layer][:, :],
                        bass.IndirectOffsetOnAxis(ap=index[:, k // 2, k % 2 * 2 + j:k % 2 * 2 + j + 1], axis=0),
                    ).then_inc(s_got[k], 16)

            skewed(pool, [(0, gather)], 0)

        @block.tensor
        def _(pe):
            pe_tile = []

            def turn_attr(it, k):
                q = it * PAIRS + k
                pe.wait_ge(s_attr[k], 32 * it + 32)
                need(pe, s_attr_t, q)
                for j in range(2):
                    last = nc.tensor.transpose(p_attr[:, j * P:(j + 1) * P], attr[:, k, j, :], c.ident_bf[:])
                last.then_inc(s_aturn, 1)

            def pick(it, k):
                q, s = it * PAIRS + k, k % 2
                if k % 2 == 0:
                    pe_tile[:] = load_four(nc, PE, c.tile_at[3 * Q], 2 * q, (TILES - 1) * 3 * Q)
                pe.wait_ge(s_hot, q + 1)
                need(pe, s_sum, q - 1)
                if messages:
                    pe.wait_ge(s_attr_t, q + 1)
                for j in range(2):
                    to = p_dst[s][:, j * Q:(j + 1) * Q]
                    parts = table_flat[:, bass.ds(pe_tile[k % 2 * 2 + j], 3 * Q)]
                    if messages:
                        nc.tensor.matmul(to, attr_t[:, k, j * P:(j + 1) * P], c.w_stack[:], start=True, stop=False)
                    for part in range(3):
                        last = nc.tensor.matmul(to, hot[:, k, j * P:(j + 1) * P],
                                                parts[:, part * Q:(part + 1) * Q],
                                                start=(part == 0 and not messages), stop=(part == 2))
                last.then_inc(s_dst, 1)

            def turn_hidden(it, k):
                q, s = it * PAIRS + k, k % 2
                pe.wait_ge(s_sum, q + 1)
                need(pe, s_hid_t, q - 1)
                for f in range(2):
                    for j in range(2):
                        last = nc.tensor.transpose(p_hid[s][:, (f * 2 + j) * P:(f * 2 + j + 1) * P],
                                                   got[:, k, j, f * P:(f + 1) * P], c.ident[:])
                last.then_inc(s_hturn, 1)

            def gate_hidden(it, k):
                q, s = it * PAIRS + k, k % 2
                pe.wait_ge(s_hid_t, q + 1)
                need(pe, s_score, q - 1)
                for j in range(2):
                    to = p_gate[s][:, j * P:(j + 1) * P]
                    nc.tensor.matmul(to, c.ones_bf[0:3, :], c.bg_parts[:], start=True, stop=False)
                    for f in range(2):
                        last = nc.tensor.matmul(to, hid_t[:, s, f, j * P:(j + 1) * P], c.wg[:, f, :],
                                                start=False, stop=(f == 1))
                last.then_inc(s_gmm, 1)

            if messages:
                skewed(pe, [(4, gate_hidden), (3, turn_hidden), (2, pick), (0, turn_attr)], 4)
            else:
                skewed(pe, [(0, pick)], 0)

        if messages:
            @block.scalar
            def _(act):
                def keep_attr(it, k):
                    q = it * PAIRS + k
                    act.wait_ge(s_aturn, q + 1)
                    need(act, s_dst, q - PAIRS + 1)
                    nc.scalar.copy(attr_t[:, k, :], p_attr[:, 0:2 * P]).then_inc(s_attr_t, 1)

                def relu_hidden(it, k):
                    q, s = it * PAIRS + k, k % 2
                    act.wait_ge(s_hturn, q + 1)
                    need(act, s_gmm, q - 1)
                    nc.scalar.activation(hid_t[:, s, :, :].rearrange("p f e -> p (f e)"), p_hid[s][:],
                                         ACT.Relu).then_inc(s_hid_t, 1)

                skewed(act, [(3, relu_hidden), (3, lambda it, k: store(act, it, k)), (0, keep_attr)], 3)

        @block.vector
        def _(dve):
            v = nc.vector

            def indices(half, step):
                v.tensor_copy(index[:, half, :], c.src_slot[:, bass.ds(step, 4)]).then_inc(s_index, 1)

            def one_hot(it, k):
                q = it * PAIRS + k
                dve.wait_ge(s_local[k // 2], 16 * it + 16)
                need(dve, s_dst, q - PAIRS + 1)
                mine = local[:, k // 2, k % 2 * 2 * P:(k % 2 + 1) * 2 * P]
                v.tensor_scalar(hot[:, k, :], mine, c.part_col[:, 0:1], None, ALU.is_equal).then_inc(s_hot, 1)

            def combine(it, k):
                q, s = it * PAIRS + k, k % 2
                dve.wait_ge(s_dst, q + 1)
                dve.wait_ge(s_got[k], 32 * it + 32)
                ps = p_dst[s][:, 0:2 * Q].rearrange("p (j f) -> p j f", j=2)
                if messages:
                    v.tensor_tensor(got[:, k, :, 0:Q], ps, got[:, k, :, 0:Q], ALU.add).then_inc(s_sum, 1)
                else:
                    need(dve, s_score, q - 1)
                    v.tensor_tensor(prod[:, s, :, :], ps, got[:, k, :, 0:D], ALU.mult).then_inc(s_sum, 1)
                if k % 2 == 1:
                    indices(k // 2, it * UNROLL + UNROLL + k // 2 * 4)

            def score(it, k):
                q, s = it * PAIRS + k, k % 2
                to = c.score[:, bass.ds(q * 2 * heads, 2 * heads)]
                if messages:
                    dve.wait_ge(s_gmm, q + 1)
                    need(dve, s_score, q - 1)
                    for j in range(2):
                        ins = v.scalar_tensor_tensor(gated[:, s, j, :], p_gate[s][:, j * P:(j + 1) * P], 0.0,
                                                     c.gate_w[:], ALU.max, ALU.mult,
                                                     accum_out=c.score[:, bass.ds(q * 2 + j, 1)])
                    ins.then_inc(s_score, 1)
                else:
                    dve.wait_ge(s_sum, q + 1)
                    v.tensor_reduce(to, prod[:, s, :, :].rearrange("p j (h f) -> p (j h) f", h=heads),
                                    AX.X, ALU.add).then_inc(s_score, 1)

            for half in range(PAIRS // 2):
                indices(half, half * 4)
            if messages:
                skewed(dve, [(5, score), (0, one_hot), (2, combine)], 5)
                dve.wait_ge(s_score, ITERS * PAIRS)
                v.tensor_scalar(c.score[:, 0:STEPS], c.score[:, 0:STEPS], c.gate_b[:], None, ALU.add)
            else:
                skewed(dve, [(0, one_hot), (1, combine), (2, score)], 2)


def softmax_weights(nc, c, name, heads):
    H, L = heads, 4 * P
    with Stage(nc, name) as st:
        score = st.sb("score", [ROWS, H, L])
        run = st.sb("run", [ROWS, H, L])
        top = st.sb("top", [ROWS, H, L])
        edge = st.sb("edge", [ROWS, H])
        edge_t = st.sb("edge_t", [H, ROWS])
        carry = st.sb("carry", [H, ROWS + 1])
        carry_t = st.sb("carry_t", [ROWS, H])
        back = st.sb("back", [H, ROWS + 1])
        back_t = st.sb("back_t", [ROWS, H])
        p_in = [st.ps(f"in{i}", [P, L]) for i in range(2)]
        p_out = [st.ps(f"out{i}", [P, L]) for i in range(2)]
        p_e = st.ps("e", [P, 4 * P])
        s_in, s_row, s_dve, s_edge, s_edge_t = (st.sem(n) for n in ("in", "row", "dve_chain", "edge_s", "edge_ts"))
        s_carry, s_carry_t, s_shift, s_exp, s_turn, s_back = (
            st.sem(n) for n in ("carry_s", "carry_ts", "shift", "exp", "turn", "back_s"))
        block = st.block()
        by_row = c.score[:, 0:STEPS * H].rearrange("p (r a h) -> p a h r", a=4, h=H)

        @block.tensor
        def _(pe):
            for h in range(H):
                need(pe, s_row, h - 1)
                for a in range(4):
                    last = nc.tensor.transpose(p_in[h % 2][0:ROWS, a * P:(a + 1) * P], by_row[:, a, h, :], c.ident[:])
                last.then_inc(s_in, 1)
            for n in range(2):
                pe.wait_ge(s_edge, n + 1)
                nc.tensor.transpose(p_e[0:H, 0:ROWS], edge[:], c.ident[0:ROWS, 0:ROWS]).then_inc(s_edge_t, 1)
                pe.wait_ge(s_carry, n + 1)
                carried = carry[:, 0:ROWS] if n == 0 else back[:, 1:ROWS + 1]
                nc.tensor.transpose(p_e[0:ROWS, 0:H], carried, c.ident[0:H, 0:H]).then_inc(s_carry_t, 1)
            for h in range(H):
                pe.wait_ge(s_exp, h + 1)
                need(pe, s_back, h - 1)
                for a in range(4):
                    last = nc.tensor.transpose(p_out[h % 2][:, a * ROWS:(a + 1) * ROWS], score[:, h, a * P:(a + 1) * P],
                                               c.ident[0:ROWS, 0:ROWS])
                last.then_inc(s_turn, 1)

        @block.scalar
        def _(act):
            for h in range(H):
                act.wait_ge(s_in, h + 1)
                nc.scalar.copy(score[:, h, :], p_in[h % 2][0:ROWS, :]).then_inc(s_row, 1)
            for h in range(H):
                act.wait_ge(s_shift, h + 1)
                nc.scalar.activation(score[:, h, :], score[:, h, :], ACT.Exp).then_inc(s_exp, 1)

        @block.vector
        def _(dve):
            v = nc.vector
            link = linker(dve, s_dve)
            scan = v.tensor_tensor_scan
            rev = slice(None, None, -1)
            for n in range(2):
                for h in range(H):
                    if n == 0:
                        dve.wait_ge(s_row, h + 1)
                    ins = scan(run[:, h, :], c.start_big[:], score[:, h, :],
                               -BIG if n == 0 else carry_t[:, h:h + 1], ALU.add, ALU.max)
                link(ins)
                if n == 0:
                    v.memset(carry[:, 0:1], -BIG)
                    v.tensor_copy(edge[:], run[:, :, L - 1]).then_inc(s_edge, 1)
                    dve.wait_ge(s_edge_t, 1)
                    link(v.tensor_copy(edge_t[:], p_e[0:H, 0:ROWS]))
                    scan(carry[:, 1:ROWS + 1], c.row_start[0:H, :], edge_t[:], -BIG, ALU.add,
                         ALU.max).then_inc(s_carry, 1)
                    dve.wait_ge(s_carry_t, 1)
                    link(v.tensor_copy(carry_t[:], p_e[0:ROWS, 0:H]))
            link(v.tensor_tensor(run[:], run[:], c.last[:].unsqueeze(1).to_broadcast([ROWS, H, L]), ALU.mult))
            for n in range(2):
                for h in range(H):
                    ins = scan(top[:, h, rev], c.not_last[:, rev], run[:, h, rev],
                               0.0 if n == 0 else back_t[:, h:h + 1], ALU.mult, ALU.add)
                link(ins)
                if n == 0:
                    v.memset(back[:, ROWS:ROWS + 1], 0.0)
                    v.tensor_copy(edge[:], top[:, :, 0]).then_inc(s_edge, 1)
                    dve.wait_ge(s_edge_t, 2)
                    link(v.tensor_copy(edge_t[:], p_e[0:H, 0:ROWS]))
                    scan(back[:, slice(ROWS - 1, None, -1)], c.row_open[0:H, rev], edge_t[:, rev], 0.0, ALU.mult,
                         ALU.add).then_inc(s_carry, 1)
                    dve.wait_ge(s_carry_t, 2)
                    link(v.tensor_copy(back_t[:], p_e[0:ROWS, 0:H]))
            for h in range(H):
                v.tensor_tensor(score[:, h, :], score[:, h, :], top[:, h, :], ALU.subtract).then_inc(s_shift, 1)
            for h in range(H):
                dve.wait_ge(s_turn, h + 1)
                v.tensor_copy(by_row[:, :, h, :], p_out[h % 2][:, 0:4 * ROWS].rearrange("p (a r) -> p a r", a=4)
                              ).then_inc(s_back, 1)


def aggregate(nc, c, name, heads, messages):
    H = heads
    F = value_width(H, HM if messages else D)
    with Stage(nc, name) as st:
        pay = st.sb("pay", [P, PAIRS, 2, F])
        hot = st.sb("hot", [P, PAIRS, 2, P])
        sum_odd = st.sb("sum_odd", [P, TILES * F])
        sums = (c.sum[:].rearrange("p t f -> p (t f)"), sum_odd[:])
        p_sum = [st.ps(f"sum{i}", [P, 4 * P]) for i in range(BANKS)]
        s_pay = [st.sem(f"pay{k}") for k in range(PAIRS)]
        s_hot, s_weighted, s_mm, s_zero = (st.sem(n) for n in ("hot", "weighted", "mm", "zero"))
        s_sum = (st.sem("sum_even"), st.sem("sum_odd"))
        block = st.block()
        payload = c.payload_dram[0:STEPS * P * F].rearrange("(q p f) -> q p f", p=P, f=2 * F)

        @block.sync
        def _(sp):
            def load(it, k):
                q = it * PAIRS + k
                need(sp, s_mm, q - PAIRS + 1)
                sp.dma_start(pay[:, k, :, :].rearrange("p j f -> p (j f)"),
                             payload[bass.ds(q, 1), :, :].rearrange("o p f -> (o p) f")).then_inc(s_pay[k], 16)
            skewed(sp, [(0, load)], 0)

        if H == 1:
            @block.scalar
            def _(act):
                def weigh(it, k):
                    q = it * PAIRS + k
                    act.wait_ge(s_pay[k], 16 * it + 16)
                    for j in range(2):
                        ins = nc.scalar.activation(pay[:, k, j, :], pay[:, k, j, :], ACT.Relu if messages else ACT.Copy,
                                                   scale=c.score[:, bass.ds(2 * q + j, 1)])
                    ins.then_inc(s_weighted, 1)
                skewed(act, [(0, weigh)], 0)
        else:
            @block.gpsimd
            def _(pool):
                def weigh(it, k):
                    q = it * PAIRS + k
                    pool.wait_ge(s_pay[k], 16 * it + 16)
                    of = pay[:, k, :, :].rearrange("p j (h f) -> p (j h) f", h=H)
                    nc.gpsimd.tensor_tensor(of, of, c.score[:, bass.ds(2 * q * H, 2 * H)].unsqueeze(2)
                                            .to_broadcast([P, 2 * H, F // H]), ALU.mult).then_inc(s_weighted, 1)
                skewed(pool, [(0, weigh)], 0)

        @block.tensor
        def _(pe):
            def matmul(it, k):
                q = it * PAIRS + k
                pe.wait_ge(s_hot, q + 1)
                pe.wait_ge(s_weighted, q + 1)
                for j in range(2):
                    need(pe, s_sum[j], q - BANKS // 2 + 1)
                for j in range(2):
                    last = nc.tensor.matmul(p_sum[(2 * k + j) % BANKS][:, 0:F], hot[:, k, j, :], pay[:, k, j, :],
                                            start=True, stop=True)
                last.then_inc(s_mm, 1)
            skewed(pe, [(0, matmul)], 0)

        @block.vector
        def _(dve):
            for x in (c.sum, sum_odd):
                nc.vector.memset(x[:], 0.0).then_inc(s_zero, 1)
            dve.wait_ge(s_zero, 2)
            tile = []

            def one_hot(it, k):
                q = it * PAIRS + k
                if k % 2 == 0:
                    need(dve, s_mm, q - PAIRS + 2)
                    nc.vector.tensor_tensor(hot[:, k:k + 2, :, :].rearrange("p k j n -> p (k j) n"),
                                            c.node_row[:].unsqueeze(1).to_broadcast([P, 4, P]),
                                            c.local[:, bass.ds(2 * q, 4)].unsqueeze(2).to_broadcast([P, 4, P]),
                                            ALU.is_equal).then_inc(s_hot, 2)

            def accumulate(it, k):
                q = it * PAIRS + k
                if k % 2 == 0:
                    tile[:] = load_four(nc, DVE, c.tile_at[F], 2 * q, (TILES - 1) * F)
                dve.wait_ge(s_mm, q + 1)
                for j in range(2):
                    need(dve, s_sum[j], q)
                    to = sums[j][:, bass.ds(tile[k % 2 * 2 + j], F)]
                    nc.vector.tensor_tensor(to, to, p_sum[(2 * k + j) % BANKS][:, 0:F], ALU.add).then_inc(s_sum[j], 1)

            skewed(dve, [(0, one_hot), (2, accumulate)], 2)
            for j in range(2):
                dve.wait_ge(s_sum[j], ITERS * PAIRS)
            nc.vector.tensor_tensor(sums[0], sums[0], sums[1], ALU.add)


def update_nodes(nc, c):
    with Stage(nc, "update") as st:
        inv = st.sb("inv", [P, TILES])
        mean = st.sb("mean", [P, GROUP, HM + 1])
        mean_t = st.sb("mean_t", [P, GROUP, 3 * P])
        agg_t = st.sb("agg_t", [P, GROUP, P])
        hid_t = st.sb("hid_t", [P, GROUP, 2 * P])
        bank = [st.ps(f"bank{j}", [P, 4 * P]) for j in range(GROUP)]
        p_turn = [st.ps(f"turned{i}", [P, 4 * P]) for i in range(3)]
        s_inv, s_mean, s_turn, s_mean_t, s_agg = (st.sem(n) for n in ("inv_s", "mean_s", "turn", "mean_ts", "agg"))
        s_agg_t, s_hid, s_hid_t, s_out, s_done = (st.sem(n) for n in ("agg_ts", "hid", "hid_ts", "out", "done"))
        block = st.block()

        @block.tensor
        def _(pe):
            mm = nc.tensor.matmul

            def turn(g, j):
                n = g * GROUP + j
                to = p_turn[TURN_BANK[j]]
                pe.wait_ge(s_mean, n + 1)
                need(pe, s_mean_t, n - TURN_SINCE[j] + 1)
                for f in range(2):
                    nc.tensor.transpose(to[:, f * P:(f + 1) * P], mean[:, j, f * P:(f + 1) * P], c.ident[:])
                nc.tensor.transpose(to[0:1, 2 * P:3 * P], mean[:, j, HM:HM + 1], c.ident[:]).then_inc(s_turn, 1)

            def body(g, more=True):
                n = g * GROUP
                for j in range(GROUP):
                    pe.wait_ge(s_mean_t, n + j + 1)
                    need(pe, s_done, n + j - GROUP + 1)
                    to = bank[j][:, 0:P]
                    for f in range(2):
                        mm(to, c.w23[:, f, :], mean_t[:, j, f * P:(f + 1) * P], start=(f == 0), stop=False)
                    mm(to, c.b23[:], mean_t[0:1, j, 2 * P:3 * P], start=False, stop=True).then_inc(s_agg, 1)
                for j in range(GROUP):
                    pe.wait_ge(s_agg_t, n + j + 1)
                    for f in range(2):
                        to = bank[j][:, f * P:(f + 1) * P]
                        mm(to, c.up1[:, 0, f * P:(f + 1) * P],
                           c.ht[:, bass.ds(n + j, 1), :].rearrange("p o n -> p (o n)"), start=True, stop=False)
                        last = mm(to, c.up1[:, 1, f * P:(f + 1) * P], agg_t[:, j, :], start=False, stop=True)
                    last.then_inc(s_hid, 1)
                for j in range(GROUP):
                    pe.wait_ge(s_hid_t, n + j + 1)
                    to = bank[j][:, 0:P]
                    for f in range(2):
                        mm(to, hid_t[:, j, f * P:(f + 1) * P], c.u23[:, f, :], start=(f == 0), stop=False)
                    mm(to, c.ones[0:1, :], c.ub23[:], start=False, stop=True).then_inc(s_out, 1)
                    if more:
                        turn(g + 1, j)

            for j in range(GROUP):
                turn(0, j)
            body(0)
            with pe.Fori(1, GROUPS - 1) as g:
                body(g)
            body(GROUPS - 1, more=False)

        @block.scalar
        def _(act):
            def keep(g, j):
                n = g * GROUP + j
                of = p_turn[TURN_BANK[j]]
                act.wait_ge(s_turn, n + 1)
                need(act, s_agg, n - GROUP + 1)
                nc.scalar.copy(mean_t[:, j, 0:2 * P], of[:, 0:2 * P])
                nc.scalar.copy(mean_t[0:1, j, 2 * P:3 * P], of[0:1, 2 * P:3 * P]).then_inc(s_mean_t, 1)

            def body(g, more=True):
                n = g * GROUP
                for j in range(GROUP):
                    act.wait_ge(s_hid, n + j + 1)
                    need(act, s_out, n + j - GROUP + 1)
                    for f in range(2):
                        ins = nc.scalar.activation(hid_t[:, j, f * P:(f + 1) * P], bank[j][:, f * P:(f + 1) * P],
                                                   ACT.Relu, bias=c.up_b1[:, f:f + 1])
                    ins.then_inc(s_hid_t, 1)
                if more:
                    for j in range(GROUP):
                        keep(g + 1, j)

            for j in range(GROUP):
                keep(0, j)
            body(0)
            with act.Fori(1, GROUPS - 1) as g:
                body(g)
            body(GROUPS - 1, more=False)

        @block.gpsimd
        def _(pool):
            pool.wait_ge(s_inv, 2)

            def body(g):
                for j in range(GROUP):
                    n = g * GROUP + j
                    need(pool, s_turn, n - GROUP + 1)
                    nc.gpsimd.tensor_tensor(mean[:, j, :], c.sum[:, bass.ds(n, 1), 0:HM + 1].rearrange("p o f -> p (o f)"),
                                            inv[:, bass.ds(n, 1)].to_broadcast([P, HM + 1]),
                                            ALU.mult).then_inc(s_mean, 1)

            body(0)
            with pool.Fori(1, GROUPS) as g:
                body(g)

        @block.vector
        def _(dve):
            v = nc.vector
            v.tensor_scalar(inv[:], c.sum[:, :, HM], ATTN_EPS, None, ALU.add).then_inc(s_inv, 1)
            dve.wait_ge(s_inv, 1)
            v.reciprocal(inv[:], inv[:]).then_inc(s_inv, 1)

            def body(g):
                n = g * GROUP
                for j in range(GROUP):
                    dve.wait_ge(s_agg, n + j + 1)
                    need(dve, s_hid, n + j - GROUP + 1)
                    v.tensor_copy(agg_t[:, j, :], bank[j][:, 0:P]).then_inc(s_agg_t, 1)
                for j in range(GROUP):
                    dve.wait_ge(s_out, n + j + 1)
                    to = c.x[:, bass.ds(n + j, 1), :].rearrange("p o d -> p (o d)")
                    v.tensor_tensor(to, to, bank[j][:, 0:P], ALU.add).then_inc(s_done, 1)

            body(0)
            with dve.Fori(1, GROUPS) as g:
                body(g)


def combine_heads(nc, c, name, heads, out):
    H = heads
    with Stage(nc, name) as st:
        inv = st.sb("inv", [P, TILES, H])
        s_chain, s_done, s_out = st.sem("chain"), st.sem("done"), st.sem("out")
        block = st.block()

        @block.vector
        def _(dve):
            v = nc.vector
            link = linker(dve, s_chain)
            sums = c.sum[:].rearrange("p t (h f) -> p t h f", h=H)
            link(v.tensor_scalar(inv[:], sums[:, :, :, D // H], ATTN_EPS, None, ALU.add))
            link(v.reciprocal(inv[:], inv[:]))
            link(v.tensor_tensor(c.h[:].rearrange("p t (h f) -> p t h f", h=H), sums[:, :, :, 0:D // H],
                                 inv[:].unsqueeze(3).to_broadcast([P, TILES, H, D // H]), ALU.mult))
            link(v.tensor_tensor(c.h[:], c.h[:], c.skip[:], ALU.add))
            if out is not None:
                v.tensor_tensor(c.h[:], c.h[:], c.x[:], ALU.add).then_inc(s_done, 1)

        if out is not None:
            @block.sync
            def _(sp):
                sp.wait_ge(s_done, 1)
                sp.dma_start(out[0:(TILES - 1) * P, :].rearrange("(t p) d -> p t d", p=P),
                             c.h[:, 0:TILES - 1, :]).then_inc(s_out, 16)
                sp.dma_start(out[(TILES - 1) * P:N, :], c.h[0:LAST_ROWS, TILES - 1, :]).then_inc(s_out, 16)
                sp.wait_ge(s_out, 32)


def stack_attributes(nc, c, st, attr):
    ROWS_IN = P - 3
    EDGES = E // ROWS_IN // STACK_BLOCKS
    x = st.sb("x", [ROWS_IN, STACK_BLOCKS, EDGES, DE])
    rest = st.sb("rest", [ROWS_IN, 2, EDGES, DE])
    parts = st.sb("parts", [ROWS_IN, 2, EDGES, STACK], BF16)
    zeros = st.sb("zeros", [P, 2 * STACK], BF16)
    w_rest = st.sb("w_rest", [DE, HM])
    w_part = st.sb("w_part", [DE, 3, HM], BF16)
    s_out = [st.sem(f"out{i}") for i in range(2)]
    s_x = [st.sem(f"x{n}") for n in range(STACK_BLOCKS)]
    s_hi, s_rest, s_mid, s_low, s_copy, s_w, s_wout, s_zero, s_tail = (
        st.sem(n) for n in ("hi", "rest_s", "mid", "low", "copy", "w", "wout", "zero", "tail"))
    rows = c.attr_dram[0:E * STACK].rearrange("(p b e d) -> b p e d", b=STACK_BLOCKS, e=EDGES, d=STACK)
    behind = (CHUNKS + 1) * P - E

    def part(i, n):
        return parts[:, i, :, n * DE:(n + 1) * DE]

    def load(sp, attr):
        for n in range(STACK_BLOCKS):
            sp.dma_start(x[:, n, :, :], attr.rearrange("(p b e) d -> b p e d", b=STACK_BLOCKS, e=EDGES)[n]
                         ).then_inc(s_x[n], 16)

    def weights(sp):
        sp.wait_ge(s_w, 4)
        for n, of in enumerate((0, 1, 2, 0, 1, 0)):
            sp.dma_start(c.w_stack[n * DE:(n + 1) * DE, :], w_part[:, of, :]).then_inc(s_wout, 16)
        sp.wait_ge(s_wout, 16 * PARTS)

    def pool(pool):
        link = linker(pool, s_w)
        v = nc.gpsimd
        v.memset(zeros[:], 0.0).then_inc(s_zero, 1)
        link(v.tensor_copy(w_part[:, 0, :], c.w_edge[:]))
        link(v.tensor_tensor(w_rest[:], c.w_edge[:], w_part[:, 0, :], ALU.subtract))
        link(v.tensor_copy(w_part[:, 1, :], w_rest[:]))
        link(v.tensor_tensor(w_part[:, 2, :], w_rest[:], w_part[:, 1, :], ALU.subtract))
        for n in range(STACK_BLOCKS):
            i = n % 2
            pool.wait_ge(s_hi, n + 1)
            v.tensor_tensor(rest[:, i], x[:, n], part(i, 0), ALU.subtract).then_inc(s_rest, 1)
            pool.wait_ge(s_mid, n + 1)
            v.tensor_tensor(part(i, 5), rest[:, i], part(i, 3), ALU.subtract).then_inc(s_low, 1)

    def act(act):
        act.wait_ge(s_zero, 1)
        half = behind * STACK // (2 * STACK)
        act.dma_start(c.attr_dram[E * STACK:(E + behind) * STACK].rearrange("(p d) -> p d", d=2 * STACK),
                      zeros[0:half, :]).then_inc(s_tail, 16)
        for n in range(STACK_BLOCKS):
            i = n % 2
            act.wait_ge(s_x[n], 16)
            need(act, s_out[i], 16 * (n // 2))
            nc.scalar.copy(part(i, 0), x[:, n]).then_inc(s_hi, 1)
            nc.scalar.copy(part(i, 1), x[:, n])
            nc.scalar.copy(part(i, 2), x[:, n])
            act.wait_ge(s_rest, n + 1)
            nc.scalar.copy(part(i, 3), rest[:, i]).then_inc(s_mid, 1)
            nc.scalar.copy(part(i, 4), rest[:, i]).then_inc(s_copy, 1)
            act.wait_ge(s_copy, n + 1)
            act.wait_ge(s_low, n + 1)
            act.dma_start(rows[n], parts[:, i, :, :]).then_inc(s_out[i], 16)
        act.wait_ge(s_tail, 16)
        for i in range(2):
            act.wait_ge(s_out[i], 16 * (STACK_BLOCKS // 2))

    return load, weights, pool, act


class Shared:
    pass


def build(nc, a, out):
    c = Shared()
    with Stage(nc, "keep") as st:
        c.ones = st.sb("ones", [P, P])
        c.ident = st.sb("ident", [P, P])
        c.ident_bf = st.sb("ident_bf", [P, P], BF16)
        c.node_row = st.sb("node_row", [P, P])
        c.step_row = st.sb("step_row", [P, STEPS])
        c.part_col = st.sb("part_col", [P, KB])
        c.src_slot = st.sb("src_slot", [P, STEPS + UNROLL], I32)
        c.local = st.sb("local", [P, STEPS])
        c.start_big = st.sb("start_big", [ROWS, 4 * P])
        c.last = st.sb("last", [ROWS, 4 * P])
        c.not_last = st.sb("not_last", [ROWS, 4 * P])
        c.row_start = st.sb("row_start", [8, ROWS])
        c.row_open = st.sb("row_open", [8, ROWS])
        c.tile_at = {w: st.sb(f"tile_at{w}", [1, STEPS], I32)
                     for w in (3 * HM, 3 * D, HM + 1, HEADS * (D // HEADS + 1), D + 1)}
        c.unsorted = st.sb("unsorted", [1, 4], I32)
        c.chunk_at = st.sb("chunk_at", [1, STEPS], I32)
        c.x = st.sb("x", [P, TILES, D])
        c.h = st.sb("h", [P, TILES, D])
        c.ht = st.sb("ht", [P, TILES, P])
        c.skip = c.ht
        c.w_edge = st.sb("w_edge", [DE, HM])
        c.w_stack = st.sb("w_stack", [STACK, HM], BF16)
        c.w_node = [st.sb(f"w_node{i}", [P, 4 * D]) for i in range(3)]
        c.ones_bf = st.sb("ones_bf", [P, P], BF16)
        c.b_parts = st.sb("b_parts", [3, 3, 4 * D], BF16)
        c.up1 = st.sb("up1", [P, 2, HM])
        c.up_b1 = st.sb("up_b1", [P, 2])
        c.w23 = st.sb("w23", [P, 2, D])
        c.u23 = st.sb("u23", [P, 2, D])
        c.wg = st.sb("wg", [P, 2, D])
        c.gate_w = st.sb("gate_w", [P, D])
        c.gate_b = st.sb("gate_b", [P, 1])
        c.bg_part = st.sb("bg_part", [1, 3, D], BF16)
        c.bg_parts = st.sb("bg_parts", [3, D], BF16)
        c.b23, c.ub23 = (st.sb(n, [1, D]) for n in ("b23", "ub23"))
        c.score = st.sb("score", [P, (STEPS + UNROLL) * HEADS])
        c.payload_dram = nc.dram_tensor("payload_dram", [STEPS * P * (HM + 1)], F32, kind="Internal").ap()
        c.attr_dram = nc.dram_tensor("attr_dram", [(CHUNKS + 1) * P * STACK], BF16, kind="Internal").ap()
        c.gather_dram = [nc.dram_tensor(f"gather{n}_dram", [NPAD, value_width(h, HM)], F32, kind="Internal").ap()
                         for n, h in enumerate((1, HEADS, 1))]
        c.local_dram = nc.dram_tensor("local_dram", [STEPS * P], BF16, kind="Internal").ap()
        c.key_dram = nc.dram_tensor("key_dram", [STEPS * P + 2], F32, kind="Internal").ap()
        c.edges = (nc.dram_tensor("src_dram", [E, 1], I32, kind="Internal").ap(),
                   nc.dram_tensor("dst_dram", [E, 1], I32, kind="Internal").ap(),
                   nc.dram_tensor("edge_attr_dram", [E, DE], F32, kind="Internal").ap())
        make_constants(nc, c)
        check_order(nc, c, a["dst"])
        sort_edges(nc, c, a["src"], a["dst"], a["edge_attr_16"])
        fold_weights(nc, c, a)
        plan_and_stack(nc, c, a["src"], a["dst"], a["edge_attr_16"])
        with Stage(nc, "layer0") as s0:
            table = s0.sb("table", [P, TILES, 3, HM], BF16)
            project(nc, c, "proj0", 0, 1, HM, 1.0, table, True)
            edge_scores(nc, c, "score0", 0, 1, True, table)
        softmax_weights(nc, c, "soft0", 1)
        with Stage(nc, "sums0") as s1:
            c.sum = s1.sb("sum", [P, TILES, HM + 1])
            aggregate(nc, c, "agg0", 1, True)
            update_nodes(nc, c)
        layer_norm(nc, c, "ln1")
        for layer, heads in ((1, HEADS), (2, 1)):
            with Stage(nc, f"layer{layer}") as s2:
                table = s2.sb("table", [P, TILES, 3, D], BF16)
                project(nc, c, f"proj{layer}", layer, heads, D, float(heads / D) ** 0.5, table, False)
                edge_scores(nc, c, f"score{layer}", layer, heads, False, table)
            softmax_weights(nc, c, f"soft{layer}", heads)
            with Stage(nc, f"sums{layer}") as s3:
                c.sum = s3.sb("sum", [P, TILES, D + heads])
                aggregate(nc, c, f"agg{layer}", heads, False)
                combine_heads(nc, c, f"heads{layer}", heads, out if layer == 2 else None)


_OUTS = [((N, D), "float32")]


def kernel(**inputs):
    import numpy as _np
    import concourse.bacc as _bacc
    from concourse import mybir as _mybir
    from concourse.bass_utils import run_bass_kernel_spmd as _run

    nc = _bacc.Bacc("TRN2", target_bir_lowering=False, num_devices=1)
    arrays, args = {}, {}
    for name, value in inputs.items():
        a = _np.ascontiguousarray(value)
        arrays[f"in_{name}_dram"] = a
        args[name] = nc.dram_tensor(f"in_{name}_dram", a.shape, _mybir.dt.from_np(a.dtype), kind="ExternalInput").ap()
    shape, dtype = _OUTS[0]
    out = nc.dram_tensor("out_0_dram", shape, _mybir.dt.from_np(_np.dtype(dtype)), kind="ExternalOutput").ap()
    build(nc, args, out)
    r = _run(nc, [arrays], core_ids=[0])
    return r.results[0]["out_0_dram"]
```
